# Optimizing a Trainium2 kernel written in Bass

```python
import numpy as np
import jax
import jax.numpy as jnp

def _softmax(x, axis=-1):
    return jax.nn.softmax(x, axis=axis)

def _gelu(x):
    return jax.nn.gelu(x, approximate=True)

def _silu(x):
    return jax.nn.silu(x)

def _sigmoid(x):
    return jax.nn.sigmoid(x)

def _layernorm(x, axis=-1, eps=1e-05):
    m = jnp.mean(x, axis=axis, keepdims=True)
    v = jnp.var(x, axis=axis, keepdims=True)
    return (x - m) / jnp.sqrt(v + eps)

def _scatter_add(tgt, idx, src, axis=0):
    return tgt.at[idx].add(src)

def _segment_sum(src, seg, n):
    return jax.ops.segment_sum(src, seg, n)
kernel_name = 'mk_decoder_postln_d1_seqx_r4_52bafe'

def setup_inputs(seed: int=0):
    np.random.seed(seed)
    _w = jnp.asarray

    def _rec_inputs():
        import jax
        import jax.numpy as jnp
        _rk = jax.random.key(seed)
        x = -0.0002928 + 1 * jax.random.normal(jax.random.fold_in(_rk, 1), (2, 1024, 256), jnp.float32)
        _lenS = 1024 - jax.random.randint(jax.random.fold_in(_rk, 7), (2,), 0, max(1, 1024 // 4) + 1, jnp.int32)
        _lenS2 = 64 - jax.random.randint(jax.random.fold_in(_rk, 8), (2,), 0, max(1, 64 // 4) + 1, jnp.int32)
        _ctx_1024P = jax.random.normal(jax.random.fold_in(_rk, 11), (2, 16, 256), jnp.float32)
        _ctx_1024c = jax.random.dirichlet(jax.random.fold_in(_rk, 511), 0.3 * jnp.ones((16,), jnp.float32), (2, 64))
        _ctx_1024t = jnp.einsum('bsk,bkd->bsd', _ctx_1024c, _ctx_1024P)
        _ctx_1024t = _ctx_1024t * jax.lax.rsqrt(jnp.mean(jnp.square(_ctx_1024t)) + 1e-12) * 0.953939
        ctx_1024 = 4.13588e-05 + 0.999923 * (_ctx_1024t + 0.3 * jax.random.normal(jax.random.fold_in(_rk, 611), (2, 64, 256), jnp.float32))
        return (x, ctx_1024)
    x, ctx_1024 = _rec_inputs()

    def _L0_attn_setup():
        import jax, jax.numpy as jnp
        import numpy as np
        B, T, D_MODEL, D_STATE = (8, 512, 256, 64)
        key = jax.random.key(seed)
        ks = jax.random.split(key, 10)

        def lecun(k, shape):
            fan_in = shape[0]
            return jax.random.normal(k, shape, dtype=jnp.float32) / jnp.sqrt(jnp.float32(fan_in))
        return {'x': jax.random.normal(ks[0], (B, T, D_MODEL), dtype=jnp.float32), 'W_in': lecun(ks[1], (D_MODEL, D_STATE)), 'b_in': jnp.zeros((D_STATE,), dtype=jnp.float32), 'W_gate': lecun(ks[2], (D_MODEL, D_MODEL)), 'b_gate': jnp.zeros((D_MODEL,), dtype=jnp.float32), 'W_out': lecun(ks[3], (D_MODEL, D_MODEL)), 'b_out': jnp.zeros((D_MODEL,), dtype=jnp.float32), 'A': lecun(ks[4], (D_STATE, D_STATE)) * 0.1, 'Bm': lecun(ks[5], (D_STATE, D_STATE)), 'C': lecun(ks[6], (D_MODEL, D_STATE)), 'D': lecun(ks[7], (D_MODEL, D_STATE))}
    _L0_attn_all = _L0_attn_setup()
    _L0_attn_in = {k: v for k, v in _L0_attn_all.items() if k in ('W_in', 'b_in', 'W_gate', 'b_gate', 'W_out', 'b_out', 'A', 'Bm', 'C', 'D')}
    del _L0_attn_all

    def _L0_xattn_setup():
        import jax, jax.numpy as jnp
        import numpy as np
        import math
        EMBED_DIM = 256
        NUM_HEADS = 16
        D_K = EMBED_DIM // NUM_HEADS
        B, S_DEC, S_ENC = (4, 256, 512)
        key = jax.random.key(seed)
        ks = jax.random.split(key, 12)
        s = 1.0 / math.sqrt(EMBED_DIM)
        return {'Q_decoder': jax.random.normal(ks[0], (B, S_DEC, EMBED_DIM), jnp.float32), 'K_encoder': jax.random.normal(ks[1], (B, S_ENC, EMBED_DIM), jnp.float32), 'V_encoder': jax.random.normal(ks[2], (B, S_ENC, EMBED_DIM), jnp.float32), 'Wq': jax.random.normal(ks[3], (EMBED_DIM, EMBED_DIM), jnp.float32) * s, 'bq': jnp.zeros((EMBED_DIM,), jnp.float32), 'Wk': jax.random.normal(ks[4], (EMBED_DIM, EMBED_DIM), jnp.float32) * s, 'bk': jnp.zeros((EMBED_DIM,), jnp.float32), 'Wv': jax.random.normal(ks[5], (EMBED_DIM, EMBED_DIM), jnp.float32) * s, 'bv': jnp.zeros((EMBED_DIM,), jnp.float32), 'Wo': jax.random.normal(ks[6], (EMBED_DIM, EMBED_DIM), jnp.float32) * s, 'bo': jnp.zeros((EMBED_DIM,), jnp.float32)}
    _L0_xattn_all = _L0_xattn_setup()
    _L0_xattn_in = {k: v for k, v in _L0_xattn_all.items() if k in ('Wq', 'bq', 'Wk', 'bk', 'Wv', 'bv', 'Wo', 'bo')}
    del _L0_xattn_all

    def _L0_ffn_setup():
        import jax, jax.numpy as jnp
        import numpy as np
        B, S, H = (4, 512, 256)
        E = 8
        GS = 2
        NG = E // GS
        F = int(H * 4 * (2.0 / 3.0))
        key = jax.random.key(seed)
        ks = jax.random.split(key, 7)
        sc_h = 1.0 / np.sqrt(H)
        sc_f = 1.0 / np.sqrt(F)
        return {'x': jax.random.normal(ks[0], (B, S, H), dtype=jnp.float32), 'Wr': jax.random.normal(ks[1], (H, E), dtype=jnp.float32) * sc_h, 'br': jnp.zeros((E,), dtype=jnp.float32), 'W_up': jax.random.normal(ks[2], (NG, H, F), dtype=jnp.float32) * sc_h, 'b_up': jax.random.normal(ks[3], (NG, F), dtype=jnp.float32) * 0.01, 'W_down': jax.random.normal(ks[4], (E, F, H), dtype=jnp.float32) * sc_f, 'b_down': jax.random.normal(ks[5], (E, H), dtype=jnp.float32) * 0.01}
    _L0_ffn_all = _L0_ffn_setup()
    _L0_ffn_in = {k: v for k, v in _L0_ffn_all.items() if k in ('Wr', 'br', 'W_up', 'b_up', 'W_down', 'b_down')}
    del _L0_ffn_all
    return {'x': x, 'ctx_1024': ctx_1024, 'L0_attn_W_in': _L0_attn_in['W_in'], 'L0_attn_b_in': _L0_attn_in['b_in'], 'L0_attn_W_gate': _L0_attn_in['W_gate'], 'L0_attn_b_gate': _L0_attn_in['b_gate'], 'L0_attn_W_out': _L0_attn_in['W_out'], 'L0_attn_b_out': _L0_attn_in['b_out'], 'L0_attn_A': _L0_attn_in['A'], 'L0_attn_Bm': _L0_attn_in['Bm'], 'L0_attn_C': _L0_attn_in['C'], 'L0_attn_D': _L0_attn_in['D'], 'L0_xattn_Wq': _L0_xattn_in['Wq'], 'L0_xattn_bq': _L0_xattn_in['bq'], 'L0_xattn_Wk': _L0_xattn_in['Wk'], 'L0_xattn_bk': _L0_xattn_in['bk'], 'L0_xattn_Wv': _L0_xattn_in['Wv'], 'L0_xattn_bv': _L0_xattn_in['bv'], 'L0_xattn_Wo': _L0_xattn_in['Wo'], 'L0_xattn_bo': _L0_xattn_in['bo'], 'L0_ffn_Wr': _L0_ffn_in['Wr'], 'L0_ffn_br': _L0_ffn_in['br'], 'L0_ffn_W_up': _L0_ffn_in['W_up'], 'L0_ffn_b_up': _L0_ffn_in['b_up'], 'L0_ffn_W_down': _L0_ffn_in['W_down'], 'L0_ffn_b_down': _L0_ffn_in['b_down']}

def reference(x, ctx_1024, L0_attn_W_in, L0_attn_b_in, L0_attn_W_gate, L0_attn_b_gate, L0_attn_W_out, L0_attn_b_out, L0_attn_A, L0_attn_Bm, L0_attn_C, L0_attn_D, L0_xattn_Wq, L0_xattn_bq, L0_xattn_Wk, L0_xattn_bk, L0_xattn_Wv, L0_xattn_bv, L0_xattn_Wo, L0_xattn_bo, L0_ffn_Wr, L0_ffn_br, L0_ffn_W_up, L0_ffn_b_up, L0_ffn_W_down, L0_ffn_b_down):
    import jax
    import jax.numpy as jnp

    def _L0_attn_ref(x, W_in, b_in, W_gate, b_gate, W_out, b_out, A, Bm, C, D):
        import jax, jax.numpy as jnp
        import numpy as np
        B, T, D_MODEL, D_STATE = (8, 512, 256, 64)
        u = x @ W_in + b_in
        gate = jax.nn.sigmoid(x @ W_gate + b_gate)
        u_t_first = jnp.swapaxes(u, 0, 1)
        h0 = jnp.zeros((x.shape[0], A.shape[0]), dtype=x.dtype)

        def step(h, u_t):
            h = h @ A + u_t @ Bm
            return (h, h)
        _, hs = jax.lax.scan(step, h0, u_t_first)
        hs = jnp.swapaxes(hs, 0, 1)
        y = jnp.einsum('btn,dn->btd', hs, C) + jnp.einsum('btn,dn->btd', u, D)
        y = y * gate
        return y @ W_out + b_out

    def _L0_xattn_ref(Q_decoder, K_encoder, V_encoder, Wq, bq, Wk, bk, Wv, bv, Wo, bo):
        import jax, jax.numpy as jnp
        import numpy as np
        import math
        EMBED_DIM = 256
        NUM_HEADS = 16
        D_K = EMBED_DIM // NUM_HEADS
        B, S_DEC, S_ENC = (4, 256, 512)
        b, sd, d = Q_decoder.shape
        se = K_encoder.shape[1]
        Q = (Q_decoder @ Wq + bq).reshape(b, sd, NUM_HEADS, D_K).transpose(0, 2, 1, 3)
        K = (K_encoder @ Wk + bk).reshape(b, se, NUM_HEADS, D_K).transpose(0, 2, 1, 3)
        V = (V_encoder @ Wv + bv).reshape(b, se, NUM_HEADS, D_K).transpose(0, 2, 1, 3)
        scores = jnp.einsum('bhqd,bhkd->bhqk', Q, K) / math.sqrt(D_K)
        attn = jax.nn.softmax(scores, axis=-1)
        out = jnp.einsum('bhqk,bhkd->bhqd', attn, V)
        out = out.transpose(0, 2, 1, 3).reshape(b, sd, d)
        return out @ Wo + bo

    def _L0_ffn_ref(x, Wr, br, W_up, b_up, W_down, b_down):
        import jax, jax.numpy as jnp
        import numpy as np
        B, S, H = (4, 512, 256)
        E = 8
        GS = 2
        NG = E // GS
        F = int(H * 4 * (2.0 / 3.0))
        b, s, h = x.shape
        n_tok = b * s
        k = n_tok // E
        xf = x.reshape(n_tok, h)
        logits = xf @ Wr + br
        Sm = jax.nn.softmax(logits, axis=-1)
        G_t, idx_t = jax.lax.top_k(Sm.T, k)
        G = G_t.T
        idx = idx_t.T
        tokens = xf[idx]
        group = jnp.arange(E) // GS
        Wu = W_up[group]
        bu = b_up[group]
        mid = jax.nn.silu(jnp.einsum('keh,ehf->kef', tokens, Wu) + bu)
        out = jnp.einsum('kef,efh->keh', mid, W_down) + b_down
        y = jnp.zeros_like(xf).at[idx].add(G[..., None] * out)
        return y.reshape(b, s, h)
    x = _layernorm(x + _L0_attn_ref(x, L0_attn_W_in, L0_attn_b_in, L0_attn_W_gate, L0_attn_b_gate, L0_attn_W_out, L0_attn_b_out, L0_attn_A, L0_attn_Bm, L0_attn_C, L0_attn_D), axis=-1)
    x = _layernorm(x + _L0_xattn_ref(x, ctx_1024, ctx_1024, L0_xattn_Wq, L0_xattn_bq, L0_xattn_Wk, L0_xattn_bk, L0_xattn_Wv, L0_xattn_bv, L0_xattn_Wo, L0_xattn_bo), axis=-1)
    x = _layernorm(x + _L0_ffn_ref(x, L0_ffn_Wr, L0_ffn_br, L0_ffn_W_up, L0_ffn_b_up, L0_ffn_W_down, L0_ffn_b_down), axis=-1)
    return x

_drawn_inputs = setup_inputs


def setup_inputs(seed=0):
    import zlib

    import numpy as np

    out = dict(_drawn_inputs(seed))
    spreads = {'L0_attn_b_in': (0.0, 0.1),
     'L0_attn_b_gate': (0.0, 0.378),
     'L0_attn_b_out': (0.0, 0.1),
     'L0_xattn_bq': (0.0, 0.1),
     'L0_xattn_bk': (0.0, 2.0),
     'L0_xattn_bv': (0.0, 0.1),
     'L0_xattn_bo': (0.0, 0.1),
     'L0_ffn_br': (0.0, 0.1)}
    factors = {'L0_ffn_b_up': 25.417, 'L0_ffn_b_down': 8.0}
    for name, (base, spread) in spreads.items():
        noise = np.random.default_rng([zlib.crc32(name.encode()), seed]).standard_normal(out[name].shape)
        drawn = base * np.exp(spread * noise) if base else spread * noise
        out[name] = jnp.asarray(drawn.astype(out[name].dtype))
    for name, factor in factors.items():
        out[name] = (out[name] * factor).astype(out[name].dtype)
    return out
```

```python
from contextlib import ExitStack

import concourse.bass as bass
from concourse import mybir


def decoder_block(
    nc, x, ctx, w_in, b_in, w_gate, b_gate, w_out, b_out, a_mat, b_mat, c_mat, d_mat,
    wq, bq, wk, bk, wv, bv, wo, bo, wr, br, w_up, b_up, w_down, b_down, out,
):
    F32, F32R, BF16 = mybir.dt.float32, mybir.dt.float32r, mybir.dt.bfloat16
    I32, U32 = mybir.dt.int32, mybir.dt.uint32
    ALU, ACT, AX = mybir.AluOpType, mybir.ActivationFunctionType, mybir.AxisListType

    B, T, D = x.shape
    P = 128
    KC = D // P
    TOK = B * T
    L = 16
    CH = T // L
    NT = TOK // P
    NB = 4
    BLK = TOK // NB
    TPB = BLK // P
    NS = w_in.shape[1]
    SE = ctx.shape[1]
    DK = 16
    HD = D // DK
    PR = HD // 2
    E = wr.shape[1]
    TOP = TOK // E
    NG = w_up.shape[0]
    GS = E // NG
    F = w_up.shape[2]
    FC = -(-F // P)
    FW = [min(P, F - f * P) for f in range(FC)]
    RW = D + E
    EPS = 1e-5
    SCALE = DK ** -0.5
    ROUNDS = 15
    KQ = 3 * 32
    LEVELS = [1 << k for k in range(6)]

    es = ExitStack()
    with es:
        def dram(name, shape):
            return nc.dram_tensor(name, shape, F32, kind="Internal").ap()

        routed = dram("routed_rows", (TOK, RW))
        summed = dram("summed_rows", (TOK, D))

        top = [16512]

        def place(name, shape, dt, at=None):
            size = 2 if dt is BF16 else 4
            for s in shape[1:]:
                size *= s
            size = -(-size // 32) * 32
            if at is None:
                at = top[0]
                top[0] += size
            assert at + size <= 229344, (name, at + size)
            t = nc.alloc_sbuf_tensor_at(name, shape, dt, offset=at)
            offset_of[name] = at
            end_of[name] = at + size
            return t

        offset_of, end_of = {}, {}

        ident = place("ident", [P, P], F32)
        ones_f = place("ones_f", [P, P], F32)
        ones_r = place("ones_r", [P, P], F32R)
        ones_b = place("ones_b", [P, P], BF16)
        ident_b = place("ident_b", [P, P], BF16)
        same_expert = place("same_expert", [P, P], BF16)
        before_b = place("before_b", [P, P], BF16)
        chunk_before_b = place("chunk_before_b", [P, P], BF16)
        even_to_odd_b = place("even_to_odd_b", [P, P], BF16)
        own_odd_to_even_b = place("own_odd_to_even_b", [P, P], BF16)
        pidx = place("pidx", [P, 1], I32)
        pbits = place("pbits", [P, 8], I32)
        pf = place("pf", [P, 8], F32)
        col_i = place("col_i", [P, P], I32)
        col_f = place("col_f", [P, P], F32)
        colm_i = place("colm_i", [P, P], I32)
        colm_f = place("colm_f", [P, P], F32)
        col7_f = place("col7_f", [P, P], F32)
        half_mask = place("half_mask", [P, 2], F32)
        mask_hi3 = place("mask_hi3", [P, 8], F32)
        mask_lo3 = place("mask_lo3", [P, 8], F32)
        mask_16 = place("mask_16", [P, 16], F32)
        steps = place("steps", [P, ROUNDS, 3], I32)
        reset_g = place("reset_g", [P, E, NT], BF16)
        reset_e = place("reset_e", [P, E * B, NT // B], BF16)
        tok_i = place("tok_i", [P, NT], I32)
        junk_m = place("junk_m", [P, 1], F32)
        tok_f = place("tok_f", [P, NT], F32)
        neg_half = place("neg_half", [P, 4], F32)
        b_in_c = place("b_in_c", [P, 1], F32)
        b_gate_c = place("b_gate_c", [P, KC], F32)
        bq_c = place("bq_c", [P, KC], F32)
        bk_c = place("bk_c", [P, KC], F32)
        bk3_c = place("bk3_c", [P, PR], F32)
        bv_row = place("bv_row", [1, D], F32)
        br_all = place("br_all", [P, E], F32)
        b_up_c = place("b_up_c", [P, NG, FC], F32)
        wr_s = place("wr_s", [P, KC, E], F32)
        bn6 = place("bn6", [P, 3 * NT, 6], F32)
        mean_var = place("mean_var", [P, 3 * NT, 2], F32)
        var_eps = place("var_eps", [P, 3 * NT], F32)
        rstd = place("rstd", [P, 3 * NT], F32)
        lgt = place("lgt", [P, NT, E], F32)
        X = place("X", [P, NT, RW], F32)
        PHASE3 = top[0]

        b_out_all = place("b_out_all", [P, D], F32)
        bo_all = place("bo_all", [P, D], F32)
        XH = place("XH", [P, NB, KC, BLK], F32R)
        XL = place("XL", [P, NB, KC, BLK], F32R)
        YH = place("YH", [P, NB, KC, BLK], F32R, offset_of["XH"])
        YL = place("YL", [P, NB, KC, BLK], F32R, offset_of["XL"])
        QH = place("QH", [P, 2, KC, BLK], F32R, offset_of["XH"])
        QL = place("QL", [P, 2, KC, BLK], F32R, offset_of["XL"])
        HU = place("HU", [P, TOK], F32)
        NMT = place("NMT", [P, 2, BLK], F32R, offset_of["HU"])
        X2T = place("X2T", [P, 2, D], F32, end_of["NMT"])
        HUH = place("HUH", [P, TOK], F32R)
        HUL = place("HUL", [P, TOK], F32R)
        PT1 = place("PT1", [P, PR, BLK], F32, offset_of["HUH"])
        G = place("G", [P, NB, KC, BLK], F32)
        X1H = [place(f"X1H{r}", [P, KC, BLK], F32R, offset_of["G"] + 8192 * r) for r in range(2)]
        X1L = [place(f"X1L{r}", [P, KC, BLK], F32R, offset_of["G"] + 8192 * r + 4096) for r in range(2)]
        QS = place("QS", [P, 2, PR, BLK], F32R)
        PT0 = place("PT0", [P, PR, BLK], F32)
        PT = [PT0, PT1]
        WIN = [place(n, [P, KC, P], F32R) for n in ("WINH", "WINL")]
        WG = [place(n, [P, KC, D], F32R) for n in ("WGH", "WGL")]
        WOUT = [place(n, [P, KC, D], F32R) for n in ("WOUTH", "WOUTL")]
        WQ = [place(n, [P, KC, D], F32R) for n in ("WQH", "WQL")]
        WO = [place(n, [P, KC, D], F32R) for n in ("WOH", "WOL")]
        W1 = [place(n, [P, D], F32R) for n in ("W1H", "W1L")]
        KS = place("KS", [P, PR, B, P], F32R)
        KM = place("KM", [P, B, KC, HD // KC, SE], F32R)
        VB = place("VB", [P, B, PR, 2, DK + 1], F32)
        ATT = place("ATT", [P, TPB, D], F32)
        ATH = place("ATH", [P, 2, KC, P], F32R)
        ATL = place("ATL", [P, 2, KC, P], F32R)
        PW = place("PW", [NS, L + 1, NS], F32, offset_of["ATT"])
        PB = place("PB", [NS, 5, NS], F32, end_of["PW"])
        TW = place("TW", [NS, 9, NS], F32)
        HS = place("HS", [NS, B, CH + 1], F32)
        NMF = place("NMF", [P, TPB, HD], F32)
        NMS = place("NMS", [P, TPB, PR, 2, 2], F32R)
        REC = place("REC", [P, 2, HD], F32)
        stage = [offset_of["QS"]]

        def staged(name, shape, dt=F32):
            t = place(name, shape, dt, stage[0])
            stage[0] = end_of[name]
            assert stage[0] <= end_of["PT0"]
            return t

        win_s = staged("win_s", [P, KC, P])
        wg_s = staged("wg_s", [P, KC, D])
        wout_s = staged("wout_s", [P, KC, D])
        wq_s = staged("wq_s", [P, KC, D])
        wo_s = staged("wo_s", [P, KC, D])
        wk_s = staged("wk_s", [P, KC, D])
        wv_s = staged("wv_s", [P, KC, D])
        wk3_s = staged("wk3_s", [P, KC * PR, 3, 32])
        ab_s = staged("ab_s", [P, NS])
        mx_s = staged("mx_s", [P, P])
        cd_s = staged("cd_s", [P, KC, P])
        cdt_s = staged("cdt_s", [P, D])
        ctx_s = staged("ctx_s", [P, D])
        ctd_s = staged("ctd_s", [P, KC, B, 2, SE])
        kt_s = staged("kt_s", [P, KC, B * SE])
        ksf_s = staged("ksf_s", [P, PR, B, 2, SE])

        top[0] = PHASE3
        idx = place("idx", [P, NT], I32)
        XG = place("XG", [P, NT, RW], F32)
        FTH = place("FTH", [P, 2, KC, GS * TOP], F32R, offset_of["X"])
        FTL = place("FTL", [P, 2, KC, GS * TOP], F32R, end_of["FTH"])
        MF = place("MF", [P, 3, GS * TOP], F32)
        MH = place("MH", [P, 2, FC, GS * TOP], F32R)
        ML = place("ML", [P, 2, FC, GS * TOP], F32R)
        OHH = place("OHH", [P, NT, E, 16], F32R, offset_of["MH"])
        OHL = place("OHL", [P, NT, E, 16], F32, offset_of["MH"] + 8192)
        OHI = place("OHI", [P, NT, E, 16], F32R, offset_of["MH"] + 16384)
        WUR = place("WUR", [P, 2, KC, F], F32)
        WUH = place("WUH", [P, 2, KC, F], F32R)
        WUL = place("WUL", [P, 2, KC, F], F32R)
        WDR = place("WDR", [P, 2, FC, D], F32)
        WDH = place("WDH", [P, 3, FC, D], F32R)
        WDL = place("WDL", [P, 3, FC, D], F32R)
        BDR = place("BDR", [1, 2, D], F32)
        BDH = place("BDH", [1, 3, D], F32R)
        BDL = place("BDL", [1, 3, D], F32R)
        OUT = place("OUT", [P, 4, D], F32)
        Y = place("Y", [P, NT, D], F32, offset_of["MH"])

        top[0] = offset_of["ML"]
        S2 = place("S2", [P, NT, E], F32)
        mxl = place("mxl", [P, NT], F32)
        lm = place("lm", [P, NT, E], F32)
        ex = place("ex", [P, NT, E], F32)
        sm = place("sm", [P, NT], F32)
        rcp = place("rcp", [P, NT], F32)
        ST = place("ST", [P, P], F32)
        junk = place("junk", [P, 3, P], BF16)
        cand = place("cand", [P, ROUNDS, 3], I32)
        cnt = place("cnt", [P, ROUNDS, 3], BF16)
        best = place("best", [P, ROUNDS + 1, 4], F32)
        rt = place("rt", [P, E], F32)
        thr = place("thr", [P, E], F32)
        gt = place("gt", [P, E, NT], BF16)
        ge = place("ge", [P, E, NT], BF16)
        eq = place("eq", [P, E, NT], BF16)
        cig = place("cig", [P, E, NT], BF16)
        cie = place("cie", [P, E * B, NT // B], BF16)
        cxg = place("cxg", [P, E, NT], BF16)
        cxe = place("cxe", [P, E, NT], BF16)
        sl = [place(f"sl{k}", [P, E, NT], F32) for k in range(5)]
        sl_i = place("sl_i", [P, 3, E, NT], I32)
        sl_f = place("sl_f", [P, 2, E, NT], F32)
        ym = place("ym", [P, E, 16], F32)
        lk = place("lk", [P, 16], F32)
        lh = place("lh", [P, 8, 16], F32)
        assert top[0] <= end_of["ML"]

        bank = [es.enter_context(nc.psum_tensor(f"bank{k}", [P, 512], F32)) for k in range(8)]

        def sem(name):
            return es.enter_context(nc.semaphore(name))

        filled = [sem(f"filled{k}") for k in range(8)]
        moved = [sem(f"moved{k}") for k in range(8)]

        norm_order = [(1, t) for t in range(TPB)]
        for n in range(NB + 3):
            if n + 1 < NB:
                norm_order += [(1, TPB * (n + 1) + s) for s in range(TPB)]
            if 0 <= n - 2 < NB:
                norm_order += [(2, TPB * (n - 2) + s) for s in range(TPB)]
        norm_order += [(3, t) for t in range(NT)]
        norm_at = {what: k for k, what in enumerate(norm_order)}

        turn_of, uses = {}, [0] * 8

        def product(name, k):
            turn_of[name] = (k, uses[k])
            uses[k] += 1

        POWERS = [1 << k for k in range(9)]
        product("ab", 6)
        for n in range(NB):
            for c in range(KC):
                product(("xt", n, c), c)
            product(("u", n), 2 + n % 2)
            product(("pw", POWERS[n]), 4)
            product(("tw", POWERS[n]), 5)
        product("cd", 0)
        product("ctx", 1)
        product("w1", 7)
        for i in range(L):
            product(("step", i), 6 + i % 2)
            if i % 2 == 0:
                product(("gate", i // 2), 2 + (i // 2) % 2)
            if i % 2 == 1 and 4 + i // 2 < 9:
                product(("pw", POWERS[4 + i // 2]), 4)
                if POWERS[4 + i // 2] < 256:
                    product(("tw", POWERS[4 + i // 2]), 5)
        KSP = [(0, 1, 2), (3, 4), (5, 6), (7,), (), ()]
        for k in range(6):
            product(("carry", k), 6 + k % 2)
            if k < 2:
                product(("kt", k), k)
                product(("v", k), 4 + k)
            for j in KSP[k]:
                product(("ks", j), 2 + j % 2)
        for q in range(4):
            product(("cor", q), 6 + q % 2)
        for n in range(NB):
            for c in range(KC):
                product(("y", n, c), 2 + c)

        def w_products(n):
            for s in range(TPB):
                product(("z1", n, s), 6 + s % 2)

        w_products(0)
        for n in range(NB + 3):
            if n < NB:
                for c in range(KC):
                    product(("x1t", n, c), c)
                for c in range(KC):
                    product(("q", n, c), 2 + c)
            if 0 <= n - 3:
                for s in range(TPB):
                    product(("x2t", n - 3, s), s % 2)
                    product(("lg", n - 3, s), 2 + s % 2)
            if n + 1 < NB:
                w_products(n + 1)
            if n < NB:
                for s in range(TPB):
                    for c in range(KC):
                        product(("mx", n, s, c), 2 + c)
                product(("nmt", n), 0)
            if 0 <= n - 2 < NB:
                for s in range(TPB):
                    product(("att", n - 2, s), s % 2)
                    product(("z2", n - 2, s), 6 + s % 2)
            if n < NB:
                for j in range(PR):
                    product(("sc", n, j), 4 + j % 2)
            if 0 <= n - 1 < NB:
                for s in range(TPB):
                    product(("pv", n - 1, s), 6 + s % 2)
        product("st", 0)
        for r in range(ROUNDS):
            product(("tot", r), 1 + r % 2)
        product("thr", 3)
        product("pg", 4)
        product("pe", 5)
        product("ids", 6)
        product("idx", 7)
        for g in range(NG + 1):
            if g < NG:
                for c in range(KC):
                    product(("gt", g, c), 5 + c)
                for f in range(FC):
                    product(("up", g, f), f % 3)
            if g > 0:
                for e in range(GS * (g - 1), GS * g):
                    for h in range(2):
                        product(("dn", e, h), 3 + h)

        def bank_of(name):
            return bank[turn_of[name][0]]

        def wait_filled(eng, name):
            k, u = turn_of[name]
            eng.wait_ge(filled[k], u + 1)

        def wait_moved(eng, name):
            k, u = turn_of[name]
            eng.wait_ge(moved[k], u + 1)

        def wait_up_low(eng, g):
            eng.wait_ge(wu_lo_pool, min(g + 1, 2))
            if g >= 2:
                eng.wait_ge(wu_lo_dve, g - 1)

        def phase2_over(eng):
            wait_moved(eng, ("lg", NB - 1, TPB - 1))

        def sem_filled(name):
            return filled[turn_of[name][0]]

        def sem_moved(name):
            return moved[turn_of[name][0]]

        x_in = [sem(f"x_in{n}") for n in range(NB)]
        ab_in, cd_in, win_in, wg_in, wout_in, wq_in, wo_in = [
            sem(n) for n in ("ab_in", "cd_in", "win_in", "wg_in", "wout_in", "wq_in", "wo_in")]
        kv_in, bias1_in, bias2_in = sem("kv_in"), sem("bias1_in"), sem("bias2_in")
        ident_made, pool_consts = sem("ident_made"), sem("pool_consts")
        head_masks, masks_made = sem("head_masks"), sem("masks_made")
        win_zero, mx_made, starts_zero = sem("win_zero"), sem("mx_made"), sem("starts_zero")
        w_hi, w_lo = sem("w_hi"), sem("w_lo")
        xh_made, u_made, xb_added = sem("xh_made"), sem("u_made"), sem("xb_added")
        tw1_made = sem("tw1_made")
        h_start = sem("h_start")
        hu_hi, hu_lo = sem("hu_hi"), sem("hu_lo")
        km_made = sem("km_made")
        wk3_made, ks_hi, ks_made, vb_made, vb_init = [
            sem(n) for n in ("wk3_made", "ks_hi", "ks_made", "vb_made", "vb_init")]
        y_hi, y_lo_dve, y_lo_pool = sem("y_hi"), sem("y_lo_dve"), sem("y_lo_pool")
        ln_var, ln_rstd, ln_out = sem("ln_var"), sem("ln_rstd"), sem("ln_out")
        x1h_made, q_hi, qs_in = sem("x1h_made"), sem("q_hi"), [sem("qs_in0"), sem("qs_in1")]
        bo_added = sem("bo_added")
        nm_made = sem("nm_made")
        ath_made = sem("ath_made")
        lm_made, ex_made, s2_made, routed_made = [
            sem(n) for n in ("lm_made", "ex_made", "s2_made", "routed_made")]
        routed_out, summed_out = sem("routed_out"), sem("summed_out")
        cnt_made, rt_made, prefix_in, slots_made, onehot_made, lh_made, idx_made = [
            sem(n) for n in ("cnt_made", "rt_made", "prefix_in", "slots_made",
                             "onehot_made", "lh_made", "idx_made")]
        gathered = [sem(f"gathered{e}") for e in range(E)]
        scattered = [sem(f"scattered{e}") for e in range(E)]
        wu_in, wd_in = [sem("wu_in0"), sem("wu_in1")], [sem("wd_in0"), sem("wd_in1")]
        wu_hi, wu_lo_pool, wu_lo_dve = sem("wu_hi"), sem("wu_lo_pool"), sem("wu_lo_dve")
        wd_hi, wd_lo = sem("wd_hi"), sem("wd_lo")
        fth_made = sem("fth_made")
        mh_made, ml_made = sem("mh_made"), sem("ml_made")
        y_in = [sem(f"y_in{q}") for q in range(4)]
        y_out = sem("y_out")
        dve_step, act_step, pool_step = sem("dve_step"), sem("act_step"), sem("pool_step")

        def chain(eng, s):
            count = [0]

            def link(ins):
                count[0] += 1
                ins.then_inc(s, 1)
                eng.wait_ge(s, count[0])

            return link

        block = es.enter_context(nc.Block())

        def by_tiles(ap):
            return ap.rearrange("(b c j i) d -> i c b j d", b=B, c=CH, i=2)

        @block.sync
        def _(sp):
            sp.dma_start(ab_s[0:NS, :], a_mat).then_inc(ab_in, 16)
            sp.dma_start(ab_s[NS:P, :], b_mat).then_inc(ab_in, 16)
            sp.dma_start(PW[:, 1, :], a_mat).then_inc(ab_in, 16)
            xr = by_tiles(x.rearrange("b t d -> (b t) d"))
            for n in range(NB):
                b, j0 = n // 2, (n % 2) * TPB
                for i in range(2):
                    sp.dma_start(X[CH * i:CH * (i + 1), TPB * n:TPB * (n + 1), 0:D],
                                 xr[i, :, b, j0:j0 + TPB, :]).then_inc(x_in[n], 16)
            sp.dma_start(wg_s[:], w_gate.rearrange("(c p) n -> p c n", p=P)).then_inc(wg_in, 16)
            sp.dma_start(wout_s[:], w_out.rearrange("(c p) n -> p c n", p=P)).then_inc(wout_in, 16)
            sp.dma_start(wq_s[:], wq.rearrange("(c p) n -> p c n", p=P)).then_inc(wq_in, 16)
            sp.dma_start(wo_s[:], wo.rearrange("(c p) n -> p c n", p=P)).then_inc(wo_in, 16)
            for n in range(NB):
                r = n % 2
                wait_moved(sp, ("q", n, 0))
                wait_moved(sp, ("q", n, 1))
                if n >= 2:
                    wait_filled(sp, ("sc", n - 2, PR - 1))
                else:
                    sp.wait_ge(ks_made, 2)
                    sp.wait_ge(km_made, 4)
                    sp.wait_ge(w_lo, 5)
                for j in range(PR):
                    c, p0 = j // 4, 32 * (j % 4)
                    for k, src in enumerate((QH, QH, QL)):
                        sp.dma_start(QS[32 * k:32 * k + 32, r, j, :].bitcast(F32),
                                     src[p0:p0 + 32, r, c, :].bitcast(F32)).then_inc(qs_in[r], 16)
                wait_moved(sp, ("nmt", n))
                for j in range(PR):
                    sp.dma_start(QS[KQ:KQ + 4, r, j, :].bitcast(F32),
                                 NMT[4 * j:4 * j + 4, r, :].bitcast(F32)).then_inc(qs_in[r], 16)
            phase2_over(sp)

            def load_up(g):
                if g >= 2:
                    sp.wait_ge(wu_hi, g - 1)
                    wait_up_low(sp, g - 2)
                sp.dma_start(WUR[:, g % 2], w_up[g].rearrange("(c p) f -> p c f", p=P))\
                    .then_inc(wu_in[g % 2], 16)

            def load_down(e):
                if e >= 2:
                    sp.wait_ge(wd_hi, e - 1)
                    sp.wait_ge(wd_lo, e - 1)
                full = (FC - 1) * P
                sp.dma_start(WDR[:, e % 2, 0:FC - 1, :],
                             w_down[e, 0:full, :].rearrange("(c p) n -> p c n", p=P))\
                    .then_inc(wd_in[e % 2], 16)
                sp.dma_start(WDR[0:FW[-1], e % 2, FC - 1, :], w_down[e, full:F, :])\
                    .then_inc(wd_in[e % 2], 16)
                sp.dma_start(BDR[:, e % 2, :], b_down[e:e + 1, :]).then_inc(wd_in[e % 2], 16)

            load_up(0)
            load_down(0)
            load_down(1)
            load_up(1)
            for i in range(2):
                for b in range(B):
                    sp.dma_start(by_tiles(summed)[i, :, b],
                                 X[CH * i:CH * (i + 1), NT // B * b:NT // B * (b + 1), 0:D])\
                        .then_inc(summed_out, 16)
            sp.wait_ge(routed_made, 1)
            for i in range(2):
                for b in range(B):
                    sp.dma_start(by_tiles(routed)[i, :, b],
                                 X[CH * i:CH * (i + 1), NT // B * b:NT // B * (b + 1), :])\
                        .then_inc(routed_out, 16)
            load_down(2)
            for g in range(2, NG):
                load_up(g)
                load_down(2 * g - 1)
                load_down(2 * g)
            load_down(E - 1)
            for e in range(E):
                sp.wait_ge(scattered[e], 32)
            ys = summed.rearrange("(p i) d -> p i d", p=P)
            for q in range(4):
                sp.dma_start(Y[:, 4 * q:4 * q + 4, :], ys[:, 4 * q:4 * q + 4, :]).then_inc(y_in[q], 16)
            os_ = out.rearrange("b t d -> (b t) d").rearrange("(p i) d -> p i d", p=P)
            for q in range(4):
                sp.wait_ge(ln_out, 2 * NT + 4 * (q + 1))
                sp.dma_start(os_[:, 4 * q:4 * q + 4, :], Y[:, 4 * q:4 * q + 4, :]).then_inc(y_out, 16)
            sp.wait_ge(y_out, 64)
            sp.wait_ge(summed_out, 64)
            sp.wait_ge(routed_out, 64)

        @block.gpsimd
        def _(pool):
            link = chain(pool, pool_step)
            link(pool.memset(ident[:], 0.0))
            pool.affine_select(out=ident[:], in_=ident[:], compare_op=ALU.not_equal, fill=1.0,
                               base=0, pattern=[[-1, P]], channel_multiplier=1).then_inc(ident_made, 1)
            pool.memset(win_s[:, :, 0:NS], 0.0).then_inc(win_zero, 1)
            pool.wait_ge(win_zero, 1)
            link(pool.memset(mx_s[NS:P, 0:NS], 0.0))
            pool.wait_ge(ident_made, 1)
            pool.tensor_copy(mx_s[NS:P, NS:P], ident[NS:P, NS:P]).then_inc(mx_made, 1)
            pool.wait_ge(mx_made, 1)
            link(pool.memset(HU[0:NS, :].rearrange("p (b i c) -> p b i c", b=B, i=L)[:, :, 0, :], 0.0))
            pool.memset(HS[:, :, 0:1], 0.0).then_inc(starts_zero, 1)
            pool.wait_ge(starts_zero, 1)
            link(pool.memset(neg_half[:], -0.5))
            link(pool.iota(pidx[:], pattern=[[0, 1]], base=0, channel_multiplier=1))
            link(pool.iota(col_i[:], pattern=[[1, P]], base=0, channel_multiplier=0))
            link(pool.iota(tok_i[:], pattern=[[T, B], [2, NT // B]], base=0, channel_multiplier=0))
            for j in range(3):
                link(pool.memset(steps[:, 0, j:j + 1], (j + 1) << 28))
            link(pool.memset(reset_g[:], 1.0))
            link(pool.memset(reset_g[:, :, 0:1], 0.0))
            link(pool.memset(reset_e[:], 1.0))
            link(pool.memset(reset_e[:, :, 0:1], 0.0))
            link(pool.memset(ones_b[:], 1.0))
            link(pool.memset(ones_r[:].bitcast(F32), 1.0))
            pool.memset(ones_f[:], 1.0).then_inc(pool_consts, 1)
            pool.wait_ge(pool_consts, 1)
            pool.memset(VB[:], 0.0).then_inc(vb_init, 1)
            pool.wait_ge(vb_init, 1)
            link(pool.memset(VB[0:SE, :, :, 0, DK:DK + 1], 1.0))
            pool.memset(VB[SE:P, :, :, 1, DK:DK + 1], 1.0).then_inc(vb_init, 1)
            pool.wait_ge(vb_init, 2)
            sel = ksf_s[KQ:KQ + 4]
            link(pool.memset(sel, 0.0))
            for base in (0, -2):
                link(pool.affine_select(out=sel, in_=sel, compare_op=ALU.not_equal, fill=1.0, base=base,
                                        pattern=[[0, PR * B], [-1, 2], [0, SE]], channel_multiplier=1))
            pool.tensor_copy(KS[KQ:KQ + 4], sel.rearrange("p j b h k -> p j b (h k)")).then_inc(ks_made, 1)
            pool.wait_ge(ks_made, 1)
            pool.wait_ge(bias1_in, 16 * 4)
            for n in range(NB):
                wait_filled(pool, ("xt", n, KC - 1))
                xs = X[:, TPB * n:TPB * (n + 1), 0:D]
                pool.tensor_tensor(xs, xs, b_out_all[:].unsqueeze(1).to_broadcast([P, TPB, D]), ALU.add)\
                    .then_inc(xb_added, 1)
            pool.wait_ge(head_masks, 1)
            for c in range(KC):
                wait_moved(pool, ("kt", c))
                for b in range(B):
                    pool.tensor_tensor(
                        KM[:, b, c], kt_s[:, c, b * SE:(b + 1) * SE].unsqueeze(1).to_broadcast([P, HD // KC, SE]),
                        mask_hi3[:].unsqueeze(2).to_broadcast([P, HD // KC, SE]), ALU.mult).then_inc(km_made, 1)
            pool.wait_ge(ks_hi, 1)
            pool.wait_ge(km_made, 4)
            pool.tensor_tensor(KS[32:64], ksf_s[32:64].rearrange("p j b h k -> p j b (h k)"),
                               KS[32:64].bitcast(F32), ALU.subtract).then_inc(ks_made, 1)
            pool.wait_ge(ks_made, 2)
            for n in range(2, NB):
                for c in range(KC):
                    pool.wait_ge(y_hi, KC * n + c + 1)
                    pool.tensor_tensor(YL[:, n, c], G[:, n, c], YH[:, n, c].bitcast(F32), ALU.subtract)\
                        .then_inc(y_lo_pool, 1)

            def root(k):
                pool.wait_ge(ln_var, k + 1)
                pool.tensor_tensor(rstd[:, k:k + 1], var_eps[:, k:k + 1], neg_half[:, 0:1], ALU.pow)\
                    .then_inc(ln_rstd, 1)

            pool.wait_ge(bias2_in, 16 * (4 + NG))
            k = 0
            for s in range(TPB):
                root(k)
                k += 1
            for n in range(NB + 3):
                if n < NB:
                    wait_filled(pool, ("x1t", n, KC - 1))
                    xs = X[:, TPB * n:TPB * (n + 1), 0:D]
                    pool.tensor_tensor(xs, xs, bo_all[:].unsqueeze(1).to_broadcast([P, TPB, D]), ALU.add)\
                        .then_inc(bo_added, 1)
                for _ in range(TPB * (n + 1 < NB) + TPB * (0 <= n - 2 < NB)):
                    root(k)
                    k += 1
            assert k == 2 * NT
            phase2_over(pool)

            def up_low(g):
                pool.wait_ge(wu_hi, g + 1)
                pool.tensor_tensor(WUL[:, g % 2], WUR[:, g % 2], WUH[:, g % 2].bitcast(F32), ALU.subtract)\
                    .then_inc(wu_lo_pool, 1)

            def down_low(e):
                pool.wait_ge(wd_hi, e + 1)
                if e >= 3:
                    wait_filled(pool, ("dn", e - 3, 1))
                pool.tensor_tensor(WDL[:, e % 3, 0:FC - 1], WDR[:, e % 2, 0:FC - 1],
                                   WDH[:, e % 3, 0:FC - 1].bitcast(F32), ALU.subtract)
                f = FW[-1]
                pool.tensor_tensor(WDL[0:f, e % 3, FC - 1], WDR[0:f, e % 2, FC - 1],
                                   WDH[0:f, e % 3, FC - 1].bitcast(F32), ALU.subtract)
                pool.tensor_tensor(BDL[:, e % 3], BDR[:, e % 2], BDH[:, e % 3].bitcast(F32), ALU.subtract)\
                    .then_inc(wd_lo, 1)

            up_low(0)
            down_low(0)
            down_low(1)
            up_low(1)
            pool.wait_ge(idx_made, 1)
            pool.wait_ge(routed_out, 64)
            pool.wait_ge(summed_out, 64)
            for s in range(NT):
                pool.indirect_dma_start(
                    XG[:, s, :], None, routed,
                    bass.IndirectOffsetOnAxis(ap=idx[:, s:s + 1].bitcast(U32), axis=0)).then_inc(gathered[s // 2], 16)
            down_low(2)

            for e in range(E):
                if e:
                    pool.wait_ge(scattered[e - 1], 32)
                for h in range(2):
                    wait_moved(pool, ("dn", e, h))
                    pool.indirect_dma_start(
                        summed, bass.IndirectOffsetOnAxis(ap=idx[:, 2 * e + h:2 * e + h + 1].bitcast(U32), axis=0),
                        OUT[:, (2 * e + h) % 4, :], None, compute_op=ALU.add).then_inc(scattered[e], 16)
                if e + 3 < E:
                    down_low(e + 3)
            for q in range(4):
                k = 2 * NT + 4 * q
                pool.wait_ge(ln_var, 2 * NT + q + 1)
                pool.tensor_tensor(rstd[:, k:k + 4], var_eps[:, k:k + 4], neg_half[:, 0:4], ALU.pow)\
                    .then_inc(ln_rstd, 1)

        @block.scalar
        def _(act):
            link = chain(act, act_step)
            with nc.allow_non_contiguous_dma(reason="short bias columns"):
                act.wait_ge(win_zero, 1)
                act.dma_start(win_s[:, :, NS:P], w_in.rearrange("(c p) n -> p c n", p=P)).then_inc(win_in, 16)
                act.dma_start(b_in_c[NS:P, :], b_in.rearrange("(p a) -> p a", a=1)).then_inc(bias1_in, 16)
                act.dma_start(b_gate_c[:], b_gate.rearrange("(c p) -> p c", p=P)).then_inc(bias1_in, 16)
                act.dma_start(bq_c[:], bq.rearrange("(c p) -> p c", p=P)).then_inc(bias1_in, 16)
                act.dma_start(b_out_all[:], b_out.rearrange("(a n) -> a n", a=1).to_broadcast([P, D]))\
                    .then_inc(bias1_in, 16)
                act.dma_start(cd_s[:, :, 0:NS], c_mat.rearrange("(c p) n -> p c n", p=P)).then_inc(cd_in, 16)
                act.dma_start(cd_s[:, :, NS:P], d_mat.rearrange("(c p) n -> p c n", p=P)).then_inc(cd_in, 16)
                act.dma_start(ctx_s[:], ctx.rearrange("b s d -> (b s) d")).then_inc(kv_in, 16)
                act.dma_start(wk_s[:], wk.rearrange("(c p) n -> p c n", p=P)).then_inc(kv_in, 16)
                act.dma_start(wv_s[:], wv.rearrange("(c p) n -> p c n", p=P)).then_inc(kv_in, 16)
                act.dma_start(bk_c[:], bk.rearrange("(c p) -> p c", p=P)).then_inc(kv_in, 16)
                for k in range(3):
                    act.dma_start(bk3_c[32 * k:32 * k + 32, :], bk.rearrange("(j p) -> p j", p=32))\
                        .then_inc(kv_in, 16)
                act.dma_start(bv_row[:], bv.rearrange("(a n) -> a n", a=1)).then_inc(kv_in, 16)
                act.dma_start(bo_all[:], bo.rearrange("(a n) -> a n", a=1).to_broadcast([P, D]))\
                    .then_inc(bias2_in, 16)
                act.dma_start(br_all[:], br.rearrange("(a n) -> a n", a=1).to_broadcast([P, E]))\
                    .then_inc(bias2_in, 16)
                act.dma_start(wr_s[:], wr.rearrange("(c p) n -> p c n", p=P)).then_inc(bias2_in, 16)
                full = (FC - 1) * P
                for g in range(NG):
                    act.dma_start(b_up_c[:, g, 0:FC - 1], b_up[g, 0:full].rearrange("(c p) -> p c", p=P))\
                        .then_inc(bias2_in, 16)
                act.dma_start(b_up_c[0:FW[-1], :, FC - 1], b_up[:, full:F].rearrange("g p -> p g"))\
                    .then_inc(bias2_in, 16)

            def whole(w, src, arrived):
                act.wait_ge(arrived, 16)
                act.activation(w[0][:], src[:], ACT.Copy).then_inc(w_hi, 1)

            whole(WIN, win_s, win_in)
            for n in range(NB):
                for c in range(KC):
                    wait_filled(act, ("xt", n, c))
                    act.activation(XH[:, n, c], bank[c][:], ACT.Copy).then_inc(xh_made, 1)
                if n == 0:
                    act.wait_ge(bias1_in, 64)
                wait_filled(act, ("u", n))
                act.activation(HU[NS:P, n * BLK:(n + 1) * BLK], bank_of(("u", n))[NS:P, :], ACT.Identity,
                               bias=b_in_c[NS:P, :]).then_inc(sem_moved(("u", n)), 1)
                m = POWERS[n]
                wait_filled(act, ("tw", m))
                act.activation(TW[:, n + 1, :], bank[5][0:NS, 0:NS], ACT.Copy).then_inc(moved[5], 1)
                if n == 1:
                    whole(WG, wg_s, wg_in)
            whole(WOUT, wout_s, wout_in)
            whole(WQ, wq_s, wq_in)
            whole(WO, wo_s, wo_in)
            wait_filled(act, "w1")
            act.activation(W1[0][:], bank[7][:, 0:D], ACT.Copy).then_inc(w_hi, 1)
            for i in range(L):
                if i % 2 == 1 and 4 + i // 2 < 9:
                    m = POWERS[4 + i // 2]
                    if m < 256:
                        wait_filled(act, ("tw", m))
                        act.activation(TW[:, 5 + i // 2, :], bank[5][0:NS, 0:NS], ACT.Copy).then_inc(moved[5], 1)
                if i % 2 == 1:
                    g = i // 2
                    n, c = g // 2, g % 2
                    wait_filled(act, ("gate", g))
                    act.activation(G[:, n, c], bank_of(("gate", g))[:], ACT.Sigmoid,
                                   bias=b_gate_c[:, c:c + 1]).then_inc(sem_moved(("gate", g)), 1)
            act.wait_ge(kv_in, 128)
            for c in range(KC):
                wait_filled(act, ("kt", c))
                act.activation(kt_s[:, c], bank[c][:, 0:B * SE], ACT.Identity, bias=bk_c[:, c:c + 1])\
                    .then_inc(moved[c], 1)
            for n in range(NB):
                act.wait_ge(h_start, 1)
                wait_moved(act, ("cor", 1 + 2 * (n % 2)))
                wait_moved(act, ("cor", 2 * (n % 2)))
                act.activation(HUH[:, n * BLK:(n + 1) * BLK], HU[:, n * BLK:(n + 1) * BLK], ACT.Copy)\
                    .then_inc(hu_hi, 1)
            for n in range(NB):
                for c in range(KC):
                    wait_moved(act, ("y", n, c))
                    act.activation(YH[:, n, c], G[:, n, c], ACT.Copy).then_inc(y_hi, 1)
            for n in range(NB + 3):
                r = n % 2
                if n < NB:
                    for c in range(KC):
                        wait_filled(act, ("x1t", n, c))
                        if n < 2:
                            act.wait_ge(y_hi, 4 * n + 4)
                            act.wait_ge(*((y_lo_dve, 4), (y_lo_pool, 4))[n])
                        else:
                            wait_filled(act, ("q", n - 2, KC - 1))
                        act.activation(X1H[r][:, c], bank[c][:], ACT.Copy).then_inc(x1h_made, 1)
                    for c in range(KC):
                        wait_filled(act, ("q", n, c))
                        wait_filled(act, ("z1", n % 2, TPB - 1))
                        if n >= 2:
                            wait_filled(act, ("mx", n - 2, TPB - 1, KC - 1))
                            act.wait_ge(qs_in[r], 16 * 4 * PR * (n // 2))
                        act.activation(QH[:, r, c], bank_of(("q", n, c))[:], ACT.Identity,
                                       bias=bq_c[:, c:c + 1]).then_inc(q_hi, 1)
                if 0 <= n - 3:
                    for s in range(TPB):
                        wait_filled(act, ("x2t", n - 3, s))
                        if s >= 2:
                            wait_filled(act, ("lg", n - 3, s - 2))
                        elif n > 3:
                            wait_filled(act, ("lg", n - 4, s + 2))
                        act.activation(X2T[:, s % 2, :], bank[s % 2][:, 0:D], ACT.Copy)\
                            .then_inc(moved[s % 2], 1)
                if n < NB:
                    wait_filled(act, ("nmt", n))
                    act.activation(NMT[0:32, r, :], bank[0][0:32, :], ACT.Copy).then_inc(moved[0], 1)
                if 0 <= n - 2 < NB:
                    for s in range(TPB):
                        wait_filled(act, ("att", n - 2, s))
                        if s >= 2:
                            wait_filled(act, ("z2", n - 2, s - 2))
                        elif n > 2:
                            wait_filled(act, ("z2", n - 3, s + 2))
                        act.activation(ATH[:, s % 2], bank[s % 2][:, 0:D], ACT.Copy).then_inc(ath_made, 1)
                if n < NB:
                    if n == 0:
                        act.wait_ge(ks_made, 2)
                        act.wait_ge(km_made, 4)
                    if n >= 2:
                        wait_filled(act, ("pv", n - 2, TPB - 1))
                    for j in range(PR):
                        wait_filled(act, ("sc", n, j))
                        act.activation(PT[r][:, j, :], bank_of(("sc", n, j))[:], ACT.Exp, scale=SCALE)\
                            .then_inc(sem_moved(("sc", n, j)), 1)
            act.wait_ge(lm_made, 1)
            act.activation(ex[:], lm[:], ACT.Exp).then_inc(ex_made, 1)
            act.wait_ge(s2_made, 1)
            act.activation(X[:, :, D:RW], S2[:], ACT.Copy).then_inc(routed_made, 1)

            def down_high(e):
                act.wait_ge(wd_in[e % 2], 48 * (e // 2 + 1))
                if e >= 3:
                    wait_filled(act, ("dn", e - 3, 1))
                act.activation(WDH[:, e % 3, 0:FC - 1], WDR[:, e % 2, 0:FC - 1], ACT.Copy)
                f = FW[-1]
                act.activation(WDH[0:f, e % 3, FC - 1], WDR[0:f, e % 2, FC - 1], ACT.Copy)
                act.activation(BDH[:, e % 3], BDR[:, e % 2], ACT.Copy).then_inc(wd_hi, 1)

            def up_high(g):
                act.wait_ge(wu_in[g % 2], 16 * (g // 2 + 1))
                if g >= 2:
                    wait_filled(act, ("up", g - 2, FC - 1))
                act.activation(WUH[:, g % 2], WUR[:, g % 2], ACT.Copy).then_inc(wu_hi, 1)

            up_high(0)
            down_high(0)
            down_high(1)
            up_high(1)
            down_high(2)
            for g in range(NG):
                for c in range(KC):
                    wait_filled(act, ("gt", g, c))
                    if g >= 2:
                        wait_filled(act, ("up", g - 2, FC - 1))
                    act.activation(FTH[:, g % 2, c], bank[5 + c][:], ACT.Copy).then_inc(fth_made, 1)
                if g >= 2:
                    down_high(2 * g)
                for f in range(FC):
                    wait_filled(act, ("up", g, f))
                    q = g * FC + f
                    if q >= 3:
                        act.wait_ge(ml_made, q - 2)
                    act.activation(MF[0:FW[f], q % 3], bank[f % 3][0:FW[f], :], ACT.Silu,
                                   bias=b_up_c[0:FW[f], g, f:f + 1]).then_inc(moved[f % 3], 1)
                    if f == 1 and 2 <= g + 1 < NG:
                        up_high(g + 1)
                if g >= 1:
                    down_high(2 * g + 1)

        @block.tensor
        def _(pe):
            order = [0] * 8

            def turn(name):
                k, u = turn_of[name]
                assert order[k] == u, name
                order[k] += 1
                if u:
                    pe.wait_ge(moved[k], u)
                return bank[k]

            def split_matmuls(o, pairs):
                last, n = None, 0
                for (ah, al), (bh, bl) in pairs:
                    for a, b in ((ah, bh), (ah, bl), (al, bh)):
                        last = pe.matmul(o, a, b, start=(n == 0), stop=(n == 3 * len(pairs) - 1))
                        n += 1
                return last

            def both(w, *at):
                return tuple(x[at] for x in w)

            ALLP = slice(None)
            pe.wait_ge(ident_made, 1)
            pe.wait_ge(ab_in, 48)
            o = turn("ab")
            pe.transpose(o[0:NS, 0:P], ab_s[:, :], ident[:]).then_inc(filled[6], 1)

            def power(m):
                l = POWERS.index(m)
                o = turn(("pw", m))
                width = m if m <= 8 else 1
                pe.wait_ge(tw1_made, 1)
                if m > 1:
                    wait_moved(pe, ("tw", m // 2))
                    wait_moved(pe, ("pw", m // 2))
                rhs = PW[:, 1:m + 1, :] if m <= 8 else (PW[:, 16, :] if m == 16 else PB[:, l - 5, :])
                own = PW[:, m, :] if m <= 16 else PB[:, l - 5, :]
                pe.matmul(o[0:NS, 0:width * NS], TW[:, l, :], rhs, start=True, stop=True).then_inc(filled[4], 1)
                if m < 256:
                    o = turn(("tw", m))
                    pe.matmul(o[0:NS, 0:NS], own, TW[:, l, :], start=True, stop=True).then_inc(filled[5], 1)

            for n in range(NB):
                pe.wait_ge(x_in[n], 32)
                for c in range(KC):
                    o = turn(("xt", n, c))
                    for s in range(TPB):
                        last = pe.transpose(o[:, s * P:(s + 1) * P], X[:, TPB * n + s, c * P:(c + 1) * P], ident[:])
                    last.then_inc(filled[c], 1)
                if n == 0:
                    pe.wait_ge(w_hi, 1)
                    pe.wait_ge(w_lo, 1)
                o = turn(("u", n))
                wait_moved(pe, ("xt", n, 0))
                wait_moved(pe, ("xt", n, 1))
                split_matmuls(o[:, :], [
                    (both(WIN, ALLP, c, ALLP), (XH[:, n, c], XL[:, n, c])) for c in range(KC)
                ]).then_inc(sem_filled(("u", n)), 1)
                power(POWERS[n])
            pe.wait_ge(cd_in, 32)
            o = turn("cd")
            for c in range(KC):
                last = pe.transpose(o[:, c * P:(c + 1) * P], cd_s[:, c, :], ident[:])
            last.then_inc(filled[0], 1)
            pe.wait_ge(kv_in, 128)
            o = turn("ctx")
            for c in range(KC):
                last = pe.transpose(o[:, c * P:(c + 1) * P], ctx_s[:, c * P:(c + 1) * P], ident[:])
            last.then_inc(filled[1], 1)
            o = turn("w1")
            wait_moved(pe, "cd")
            pe.wait_ge(mx_made, 1)
            pe.matmul(o[:, 0:D], mx_s[:], cdt_s[:], start=True, stop=True).then_inc(filled[7], 1)

            hu4 = HU[:].rearrange("p (b i c) -> p b i c", b=B, i=L)
            for n in range(NB):
                wait_moved(pe, ("u", n))
            pe.wait_ge(w_hi, 2)
            pe.wait_ge(w_lo, 2)
            pe.wait_ge(starts_zero, 1)
            gate_bank = None
            for i in range(L):
                o = turn(("step", i))
                if i:
                    wait_moved(pe, ("step", i - 1))
                pe.matmul(o[0:NS, 0:B * CH], ab_s[:], hu4[:, :, i, :], start=True, stop=True)\
                    .then_inc(sem_filled(("step", i)), 1)
                g = i // 2
                n, m = g // 2, g % 2
                if i % 2 == 0:
                    gate_bank = turn(("gate", g))
                k = 0
                for c in range(KC):
                    for a, b in ((0, 0), (0, 1), (1, 0)):
                        if k // 3 == i % 2:
                            last = pe.matmul(gate_bank[:, :], WG[a][:, c, m * P:(m + 1) * P], (XH, XL)[b][:, n, c],
                                             start=(k == 0), stop=(k == 5))
                        k += 1
                if i % 2 == 1:
                    last.then_inc(sem_filled(("gate", g)), 1)
                    if 4 + i // 2 < 9:
                        power(POWERS[4 + i // 2])
            pe.wait_ge(wk3_made, 1)
            for k, d in enumerate(LEVELS):
                o = turn(("carry", k))
                if k:
                    wait_moved(pe, ("carry", k - 1))
                else:
                    wait_moved(pe, ("step", L - 1))
                    wait_moved(pe, ("pw", 256))
                own = PW[:, 16, :] if k == 0 else PB[:, k - 1, :]
                pe.matmul(o[0:NS, 0:B * (CH - d)], own, HS[:, :, 1:1 + CH - d], start=True, stop=True)\
                    .then_inc(sem_filled(("carry", k)), 1)
                if k < 2:
                    o = turn(("kt", k))
                    wait_moved(pe, "ctx")
                    for c in range(KC):
                        last = pe.matmul(o[:, 0:B * SE], wk_s[:, c, k * P:(k + 1) * P], ctd_s[:, c, :, 0, :],
                                         start=(c == 0), stop=(c == KC - 1))
                    last.then_inc(filled[k], 1)
                    o = turn(("v", k))
                    for c in range(KC):
                        pe.matmul(o[:, 0:D], ctd_s[:, c, k].rearrange("p r s -> p (r s)"), wv_s[:, c, :],
                                  start=(c == 0), stop=False)
                    pe.matmul(o[:, 0:D], ones_f[0:1, :], bv_row[:], start=False, stop=True)\
                        .then_inc(filled[4 + k], 1)
                for j in KSP[k]:
                    o = turn(("ks", j))
                    for c in range(KC):
                        last = pe.matmul(o[0:KQ, 0:B * SE], wk3_s[:, c * PR + j].rearrange("p r s -> p (r s)"),
                                         ctd_s[:, c, :, 0, :], start=(c == 0), stop=(c == KC - 1))
                    last.then_inc(sem_filled(("ks", j)), 1)
            wait_moved(pe, ("carry", 5))
            for q in range(4):
                o = turn(("cor", q))
                for i in range(4 * q, 4 * q + 4):
                    if i:
                        last = pe.matmul(o[0:NS, (i % 4) * P:(i % 4 + 1) * P], PW[:, i, :], HS[:, :, 0:CH],
                                         start=True, stop=True)
                last.then_inc(sem_filled(("cor", q)), 1)
            wait_moved(pe, "w1")
            pe.wait_ge(w_lo, 5)
            for n in range(NB):
                pe.wait_ge(hu_lo, n + 1)
                for c in range(KC):
                    o = turn(("y", n, c))
                    cols = slice(n * BLK, (n + 1) * BLK)
                    split_matmuls(o[:, :], [(both(W1, ALLP, slice(c * P, (c + 1) * P)), (HUH[:, cols], HUL[:, cols]))])\
                        .then_inc(filled[2 + c], 1)

            def mixer_out(n):
                pe.wait_ge(y_hi, KC * (n + 1))
                if n < 2:
                    pe.wait_ge(y_lo_dve, KC * (n + 1))
                else:
                    pe.wait_ge(y_lo_pool, KC * (n - 1))
                for s in range(TPB):
                    o = turn(("z1", n, s))
                    cols = slice(s * P, (s + 1) * P)
                    split_matmuls(o[:, 0:D], [
                        ((YH[:, n, c, cols], YL[:, n, c, cols]), both(WOUT, ALLP, c, ALLP)) for c in range(KC)
                    ]).then_inc(sem_filled(("z1", n, s)), 1)

            mixer_out(0)
            for n in range(NB + 3):
                r = n % 2
                if n < NB:
                    pe.wait_ge(ln_out, norm_at[1, TPB * (n + 1) - 1] + 1)
                    for c in range(KC):
                        o = turn(("x1t", n, c))
                        for s in range(TPB):
                            last = pe.transpose(o[:, s * P:(s + 1) * P], X[:, TPB * n + s, c * P:(c + 1) * P], ident[:])
                        last.then_inc(filled[c], 1)
                    for c in range(KC):
                        o = turn(("q", n, c))
                        wait_moved(pe, ("x1t", n, 0))
                        wait_moved(pe, ("x1t", n, 1))
                        split_matmuls(o[:, :], [
                            (both(WQ, ALLP, k, slice(c * P, (c + 1) * P)), (X1H[r][:, k], X1L[r][:, k]))
                            for k in range(KC)
                        ]).then_inc(filled[2 + c], 1)
                if 0 <= n - 3:
                    def logits(s):
                        o = turn(("lg", n - 3, s))
                        wait_moved(pe, ("x2t", n - 3, s))
                        for c in range(KC):
                            last = pe.matmul(o[:, 0:E], X2T[:, s % 2, c * P:(c + 1) * P], wr_s[:, c, :],
                                             start=(c == 0), stop=(c == KC - 1))
                        last.then_inc(sem_filled(("lg", n - 3, s)), 1)

                    if n == 3:
                        pe.wait_ge(bias2_in, 16 * (4 + NG))
                    for s in range(TPB):
                        t = TPB * (n - 3) + s
                        pe.wait_ge(ln_out, norm_at[2, t] + 1)
                        o = turn(("x2t", n - 3, s))
                        for c in range(KC):
                            last = pe.transpose(o[:, c * P:(c + 1) * P], X[:, t, c * P:(c + 1) * P], ident[:])
                        last.then_inc(filled[s % 2], 1)
                        if s:
                            logits(s - 1)
                    logits(TPB - 1)
                if n + 1 < NB:
                    mixer_out(n + 1)
                if n < NB:
                    if n == 0:
                        pe.wait_ge(km_made, 4)
                    wait_moved(pe, ("q", n, 0))
                    wait_moved(pe, ("q", n, 1))
                    for s in range(TPB):
                        for c in range(KC):
                            o = turn(("mx", n, s, c))
                            pe.matmul(o[:, :], QH[:, r, c, s * P:(s + 1) * P],
                                      KM[:, n // 2, c].rearrange("p h k -> p (h k)"), start=True, stop=True)\
                                .then_inc(filled[2 + c], 1)
                    o = turn(("nmt", n))
                    for s in range(TPB):
                        pe.wait_ge(nm_made, TPB * n + s + 1)
                        last = pe.transpose(o[0:32, s * P:(s + 1) * P],
                                            NMS[:, s].rearrange("p j l h -> p (j l h)").bitcast(F32), ident[:])
                    last.then_inc(filled[0], 1)
                if 0 <= n - 2 < NB:
                    def project(s):
                        o = turn(("z2", n - 2, s))
                        wait_moved(pe, ("att", n - 2, s))
                        split_matmuls(o[:, 0:D], [
                            ((ATH[:, s % 2, c], ATL[:, s % 2, c]), both(WO, ALLP, c, ALLP)) for c in range(KC)
                        ]).then_inc(sem_filled(("z2", n - 2, s)), 1)

                    for s in range(TPB):
                        wait_moved(pe, ("pv", n - 2, s))
                        o = turn(("att", n - 2, s))
                        for c in range(KC):
                            last = pe.transpose(o[:, c * P:(c + 1) * P], ATT[:, s, c * P:(c + 1) * P], ident[:])
                        last.then_inc(filled[s % 2], 1)
                        if s:
                            project(s - 1)
                    project(TPB - 1)
                if n < NB:
                    pe.wait_ge(ks_made, 2)
                    pe.wait_ge(qs_in[r], 16 * 4 * PR * (n // 2 + 1))
                for j in range(PR):
                    if n < NB:
                        o = turn(("sc", n, j))
                        pe.matmul(o[:, :], KS[0:KQ + 4, j, n // 2, :], QS[0:KQ + 4, r, j, :], start=True, stop=True)\
                            .then_inc(sem_filled(("sc", n, j)), 1)
                    m = n - 1
                    if 0 <= m < NB:
                        s, half = j // 2, j % 2
                        if half == 0:
                            o_pv = turn(("pv", m, s))
                        if m == 0:
                            pe.wait_ge(vb_made, 2)
                            wait_moved(pe, ("v", 1))
                        for jj in range(4 * half, 4 * half + 4):
                            wait_moved(pe, ("sc", m, jj))
                            last = pe.matmul(o_pv[:, jj * 34:(jj + 1) * 34], PT[m % 2][:, jj, s * P:(s + 1) * P],
                                             VB[:, m // 2, jj].rearrange("p h d -> p (h d)"), start=True, stop=True)
                        if half == 1:
                            last.then_inc(sem_filled(("pv", m, s)), 1)

            pe.wait_ge(s2_made, 1)
            o = turn("st")
            pe.transpose(o[:, 0:P], S2[:].rearrange("p t e -> p (t e)"), ident[:]).then_inc(filled[0], 1)
            pe.wait_ge(masks_made, 1)
            for r in range(ROUNDS):
                o = turn(("tot", r))
                pe.wait_ge(cnt_made, r + 1)
                pe.matmul(o[:, 0:3], same_expert[:], cnt[:, r, :], start=True, stop=True)\
                    .then_inc(sem_filled(("tot", r)), 1)
            pe.wait_ge(rt_made, 1)
            o = turn("thr")
            pe.matmul(o[:, 0:E], ones_f[:], rt[:], start=True, stop=True).then_inc(filled[3], 1)
            pe.wait_ge(prefix_in, 1)
            rows_g = cig[:, :, NT - 1:NT].to_broadcast([P, E, NT])
            rows_e = cie[:, :, NT // B - 1:NT // B].to_broadcast([P, E * B, NT // B])
            flat = lambda t: t[:].rearrange("p e t -> p (e t)")
            o = turn("pg")
            pe.matmul(o[:, 0:P], before_b[:], rows_g, start=True, stop=False)
            pe.matmul(o[:, 0:P], ident_b[:], flat(cxg), start=False, stop=True).then_inc(filled[4], 1)
            o = turn("pe")
            pe.matmul(o[:, 0:P], chunk_before_b[:], rows_e, start=True, stop=False)
            pe.matmul(o[:, 0:P], even_to_odd_b[:], flat(cie), start=False, stop=False)
            pe.matmul(o[:, 0:P], own_odd_to_even_b[:], flat(cxe), start=False, stop=False)
            second = o[:, 0:P].rearrange("p (e b j) -> p e b j", e=E, b=B)[:, :, 1, :]
            first_rows = cie[:].rearrange("p (e b) j -> p e b j", b=B)[:, :, 0, NT // B - 1:NT // B]
            pe.matmul(second, ones_b[:], first_rows.to_broadcast([P, E, NT // B]), start=False, stop=False)
            pe.matmul(o[:, 0:P], ones_b[:], rows_g, start=False, stop=True).then_inc(filled[5], 1)
            pe.wait_ge(onehot_made, 1)
            o = turn("ids")
            for t in range(NT):
                last = pe.matmul(o[:, 0:P], OHH[:, t].rearrange("p e s -> p (e s)"),
                                 OHI[:, t].rearrange("p e s -> p (e s)"), start=(t == 0), stop=(t == NT - 1))
            last.then_inc(filled[6], 1)
            pe.wait_ge(lh_made, 1)
            o = turn("idx")
            pe.matmul(o[:, 0:16], lh[:].rearrange("p a l -> p (a l)"), mask_16[:], start=True, stop=True)\
                .then_inc(filled[7], 1)

            def tokens(g):
                for c in range(KC):
                    o = turn(("gt", g, c))
                    for k in range(2 * GS):
                        if c == 0 and k % 2 == 0:
                            pe.wait_ge(gathered[GS * g + k // 2], 32)
                        last = pe.transpose(o[:, k * P:(k + 1) * P], XG[:, 2 * GS * g + k, c * P:(c + 1) * P], ident[:])
                    last.then_inc(filled[5 + c], 1)

            def up(g):
                pe.wait_ge(wu_hi, g + 1)
                wait_up_low(pe, g)
                wait_moved(pe, ("gt", g, 0))
                wait_moved(pe, ("gt", g, 1))
                for f in range(FC):
                    o = turn(("up", g, f))
                    cols = slice(f * P, f * P + FW[f])
                    split_matmuls(o[0:FW[f], :], [
                        ((WUH[:, g % 2, c, cols], WUL[:, g % 2, c, cols]), (FTH[:, g % 2, c], FTL[:, g % 2, c]))
                        for c in range(KC)]).then_inc(filled[f % 3], 1)

            def down(e):
                g, first = e // GS, (e % GS) * TOP
                pe.wait_ge(wd_hi, e + 1)
                pe.wait_ge(wd_lo, e + 1)
                pe.wait_ge(ml_made, FC * (g + 1))
                for h in range(2):
                    o = turn(("dn", e, h))
                    pe.matmul(o[:, 0:D], ones_r[0:1, :], BDH[:, e % 3], start=True, stop=False)
                    pe.matmul(o[:, 0:D], ones_r[0:1, :], BDL[:, e % 3], start=False, stop=False)
                    cols = slice(first + h * P, first + (h + 1) * P)
                    for f in range(FC):
                        w = FW[f]
                        for a, b in ((MH, WDH), (MH, WDL), (ML, WDH)):
                            last = pe.matmul(o[:, 0:D], a[0:w, g % 2, f, cols], b[0:w, e % 3, f],
                                             start=False, stop=(f == FC - 1 and b is WDH and a is ML))
                    last.then_inc(filled[3 + h], 1)

            tokens(0)
            up(0)
            for g in range(1, NG + 1):
                if g < NG:
                    tokens(g)
                    up(g)
                for e in range(GS * (g - 1), GS * g):
                    down(e)

        @block.vector
        def _(dve):
            link = chain(dve, dve_step)

            def low(w, src, n):
                dve.wait_ge(w_hi, n)
                dve.tensor_tensor(w[1][:], src[:], w[0][:].bitcast(F32), ALU.subtract).then_inc(w_lo, 1)

            wait_filled(dve, "ab")
            dve.tensor_copy(mx_s[0:NS, :], bank[6][0:NS, 0:P]).then_inc(moved[6], 1)
            wait_moved(dve, "ab")
            dve.tensor_copy(TW[:, 0, :], mx_s[0:NS, 0:NS]).then_inc(tw1_made, 1)
            low(WIN, win_s, 1)
            for n in range(NB):
                for c in range(KC):
                    dve.wait_ge(xh_made, KC * n + c + 1)
                    dve.tensor_tensor(XL[:, n, c], bank[c][:], XH[:, n, c].bitcast(F32), ALU.subtract)\
                        .then_inc(moved[c], 1)
                m = POWERS[n]
                wait_filled(dve, ("pw", m))
                dve.tensor_copy(PW[:, m + 1:2 * m + 1, :],
                                bank[4][0:NS, 0:m * NS].rearrange("p (k n) -> p k n", n=NS)).then_inc(moved[4], 1)
            low(WG, wg_s, 2)
            wait_filled(dve, "cd")
            dve.tensor_copy(cdt_s[:], bank[0][:, 0:D]).then_inc(moved[0], 1)
            wait_filled(dve, "ctx")
            for c in range(KC):
                last = dve.tensor_copy(ctd_s[:, c], bank[1][:, c * P:(c + 1) * P].rearrange("p (b s) -> p b s", b=B)
                                       .unsqueeze(2).to_broadcast([P, B, 2, SE]))
            last.then_inc(moved[1], 1)

            def between_steps(i):
                if i == 0:
                    dve.wait_ge(w_hi, 6)
                    dve.tensor_tensor(W1[1][:], bank[7][:, 0:D], W1[0][:].bitcast(F32), ALU.subtract)\
                        .then_inc(moved[7], 1)
                if i == 2:
                    low(WOUT, wout_s, 3)
                if i == 4:
                    low(WQ, wq_s, 4)
                if i == 6:
                    low(WO, wo_s, 5)
                if i == 8:
                    dve.wait_ge(kv_in, 128)
                    dve.tensor_copy(wk3_s[:], wk_s[:].rearrange("p c (j s) -> p (c j) s", s=32).unsqueeze(2)
                                    .to_broadcast([P, KC * PR, 3, 32])).then_inc(wk3_made, 1)
                if i == 10:
                    dve.wait_ge(pool_consts, 1)
                    dve.tensor_scalar(pbits[:, 0:1], pidx[:], 4, 1, ALU.logical_shift_right, ALU.bitwise_and)
                    dve.tensor_scalar(pbits[:, 1:2], pidx[:], 4, None, ALU.logical_shift_right)
                    link(dve.tensor_copy(col_f[:], col_i[:]))
                    link(dve.tensor_copy(pf[:, 0:2], pbits[:, 0:2]))
                    dve.tensor_scalar(half_mask[:, 0:1], pf[:, 0:1], 0.0, None, ALU.is_equal)
                    dve.tensor_scalar(half_mask[:, 1:2], pf[:, 0:1], 1.0, None, ALU.is_equal)
                    dve.tensor_scalar(mask_hi3[:], col_f[:, 0:8], pf[:, 1:2], None, ALU.is_equal)\
                        .then_inc(head_masks, 1)

            hu4 = HU[0:NS, :].rearrange("p (b i c) -> p b i c", b=B, i=L)
            for i in range(L):
                name = ("step", i)
                wait_filled(dve, name)
                got = bank_of(name)[0:NS, 0:B * CH].rearrange("p (b c) -> p b c", b=B)
                dst = hu4[:, :, i + 1, :] if i + 1 < L else HS[:, :, 1:CH + 1]
                dve.tensor_copy(dst, got).then_inc(sem_moved(name), 1)
                if i % 2 == 1 and 4 + i // 2 < 9:
                    m = POWERS[4 + i // 2]
                    wait_filled(dve, ("pw", m))
                    dst = PB[:, i // 2, :] if m >= 16 else None
                    dve.tensor_copy(dst, bank[4][0:NS, 0:NS]).then_inc(moved[4], 1)
                between_steps(i)
            for k, d in enumerate(LEVELS):
                name = ("carry", k)
                wait_filled(dve, name)
                if k == 0:
                    wait_moved(dve, ("step", L - 1))
                else:
                    wait_moved(dve, ("carry", k - 1))
                dve.tensor_tensor(HS[:, :, 1 + d:CH + 1], HS[:, :, 1 + d:CH + 1],
                                  bank_of(name)[0:NS, 0:B * (CH - d)].rearrange("p (b c) -> p b c", b=B), ALU.add)\
                    .then_inc(sem_moved(name), 1)
                if k < 2:
                    wait_filled(dve, ("v", k))
                    dve.wait_ge(vb_init, 2)
                    got = bank[4 + k][:, 0:D].rearrange("p (j h d) -> p j h d", j=PR, h=2)
                    dve.tensor_copy(VB[0:SE, k, :, 0, 0:DK], got[0:SE, :, 0, :]).then_inc(vb_made, 1)
                    dve.tensor_copy(VB[SE:P, k, :, 1, 0:DK], got[SE:P, :, 1, :]).then_inc(moved[4 + k], 1)
                for j in KSP[k]:
                    wait_filled(dve, ("ks", j))
                    got = bank_of(("ks", j))[0:KQ, 0:B * SE].rearrange("p (b s) -> p b s", b=B)
                    for h in range(2):
                        last = dve.tensor_scalar(ksf_s[0:KQ, j, :, h, :], got, bk3_c[0:KQ, j:j + 1],
                                                 half_mask[0:KQ, h:h + 1], ALU.add, ALU.mult)
                    last.then_inc(sem_moved(("ks", j)), 1)
            wait_moved(dve, ("carry", 5))
            dve.tensor_copy(hu4[:, :, 0, :], HS[:, :, 0:CH]).then_inc(h_start, 1)
            for q in range(4):
                name = ("cor", q)
                wait_filled(dve, name)
                i0 = 1 if q == 0 else 0
                to = hu4[:, :, 4 * q + i0:4 * q + 4, :]
                got = bank_of(name)[0:NS, :].rearrange("p (i b c) -> p b i c", i=4, b=B)[:, :, i0:, :]
                dve.tensor_tensor(to, to, got, ALU.add).then_inc(sem_moved(name), 1)
            for n in range(NB):
                dve.wait_ge(hu_hi, n + 1)
                cols = slice(n * BLK, (n + 1) * BLK)
                dve.tensor_tensor(HUL[:, cols], HU[:, cols], HUH[:, cols].bitcast(F32), ALU.subtract)\
                    .then_inc(hu_lo, 1)
            wait_moved(dve, ("ks", PR - 1))
            wait_moved(dve, ("ks", PR - 2))
            dve.tensor_copy(KS[0:KQ], ksf_s[0:KQ].rearrange("p j b h k -> p j b (h k)")).then_inc(ks_hi, 1)
            for n in range(NB):
                for c in range(KC):
                    wait_filled(dve, ("y", n, c))
                    wait_moved(dve, ("gate", 2 * n + c))
                    dve.tensor_tensor(G[:, n, c], bank[2 + c][:], G[:, n, c], ALU.mult).then_inc(moved[2 + c], 1)
                if n < 2:
                    for c in range(KC):
                        dve.wait_ge(y_hi, KC * n + c + 1)
                        dve.tensor_tensor(YL[:, n, c], G[:, n, c], YH[:, n, c].bitcast(F32), ALU.subtract)\
                            .then_inc(y_lo_dve, 1)

            def row(which, t):
                return Y[:, t, :] if which == 3 else X[:, t, 0:D]

            def statistics(which, t, name):
                k = norm_at[which, t]
                if t % TPB == 0:
                    dve.wait_ge(xb_added if which == 1 else bo_added, t // TPB + 1)
                wait_filled(dve, name)
                r = row(which, t)
                dve.tensor_tensor(r, bank_of(name)[:, 0:D], r, ALU.add).then_inc(sem_moved(name), 1)
                wait_moved(dve, name)
                link(dve.bn_stats(bn6[:, k, :], r))
                link(dve.bn_aggr(mean_var[:, k, :], bn6[:, k, :]))
                dve.tensor_scalar(var_eps[:, k:k + 1], mean_var[:, k, 1:2], EPS, None, ALU.add).then_inc(ln_var, 1)

            def normalise(which, t):
                k = norm_at[which, t]
                dve.wait_ge(ln_rstd, (k if which < 3 else 2 * NT + (k - 2 * NT) // 4) + 1)
                r = row(which, t)
                dve.tensor_scalar(r, r, mean_var[:, k, 0:1], rstd[:, k:k + 1], ALU.subtract, ALU.mult)\
                    .then_inc(ln_out, 1)

            def mixer_norms(n):
                for s in range(TPB):
                    statistics(1, TPB * n + s, ("z1", n, s))
                    if s:
                        normalise(1, TPB * n + s - 1)
                normalise(1, TPB * n + TPB - 1)

            def masks():
                for k, (sh, m) in enumerate(((0, 7), (0, 63), (3, 15), (6, 1))):
                    dve.tensor_scalar(pbits[:, 2 + k:3 + k], pidx[:], sh, m, ALU.logical_shift_right, ALU.bitwise_and)
                dve.tensor_scalar(colm_i[:], col_i[:], 63, None, ALU.bitwise_and)
                link(dve.tensor_copy(pf[:, 6:7], pidx[:]))
                dve.tensor_copy(pf[:, 2:6], pbits[:, 2:6])
                dve.tensor_copy(colm_f[:], colm_i[:])
                link(dve.tensor_copy(ident_b[:], ident[:]))
                dve.tensor_scalar(pf[:, 7:8], pf[:, 6:7], 64.0, None, ALU.add)
                dve.tensor_scalar(pf[:, 0:1], pf[:, 6:7], -64.0, None, ALU.add)
                link(dve.tensor_scalar(colm_i[:], col_i[:], 7, None, ALU.bitwise_and))
                dve.tensor_scalar(chunk_before_b[:], colm_f[:], pf[:, 3:4], None, ALU.is_gt)
                dve.tensor_scalar(pf[:, 1:2], pf[:, 3:4], 16.0, pf[:, 5:6], ALU.mult, ALU.add)
                dve.tensor_scalar(own_odd_to_even_b[:], col_f[:], pf[:, 0:1], None, ALU.is_equal)
                link(dve.tensor_copy(col7_f[:], colm_i[:]))
                dve.tensor_scalar(tok_f[:], tok_i[:], pf[:, 1:2], None, ALU.add)
                dve.tensor_scalar(same_expert[:], col7_f[:], pf[:, 2:3], None, ALU.is_equal)
                dve.tensor_scalar(before_b[:], col_f[:], pf[:, 6:7], None, ALU.is_gt)
                dve.tensor_scalar(even_to_odd_b[:], col_f[:], pf[:, 7:8], None, ALU.is_equal)
                dve.tensor_tensor(own_odd_to_even_b[:], own_odd_to_even_b[:], ident_b[:], ALU.add)
                dve.tensor_scalar(mask_lo3[:], col_f[:, 0:8], pf[:, 2:3], None, ALU.is_equal)
                dve.tensor_scalar(mask_16[:], col_f[:, 0:16], pf[:, 4:5], None, ALU.is_equal)
                for a, b, sh in ((1, 2, 2), (2, 4, 4), (4, 8, 8), (8, ROUNDS, 16)):
                    link(dve.tensor_scalar(steps[:, a:b, :], steps[:, 0:b - a, :], sh, None, ALU.logical_shift_right))
                dve.tensor_scalar(junk_m[:], col_f[:, 0:1], 0.0, None, ALU.mult).then_inc(masks_made, 1)

            mixer_norms(0)
            for n in range(NB + 3):
                r = n % 2
                if n < NB:
                    for c in range(KC):
                        dve.wait_ge(x1h_made, KC * n + c + 1)
                        dve.tensor_tensor(X1L[r][:, c], bank[c][:], X1H[r][:, c].bitcast(F32), ALU.subtract)\
                            .then_inc(moved[c], 1)
                    for c in range(KC):
                        dve.wait_ge(q_hi, KC * n + c + 1)
                        dve.scalar_tensor_tensor(QL[:, r, c], bank[2 + c][:], bq_c[:, c:c + 1],
                                                 QH[:, r, c].bitcast(F32), ALU.add, ALU.subtract)\
                            .then_inc(moved[2 + c], 1)
                if 0 <= n - 3:
                    if n == 3:
                        dve.wait_ge(bias2_in, 16 * (4 + NG))
                    for s in range(TPB):
                        name = ("lg", n - 3, s)
                        wait_filled(dve, name)
                        dve.tensor_tensor(lgt[:, TPB * (n - 3) + s, :], bank_of(name)[:, 0:E], br_all[:], ALU.add)\
                            .then_inc(sem_moved(name), 1)
                if n + 1 < NB:
                    mixer_norms(n + 1)
                if n < NB:
                    if n:
                        wait_filled(dve, ("nmt", n - 1))
                    for s in range(TPB):
                        for c in range(KC):
                            name = ("mx", n, s, c)
                            wait_filled(dve, name)
                            half = HD // KC
                            dve.tensor_reduce(NMF[:, s, c * half:(c + 1) * half],
                                              bank[2 + c][:].rearrange("p (h k) -> p h k", k=SE), AX.X, ALU.max,
                                              negate=True).then_inc(moved[2 + c], 1)
                            wait_moved(dve, name)
                        by_pair = NMF[:, s, :].rearrange("p (j h) -> p j h", h=2)
                        link(dve.tensor_copy(NMS[:, s, :, 0, :], by_pair))
                        dve.tensor_tensor(NMS[:, s, :, 1, :], by_pair, NMS[:, s, :, 0, :].bitcast(F32), ALU.subtract)\
                            .then_inc(nm_made, 1)
                if n == 1:
                    masks()
                if 0 <= n - 2 < NB:
                    m = n - 2
                    for s in range(TPB + 2):
                        if s < TPB:
                            dve.wait_ge(ath_made, TPB * m + s + 1)
                            dve.tensor_tensor(ATL[:, s % 2].rearrange("p c k -> p (c k)"), bank[s % 2][:, 0:D],
                                              ATH[:, s % 2].rearrange("p c k -> p (c k)").bitcast(F32), ALU.subtract)\
                                .then_inc(moved[s % 2], 1)
                        if 1 <= s <= TPB:
                            statistics(2, TPB * m + s - 1, ("z2", m, s - 1))
                        if s >= 2:
                            normalise(2, TPB * m + s - 2)
                m = n - 1
                if 0 <= m < NB:
                    if m:
                        wait_filled(dve, ("att", m - 1, TPB - 1))
                    for s in range(TPB):
                        name = ("pv", m, s)
                        wait_filled(dve, name)
                        got = bank_of(name)[:, 0:34 * PR].rearrange("p (h d) -> p h d", d=DK + 1)
                        link(dve.reciprocal(REC[:, s % 2, :].unsqueeze(2), got[:, :, DK:DK + 1]))
                        dve.tensor_tensor(ATT[:, s, :].rearrange("p (h d) -> p h d", d=DK), got[:, :, 0:DK],
                                          REC[:, s % 2, :].unsqueeze(2).to_broadcast([P, HD, DK]), ALU.mult)\
                            .then_inc(sem_moved(name), 1)

            phase2_over(dve)
            link(dve.tensor_reduce(mxl[:], lgt[:], AX.X, ALU.max))
            dve.tensor_tensor(lm[:], lgt[:], mxl[:].unsqueeze(2).to_broadcast([P, NT, E]), ALU.subtract)\
                .then_inc(lm_made, 1)
            dve.wait_ge(ex_made, 1)
            link(dve.tensor_reduce(sm[:], ex[:], AX.X, ALU.add))
            link(dve.reciprocal(rcp[:], sm[:]))
            dve.tensor_tensor(S2[:], ex[:], rcp[:].unsqueeze(2).to_broadcast([P, NT, E]), ALU.mult)\
                .then_inc(s2_made, 1)
            link(dve.memset(best[:, 0, 0:1], 0.0))
            wait_filled(dve, "st")
            dve.tensor_copy(ST[:], bank[0][:, 0:P]).then_inc(moved[0], 1)
            wait_moved(dve, "st")
            dve.wait_ge(masks_made, 1)
            link(dve.tensor_copy(cand[:, 0, :], steps[:, 0, :]))
            for r in range(ROUNDS):
                for j in range(3):
                    last = dve.tensor_scalar(junk[:, j, :], ST[:], cand[:, r, j:j + 1].bitcast(F32), 0.0, ALU.is_ge,
                                             ALU.add, accum_out=cnt[:, r, j:j + 1])
                last.then_inc(cnt_made, 1)
                name = ("tot", r)
                wait_filled(dve, name)
                dve.scalar_tensor_tensor(best[:, r, 1:4], bank_of(name)[:, 0:3], TOP - 0.5,
                                         cand[:, r, :].bitcast(F32), ALU.is_ge, ALU.mult)\
                    .then_inc(sem_moved(name), 1)
                wait_moved(dve, name)
                link(dve.tensor_reduce(best[:, r + 1, 0:1], best[:, r, :], AX.X, ALU.max))
                if r + 1 < ROUNDS:
                    link(dve.tensor_tensor(cand[:, r + 1, :], steps[:, r + 1, :],
                                           best[:, r + 1, 0:1].bitcast(I32).to_broadcast([P, 3]), ALU.bitwise_or))
            dve.tensor_scalar(rt[:], ident[:, 0:E], best[:, ROUNDS, 0:1], None, ALU.mult).then_inc(rt_made, 1)
            wait_filled(dve, "thr")
            dve.tensor_copy(thr[:], bank[3][:, 0:E]).then_inc(moved[3], 1)
            wait_moved(dve, "thr")
            probs = S2[:].rearrange("p t e -> p e t")
            limit = thr[:].unsqueeze(2).to_broadcast([P, E, NT])
            flat = lambda t: t[:].rearrange("p e t -> p (e t)")
            link(dve.tensor_tensor(gt[:], probs, limit, ALU.is_gt))
            link(dve.tensor_tensor(ge[:], probs, limit, ALU.is_ge))
            link(dve.tensor_tensor(eq[:], ge[:], gt[:], ALU.subtract))
            link(dve.tensor_tensor_scan(flat(cig), flat(reset_g), flat(gt), 0.0, ALU.mult, ALU.add))
            link(dve.tensor_tensor_scan(flat(cie), flat(reset_e), flat(eq), 0.0, ALU.mult, ALU.add))
            link(dve.tensor_tensor(cxg[:], cig[:], gt[:], ALU.subtract))
            dve.tensor_tensor(flat(cxe), flat(cie), flat(eq), ALU.subtract).then_inc(prefix_in, 1)
            dve.tensor_scalar(sl[2][:], ge[:], -4096.0, 4096.0, ALU.mult, ALU.add)
            wait_filled(dve, "pg")
            dve.tensor_tensor(flat(sl[0]), bank[4][:, 0:P], flat(gt), ALU.mult).then_inc(moved[4], 1)
            wait_filled(dve, "pe")
            dve.tensor_tensor(flat(sl[1]), bank[5][:, 0:P], flat(eq), ALU.mult).then_inc(moved[5], 1)
            wait_moved(dve, "pe")
            link(dve.tensor_tensor(sl[3][:], sl[0][:], sl[1][:], ALU.add))
            link(dve.tensor_tensor(sl_i[:, 0], sl[3][:], sl[2][:], ALU.add))
            dve.tensor_scalar(sl_i[:, 1], sl_i[:, 0], 4, None, ALU.logical_shift_right)
            link(dve.tensor_scalar(sl_i[:, 2], sl_i[:, 0], 15, None, ALU.bitwise_and))
            dve.tensor_copy(sl_f[:], sl_i[:, 1:3]).then_inc(slots_made, 1)
            dve.wait_ge(slots_made, 1)
            digit = col_f[:, 0:16].unsqueeze(1).unsqueeze(1)

            def by_tile(k):
                return sl_f[:, k].rearrange("p e t -> p t e").unsqueeze(3).to_broadcast([P, NT, E, 16])

            link(dve.tensor_tensor(OHL[:], by_tile(1), digit.to_broadcast([P, NT, E, 16]), ALU.is_equal))
            link(dve.tensor_tensor(OHH[:], by_tile(0), digit.to_broadcast([P, NT, E, 16]), ALU.is_equal))
            dve.tensor_tensor(OHI[:].rearrange("p t e s -> p t (e s)"), OHL[:].rearrange("p t e s -> p t (e s)"),
                              tok_f[:].unsqueeze(2).to_broadcast([P, NT, E * 16]), ALU.mult).then_inc(onehot_made, 1)
            wait_filled(dve, "ids")
            dve.tensor_tensor(ym[:], bank[6][:, 0:P].rearrange("p (e s) -> p e s", e=E),
                              mask_hi3[:].unsqueeze(2).to_broadcast([P, E, 16]), ALU.mult).then_inc(moved[6], 1)
            wait_moved(dve, "ids")
            link(dve.tensor_reduce(lk[:], ym[:].rearrange("p e s -> p s e"), AX.X, ALU.add))
            dve.tensor_tensor(lh[:], lk[:].unsqueeze(1).to_broadcast([P, 8, 16]),
                              mask_lo3[:].unsqueeze(2).to_broadcast([P, 8, 16]), ALU.mult).then_inc(lh_made, 1)
            wait_filled(dve, "idx")
            dve.tensor_copy(idx[:], bank[7][:, 0:16]).then_inc(idx_made, 1)

            def experts_out(e):
                for h in range(2):
                    s = 2 * e + h
                    wait_filled(dve, ("dn", e, h))
                    if e >= 2:
                        dve.wait_ge(scattered[e - 2], 32)
                    dve.tensor_scalar(OUT[:, s % 4, :], bank[3 + h][:, 0:D], XG[:, s, D + e:D + e + 1], None,
                                      ALU.mult).then_inc(moved[3 + h], 1)

            for g in range(NG):
                for c in range(KC):
                    dve.wait_ge(fth_made, KC * g + c + 1)
                    dve.tensor_tensor(FTL[:, g % 2, c], bank[5 + c][:], FTH[:, g % 2, c].bitcast(F32), ALU.subtract)\
                        .then_inc(moved[5 + c], 1)
                for f in range(FC):
                    w, q = FW[f], g * FC + f
                    if g >= 2 and f == 0:
                        wait_filled(dve, ("dn", GS * (g - 2) + 1, 1))
                    wait_moved(dve, ("up", g, f))
                    dve.tensor_copy(MH[0:w, g % 2, f], MF[0:w, q % 3]).then_inc(mh_made, 1)
                    dve.wait_ge(mh_made, q + 1)
                    dve.tensor_tensor(ML[0:w, g % 2, f], MF[0:w, q % 3], MH[0:w, g % 2, f].bitcast(F32),
                                      ALU.subtract).then_inc(ml_made, 1)
                    if f == 1 and 2 <= g + 1 < NG:
                        dve.wait_ge(wu_hi, g + 2)
                        dve.tensor_tensor(WUL[:, (g + 1) % 2], WUR[:, (g + 1) % 2], WUH[:, (g + 1) % 2].bitcast(F32),
                                          ALU.subtract).then_inc(wu_lo_dve, 1)
                if g:
                    experts_out(GS * (g - 1))
                    experts_out(GS * (g - 1) + 1)
            experts_out(E - 2)
            experts_out(E - 1)
            for q in range(5):
                if q < 4:
                    dve.wait_ge(y_in[q], 16)
                    for t in range(4 * q, 4 * q + 4):
                        last = dve.bn_stats(bn6[:, 2 * NT + t, :], Y[:, t, :])
                    link(last)
                    for t in range(4 * q, 4 * q + 4):
                        last = dve.bn_aggr(mean_var[:, 2 * NT + t, :], bn6[:, 2 * NT + t, :])
                    link(last)
                    k = 2 * NT + 4 * q
                    dve.tensor_scalar(var_eps[:, k:k + 4].unsqueeze(2), mean_var[:, k:k + 4, 1:2], EPS, None, ALU.add)\
                        .then_inc(ln_var, 1)
                if q:
                    for t in range(4 * q - 4, 4 * q):
                        normalise(3, t)


_INPUTS = ["x", "ctx_1024", "L0_attn_W_in", "L0_attn_b_in", "L0_attn_W_gate", "L0_attn_b_gate", "L0_attn_W_out",
           "L0_attn_b_out", "L0_attn_A", "L0_attn_Bm", "L0_attn_C", "L0_attn_D", "L0_xattn_Wq", "L0_xattn_bq",
           "L0_xattn_Wk", "L0_xattn_bk", "L0_xattn_Wv", "L0_xattn_bv", "L0_xattn_Wo", "L0_xattn_bo", "L0_ffn_Wr",
           "L0_ffn_br", "L0_ffn_W_up", "L0_ffn_b_up", "L0_ffn_W_down", "L0_ffn_b_down"]


def kernel(**inputs):
    import numpy as np
    from concourse import bacc
    from concourse.bass_utils import run_bass_kernel_spmd

    nc = bacc.Bacc("TRN2", target_bir_lowering=False, num_devices=1)
    arrays, args = {}, []
    for name in _INPUTS:
        a = np.ascontiguousarray(inputs[name])
        arrays[f"in_{name}"] = a
        args.append(nc.dram_tensor(f"in_{name}", a.shape, mybir.dt.from_np(a.dtype), kind="ExternalInput").ap())
    out = nc.dram_tensor("out", arrays["in_x"].shape, mybir.dt.float32, kind="ExternalOutput").ap()
    decoder_block(nc, *args, out)
    return run_bass_kernel_spmd(nc, [arrays], core_ids=[0]).results[0]["out"]
```

```python
from contextlib import ExitStack

import concourse.bass as bass
from concourse import mybir


def decoder_block(
    nc, x, ctx, w_in, b_in, w_gate, b_gate, w_out, b_out, a_mat, b_mat, c_mat, d_mat,
    wq, bq, wk, bk, wv, bv, wo, bo, wr, br, w_up, b_up, w_down, b_down, out,
):
    F32, F32R, BF16 = mybir.dt.float32, mybir.dt.float32r, mybir.dt.bfloat16
    I32, U32 = mybir.dt.int32, mybir.dt.uint32
    ALU, ACT, AX = mybir.AluOpType, mybir.ActivationFunctionType, mybir.AxisListType

    B, T, D = x.shape
    P = 128
    KC = D // P
    TOK = B * T
    L = 16
    CH = T // L
    NT = TOK // P
    NB = 4
    BLK = TOK // NB
    TPB = BLK // P
    NS = w_in.shape[1]
    SE = ctx.shape[1]
    DK = 16
    HD = D // DK
    PR = HD // 2
    E = wr.shape[1]
    TOP = TOK // E
    NG = w_up.shape[0]
    GS = E // NG
    F = w_up.shape[2]
    FC = -(-F // P)
    FW = [min(P, F - f * P) for f in range(FC)]
    RW = D + E
    EPS = 1e-5
    SCALE = DK ** -0.5
    ROUNDS = 15
    KQ = 3 * 32
    LAG = {"z1": -5, "mx": 2, "nmt": 6, "sc": 7, "pv": 11, "att": 12, "z2": 13, "x2t": 15, "lg": 16}
    UNITS = range(LAG["z1"], NT + LAG["lg"])
    LEVELS = [1 << k for k in range(6)]

    es = ExitStack()
    with es:
        def dram(name, shape):
            return nc.dram_tensor(name, shape, F32, kind="Internal").ap()

        routed = dram("routed_rows", (TOK, RW))
        summed = dram("summed_rows", (TOK, D))

        top = [16512]

        def place(name, shape, dt, at=None):
            size = 2 if dt is BF16 else 4
            for s in shape[1:]:
                size *= s
            size = -(-size // 32) * 32
            if at is None:
                at = top[0]
                top[0] += size
            assert at + size <= 229344, (name, at + size)
            t = nc.alloc_sbuf_tensor_at(name, shape, dt, offset=at)
            offset_of[name] = at
            end_of[name] = at + size
            return t

        offset_of, end_of = {}, {}

        ident = place("ident", [P, P], F32)
        ones_f = place("ones_f", [P, P], F32)
        ones_r = place("ones_r", [P, P], F32R)
        ones_b = place("ones_b", [P, P], BF16)
        ident_b = place("ident_b", [P, P], BF16)
        same_expert = place("same_expert", [P, P], BF16)
        before_b = place("before_b", [P, P], BF16)
        chunk_before_b = place("chunk_before_b", [P, P], BF16)
        even_to_odd_b = place("even_to_odd_b", [P, P], BF16)
        own_odd_to_even_b = place("own_odd_to_even_b", [P, P], BF16)
        pidx = place("pidx", [P, 1], I32)
        pbits = place("pbits", [P, 8], I32)
        pf = place("pf", [P, 8], F32)
        col_i = place("col_i", [P, P], I32)
        col_f = place("col_f", [P, P], F32)
        colm_i = place("colm_i", [P, P], I32)
        colm_f = place("colm_f", [P, P], F32)
        col7_f = place("col7_f", [P, P], F32)
        half_mask = place("half_mask", [P, 2], F32)
        mask_hi3 = place("mask_hi3", [P, 8], F32)
        mask_lo3 = place("mask_lo3", [P, 8], F32)
        mask_16 = place("mask_16", [P, 16], F32)
        steps = place("steps", [P, ROUNDS, 3], I32)
        reset_g = place("reset_g", [P, E, NT], BF16)
        reset_e = place("reset_e", [P, E * B, NT // B], BF16)
        tok_i = place("tok_i", [P, NT], I32)
        junk_m = place("junk_m", [P, 1], F32)
        tok_f = place("tok_f", [P, NT], F32)
        b_in_c = place("b_in_c", [P, 1], F32)
        b_gate_c = place("b_gate_c", [P, KC], F32)
        bq_c = place("bq_c", [P, KC], F32)
        bk_c = place("bk_c", [P, KC], F32)
        bk3_c = place("bk3_c", [P, PR], F32)
        bv_row = place("bv_row", [1, D], F32)
        br_all = place("br_all", [P, E], F32)
        b_up_c = place("b_up_c", [P, NG, FC], F32)
        wr_s = place("wr_s", [P, KC, E], F32)
        bn6 = place("bn6", [P, 3 * NT, 6], F32)
        mean_var = place("mean_var", [P, 3 * NT, 2], F32)
        var_eps = place("var_eps", [P, 3 * NT], F32)
        neg_half = place("neg_half", [P, 2], F32)
        rstd = place("rstd", [P, 3 * NT], F32)
        shift = place("shift", [P, 3 * NT], F32)
        lgt = place("lgt", [P, NT, E], F32)
        X = place("X", [P, NT, RW], F32)
        PHASE3 = top[0]

        b_out_all = place("b_out_all", [P, D], F32)
        bo_all = place("bo_all", [P, D], F32)
        XH = place("XH", [P, NB, KC, BLK], F32R)
        XL = place("XL", [P, NB, KC, BLK], F32R)
        YH = place("YH", [P, NB, KC, BLK], F32R, offset_of["XH"])
        YL = place("YL", [P, NB, KC, BLK], F32R, offset_of["XL"])
        QH = place("QH", [P, 2, KC, BLK], F32R, offset_of["XH"])
        QL = place("QL", [P, 2, KC, BLK], F32R, offset_of["XL"])
        HU = place("HU", [P, TOK], F32)
        NMT = place("NMT", [P, 2, BLK], F32R, offset_of["HU"])
        X2T = place("X2T", [P, 2, D], F32, end_of["NMT"])
        HUH = place("HUH", [P, TOK], F32R)
        HUL = place("HUL", [P, TOK], F32R)
        PT1 = place("PT1", [P, PR, BLK], F32, offset_of["HUH"])
        G = place("G", [P, NB, KC, BLK], F32)
        X1H = [place(f"X1H{r}", [P, KC, BLK], F32R, offset_of["G"] + 8192 * r) for r in range(2)]
        X1L = [place(f"X1L{r}", [P, KC, BLK], F32R, offset_of["G"] + 8192 * r + 4096) for r in range(2)]
        QS = place("QS", [P, 2, PR, BLK], F32R)
        PT0 = place("PT0", [P, PR, BLK], F32)
        PT = [PT0, PT1]
        WIN = [place(n, [P, KC, P], F32R) for n in ("WINH", "WINL")]
        WG = [place(n, [P, KC, D], F32R) for n in ("WGH", "WGL")]
        WOUT = [place(n, [P, KC, D], F32R) for n in ("WOUTH", "WOUTL")]
        WQ = [place(n, [P, KC, D], F32R) for n in ("WQH", "WQL")]
        WO = [place(n, [P, KC, D], F32R) for n in ("WOH", "WOL")]
        W1 = [place(n, [P, D], F32R) for n in ("W1H", "W1L")]
        KS = place("KS", [P, PR, B, P], F32R)
        KM = place("KM", [P, B, KC, HD // KC, SE], F32R)
        VB = place("VB", [P, B, PR, 2, DK + 1], F32)
        ATT = place("ATT", [P, TPB, D], F32)
        ATH = place("ATH", [P, 2, KC, P], F32R)
        ATL = place("ATL", [P, 2, KC, P], F32R)
        PW = place("PW", [NS, L + 1, NS], F32, offset_of["ATT"])
        PB = place("PB", [NS, 5, NS], F32, end_of["PW"])
        TW = place("TW", [NS, 9, NS], F32)
        HS = place("HS", [NS, B, CH + 1], F32)
        NMF = place("NMF", [P, TPB, HD], F32)
        NMS = place("NMS", [P, 2, TPB, PR, 2, 2], F32R)
        REC = place("REC", [P, 2, HD], F32)
        SEL = place("SEL", [32, PR, P], F32R)
        stage = [offset_of["QS"]]

        def staged(name, shape, dt=F32):
            t = place(name, shape, dt, stage[0])
            stage[0] = end_of[name]
            assert stage[0] <= end_of["PT0"]
            return t

        win_s = staged("win_s", [P, KC, P])
        wg_s = staged("wg_s", [P, KC, D])
        wout_s = staged("wout_s", [P, KC, D])
        wq_s = staged("wq_s", [P, KC, D])
        wo_s = staged("wo_s", [P, KC, D])
        wk_s = staged("wk_s", [P, KC, D])
        wv_s = staged("wv_s", [P, KC, D])
        wk3_s = staged("wk3_s", [P, KC * PR, 3, 32])
        ab_s = staged("ab_s", [P, NS])
        mx_s = staged("mx_s", [P, P])
        cd_s = staged("cd_s", [P, KC, P])
        cdt_s = staged("cdt_s", [P, D])
        ctx_s = staged("ctx_s", [P, D])
        ctd_s = staged("ctd_s", [P, KC, B, 2, SE])
        kt_s = staged("kt_s", [P, KC, B * SE])
        ksf_s = staged("ksf_s", [P, PR, B, 2, SE])
        sel_s = staged("sel_s", [32, PR, 2, SE])

        top[0] = PHASE3
        idx = place("idx", [P, NT], I32)
        XG = place("XG", [P, NT, RW], F32)
        FTH = place("FTH", [P, 2, KC, GS * TOP], F32R, offset_of["X"])
        FTL = place("FTL", [P, 2, KC, GS * TOP], F32R, end_of["FTH"])
        MF = place("MF", [P, 3, GS * TOP], F32)
        MH = place("MH", [P, 2, FC, GS * TOP], F32R)
        ML = place("ML", [P, 2, FC, GS * TOP], F32R)
        OHH = place("OHH", [P, NT, E, 16], F32R, offset_of["MH"])
        OHL = place("OHL", [P, NT, E, 16], F32, offset_of["MH"] + 8192)
        OHI = place("OHI", [P, NT, E, 16], F32R, offset_of["MH"] + 16384)
        WUR = place("WUR", [P, 2, KC, F], F32)
        WUH = place("WUH", [P, 2, KC, F], F32R)
        WUL = place("WUL", [P, 2, KC, F], F32R)
        WDR = place("WDR", [P, 2, FC, D], F32)
        WDH = place("WDH", [P, 3, FC, D], F32R)
        WDL = place("WDL", [P, 3, FC, D], F32R)
        BDR = place("BDR", [1, 2, D], F32)
        BDH = place("BDH", [1, 3, D], F32R)
        BDL = place("BDL", [1, 3, D], F32R)
        OUT = place("OUT", [P, 4, D], F32)
        Y = place("Y", [P, NT, D], F32, offset_of["MH"])

        top[0] = offset_of["ML"]
        S2 = place("S2", [P, NT, E], F32)
        mxl = place("mxl", [P, NT], F32)
        lm = place("lm", [P, NT, E], F32)
        ex = place("ex", [P, NT, E], F32)
        sm = place("sm", [P, NT], F32)
        rcp = place("rcp", [P, NT], F32)
        ST = place("ST", [P, P], F32)
        junk = place("junk", [P, 3, P], BF16)
        cand = place("cand", [P, ROUNDS, 3], I32)
        cnt = place("cnt", [P, ROUNDS, 3], BF16)
        best = place("best", [P, ROUNDS + 1, 4], F32)
        rt = place("rt", [P, E], F32)
        thr = place("thr", [P, E], F32)
        gt = place("gt", [P, E, NT], BF16)
        ge = place("ge", [P, E, NT], BF16)
        eq = place("eq", [P, E, NT], BF16)
        cig = place("cig", [P, E, NT], BF16)
        cie = place("cie", [P, E * B, NT // B], BF16)
        cxg = place("cxg", [P, E, NT], BF16)
        cxe = place("cxe", [P, E, NT], BF16)
        sl = [place(f"sl{k}", [P, E, NT], F32) for k in range(5)]
        sl_i = place("sl_i", [P, 3, E, NT], I32)
        sl_f = place("sl_f", [P, 2, E, NT], F32)
        ym = place("ym", [P, E, 16], F32)
        lk = place("lk", [P, 16], F32)
        lh = place("lh", [P, 8, 16], F32)
        assert top[0] <= end_of["ML"]

        bank = [es.enter_context(nc.psum_tensor(f"bank{k}", [P, 512], F32)) for k in range(8)]

        def sem(name):
            return es.enter_context(nc.semaphore(name))

        filled = [sem(f"filled{k}") for k in range(8)]
        moved = [sem(f"moved{k}") for k in range(8)]

        def live(g, stage):
            return 0 <= g - LAG[stage] < NT

        def block_of(g, stage):
            t = g - LAG.get(stage, 0)
            return t // TPB if 0 <= t < NT and t % TPB == 0 else None

        norm_order = []
        for g in UNITS:
            for which, stage in ((1, "z1"), (2, "z2")):
                if live(g, stage):
                    norm_order.append((which, g - LAG[stage]))
        norm_order += [(3, t) for t in range(NT)]
        norm_at = {what: k for k, what in enumerate(norm_order)}

        turn_of, uses = {}, [0] * 8

        def product(name, k):
            turn_of[name] = (k, uses[k])
            uses[k] += 1

        POWERS = [1 << k for k in range(9)]
        product("ab", 6)
        for n in range(NB):
            for c in range(KC):
                product(("xt", n, c), c)
            product(("u", n), 2 + n % 2)
            product(("pw", POWERS[n]), 4)
            product(("tw", POWERS[n]), 5)
        product("cd", 0)
        product("ctx", 1)
        product("w1", 7)
        for i in range(L):
            product(("step", i), 6 + i % 2)
            if i % 2 == 0:
                product(("gate", i // 2), 2 + (i // 2) % 2)
            if i % 2 == 1 and 4 + i // 2 < 9:
                product(("pw", POWERS[4 + i // 2]), 4)
                if POWERS[4 + i // 2] < 256:
                    product(("tw", POWERS[4 + i // 2]), 5)
        KSP = [(0, 1, 2), (3, 4), (5, 6), (7,), (), ()]
        for k in range(6):
            product(("carry", k), 6 + k % 2)
            if k < 2:
                product(("kt", k), k)
                product(("v", k), 4 + k)
            for j in KSP[k]:
                product(("ks", j), 2 + j % 2)
        for q in range(4):
            product(("cor", q), 6 + q % 2)
        for n in range(NB):
            for c in range(KC):
                product(("y", n, c), 2 + c)

        for g in UNITS:
            n = block_of(g, "x1t")
            if n is not None:
                for c in range(KC):
                    product(("x1t", n, c), c)
            if live(g, "z1"):
                product(("z1", g - LAG["z1"]), 6)
            for half in range(2):
                if live(g, "sc"):
                    t = g - LAG["sc"]
                    product(("sc", t // TPB, 2 * (t % TPB) + half), 4 + half)
                if half == 0 and live(g, "lg"):
                    product(("lg", g - LAG["lg"]), 1)
                if live(g, "mx"):
                    product(("mx", g - LAG["mx"], half), 2 + half)
                if half == 0 and block_of(g, "nmt") is not None:
                    product(("nmt", block_of(g, "nmt")), 0)
                if half == 0 and live(g, "pv"):
                    product(("pv", g - LAG["pv"]), 7)
            for c in range(KC):
                if block_of(g - c, "q") is not None:
                    product(("q", block_of(g - c, "q"), c), 2 + c)
            if live(g, "att"):
                product(("att", g - LAG["att"]), 0)
            if live(g, "z2"):
                product(("z2", g - LAG["z2"]), 6)
            if live(g, "x2t"):
                product(("x2t", g - LAG["x2t"]), 1)
        product("st", 0)
        for r in range(ROUNDS):
            product(("tot", r), 1 + r % 2)
        product("thr", 3)
        product("pg", 4)
        product("pe", 5)
        product("ids", 6)
        product("idx", 7)
        for g in range(NG + 1):
            if g < NG:
                for c in range(KC):
                    product(("gt", g, c), 5 + c)
                for f in range(FC):
                    product(("up", g, f), f % 3)
            if g > 0:
                for e in range(GS * (g - 1), GS * g):
                    for h in range(2):
                        product(("dn", e, h), 3 + h)

        def bank_of(name):
            return bank[turn_of[name][0]]

        def wait_filled(eng, name):
            k, u = turn_of[name]
            eng.wait_ge(filled[k], u + 1)

        def wait_moved(eng, name):
            k, u = turn_of[name]
            eng.wait_ge(moved[k], u + 1)

        def wait_up_low(eng, g):
            eng.wait_ge(wu_lo_pool, min(g + 1, 2))
            if g >= 2:
                eng.wait_ge(wu_lo_dve, g - 1)

        def phase2_over(eng):
            wait_moved(eng, ("lg", NT - 1))

        def sem_filled(name):
            return filled[turn_of[name][0]]

        def sem_moved(name):
            return moved[turn_of[name][0]]

        x_in = [sem(f"x_in{n}") for n in range(NB)]
        ab_in, cd_in, win_in, wg_in, wout_in, wq_in, wo_in = [
            sem(n) for n in ("ab_in", "cd_in", "win_in", "wg_in", "wout_in", "wq_in", "wo_in")]
        b_in_in = sem("b_in_in")
        kv_in, bias1_in, bias2_in = sem("kv_in"), sem("bias1_in"), sem("bias2_in")
        ident_made, pool_consts = sem("ident_made"), sem("pool_consts")
        head_masks, masks_made = sem("head_masks"), sem("masks_made")
        win_zero, mx_made, starts_zero = sem("win_zero"), sem("mx_made"), sem("starts_zero")
        w_hi, w_lo = sem("w_hi"), sem("w_lo")
        xh_made, u_made, xb_added = sem("xh_made"), sem("u_made"), sem("xb_added")
        tw1_made = sem("tw1_made")
        h_start = sem("h_start")
        hu_hi, hu_lo = sem("hu_hi"), sem("hu_lo")
        km_made = sem("km_made")
        wk3_made, ks_hi, ks_made, vb_made, vb_init = [
            sem(n) for n in ("wk3_made", "ks_hi", "ks_made", "vb_made", "vb_init")]
        y_hi, y_lo_dve, y_lo_pool = sem("y_hi"), sem("y_lo_dve"), sem("y_lo_pool")
        ln_stats, ln_var, ln_pool, ln_scale = sem("ln_stats"), sem("ln_var"), sem("ln_pool"), sem("ln_scale")
        ln1_out, ln2_out, ln3_out = sem("ln1_out"), sem("ln2_out"), sem("ln3_out")
        x1h_made, q_hi, qs_in = sem("x1h_made"), sem("q_hi"), [sem("qs_in0"), sem("qs_in1")]
        bo_added = sem("bo_added")
        rec_made = sem("rec_made")
        nm_hi, nm_made = sem("nm_hi"), sem("nm_made")
        ath_made = sem("ath_made")
        lm_made, ex_made, s2_made, routed_made = [
            sem(n) for n in ("lm_made", "ex_made", "s2_made", "routed_made")]
        routed_out, summed_out = sem("routed_out"), sem("summed_out")
        cnt_made, rt_made, prefix_in, slots_made, onehot_made, lh_made, idx_made = [
            sem(n) for n in ("cnt_made", "rt_made", "prefix_in", "slots_made",
                             "onehot_made", "lh_made", "idx_made")]
        gathered = [sem(f"gathered{e}") for e in range(E)]
        scattered = [sem(f"scattered{e}") for e in range(E)]
        wu_in, wd_in = [sem("wu_in0"), sem("wu_in1")], [sem("wd_in0"), sem("wd_in1")]
        wu_hi, wu_lo_pool, wu_lo_dve = sem("wu_hi"), sem("wu_lo_pool"), sem("wu_lo_dve")
        wd_hi, wd_lo = sem("wd_hi"), sem("wd_lo")
        fth_made = sem("fth_made")
        mh_made, ml_made = sem("mh_made"), sem("ml_made")
        y_in = [sem(f"y_in{q}") for q in range(NT // 2)]
        y_out = sem("y_out")
        dve_step, act_step, pool_step = sem("dve_step"), sem("act_step"), sem("pool_step")

        def chain(eng, s):
            count = [0]

            def link(ins):
                count[0] += 1
                ins.then_inc(s, 1)
                eng.wait_ge(s, count[0])

            return link

        block = es.enter_context(nc.Block())

        def by_tiles(ap):
            return ap.rearrange("(b c j i) d -> i c b j d", b=B, c=CH, i=2)

        @block.sync
        def _(sp):
            sp.dma_start(ab_s[0:NS, :], a_mat).then_inc(ab_in, 16)
            sp.dma_start(ab_s[NS:P, :], b_mat).then_inc(ab_in, 16)
            xr = by_tiles(x.rearrange("b t d -> (b t) d"))
            for n in range(NB):
                b, j0 = n // 2, (n % 2) * TPB
                for i in range(2):
                    sp.dma_start(X[CH * i:CH * (i + 1), TPB * n:TPB * (n + 1), 0:D],
                                 xr[i, :, b, j0:j0 + TPB, :]).then_inc(x_in[n], 16)
                if n == 0:
                    sp.dma_start(PW[:, 1, :], a_mat).then_inc(ab_in, 16)
            sp.dma_start(cd_s[:, :, 0:NS], c_mat.rearrange("(c p) n -> p c n", p=P)).then_inc(cd_in, 16)
            sp.dma_start(cd_s[:, :, NS:P], d_mat.rearrange("(c p) n -> p c n", p=P)).then_inc(cd_in, 16)
            sp.dma_start(wg_s[:], w_gate.rearrange("(c p) n -> p c n", p=P)).then_inc(wg_in, 16)
            with nc.allow_non_contiguous_dma(reason="short bias columns"):
                sp.dma_start(b_gate_c[:], b_gate.rearrange("(c p) -> p c", p=P)).then_inc(bias1_in, 16)
                sp.dma_start(b_out_all[:], b_out.rearrange("(a n) -> a n", a=1).to_broadcast([P, D]))\
                    .then_inc(bias1_in, 16)
                sp.dma_start(bq_c[:], bq.rearrange("(c p) -> p c", p=P)).then_inc(bias1_in, 16)
                sp.dma_start(ctx_s[:], ctx.rearrange("b s d -> (b s) d")).then_inc(kv_in, 16)
                sp.dma_start(wk_s[:], wk.rearrange("(c p) n -> p c n", p=P)).then_inc(kv_in, 16)
                sp.dma_start(wv_s[:], wv.rearrange("(c p) n -> p c n", p=P)).then_inc(kv_in, 16)
                sp.dma_start(bk_c[:], bk.rearrange("(c p) -> p c", p=P)).then_inc(kv_in, 16)
                for k in range(3):
                    sp.dma_start(bk3_c[32 * k:32 * k + 32, :], bk.rearrange("(j p) -> p j", p=32))\
                        .then_inc(kv_in, 16)
                sp.dma_start(bv_row[:], bv.rearrange("(a n) -> a n", a=1)).then_inc(kv_in, 16)
            sp.dma_start(wout_s[:], w_out.rearrange("(c p) n -> p c n", p=P)).then_inc(wout_in, 16)
            sp.dma_start(wq_s[:], wq.rearrange("(c p) n -> p c n", p=P)).then_inc(wq_in, 16)
            sp.dma_start(wo_s[:], wo.rearrange("(c p) n -> p c n", p=P)).then_inc(wo_in, 16)
            with nc.allow_non_contiguous_dma(reason="short bias columns"):
                sp.dma_start(bo_all[:], bo.rearrange("(a n) -> a n", a=1).to_broadcast([P, D]))\
                    .then_inc(bias2_in, 16)
                sp.dma_start(br_all[:], br.rearrange("(a n) -> a n", a=1).to_broadcast([P, E]))\
                    .then_inc(bias2_in, 16)
                sp.dma_start(wr_s[:], wr.rearrange("(c p) n -> p c n", p=P)).then_inc(bias2_in, 16)
                full = (FC - 1) * P
                for g in range(NG):
                    sp.dma_start(b_up_c[:, g, 0:FC - 1], b_up[g, 0:full].rearrange("(c p) -> p c", p=P))\
                        .then_inc(bias2_in, 16)
                sp.dma_start(b_up_c[0:FW[-1], :, FC - 1], b_up[:, full:F].rearrange("g p -> p g"))\
                    .then_inc(bias2_in, 16)
            for n in range(NB):
                r = n % 2
                wait_moved(sp, ("q", n, 0))
                wait_moved(sp, ("q", n, 1))
                if n >= 2:
                    wait_filled(sp, ("sc", n - 2, PR - 1))
                else:
                    sp.wait_ge(ks_made, 2)
                    sp.wait_ge(km_made, 4)
                    sp.wait_ge(w_lo, 5)
                for q in range(PR // KC):
                    for k, src in enumerate((QH, QH, QL)):
                        sp.dma_start(QS[32 * k:32 * k + 32, r].rearrange("p (c q) n -> p c q n", c=KC)[:, :, q, :].bitcast(F32),
                                     src[32 * q:32 * q + 32, r].bitcast(F32)).then_inc(qs_in[r], 16)
            phase2_over(sp)

            def load_up(g):
                if g >= 2:
                    sp.wait_ge(wu_hi, g - 1)
                    wait_up_low(sp, g - 2)
                sp.dma_start(WUR[:, g % 2], w_up[g].rearrange("(c p) f -> p c f", p=P))\
                    .then_inc(wu_in[g % 2], 16)

            def load_down(e):
                if e >= 2:
                    sp.wait_ge(wd_hi, e - 1)
                    sp.wait_ge(wd_lo, e - 1)
                full = (FC - 1) * P
                sp.dma_start(WDR[:, e % 2, 0:FC - 1, :],
                             w_down[e, 0:full, :].rearrange("(c p) n -> p c n", p=P))\
                    .then_inc(wd_in[e % 2], 16)
                sp.dma_start(WDR[0:FW[-1], e % 2, FC - 1, :], w_down[e, full:F, :])\
                    .then_inc(wd_in[e % 2], 16)
                sp.dma_start(BDR[:, e % 2, :], b_down[e:e + 1, :]).then_inc(wd_in[e % 2], 16)

            load_up(0)
            load_down(0)
            load_down(1)
            load_up(1)
            for i in range(2):
                for b in range(B):
                    sp.dma_start(by_tiles(summed)[i, :, b],
                                 X[CH * i:CH * (i + 1), NT // B * b:NT // B * (b + 1), 0:D])\
                        .then_inc(summed_out, 16)
            sp.wait_ge(routed_made, 1)
            for i in range(2):
                for b in range(B):
                    sp.dma_start(by_tiles(routed)[i, :, b],
                                 X[CH * i:CH * (i + 1), NT // B * b:NT // B * (b + 1), :])\
                        .then_inc(routed_out, 16)
            load_down(2)
            for g in range(2, NG):
                load_up(g)
                load_down(2 * g - 1)
                load_down(2 * g)
            load_down(E - 1)
            for e in range(E):
                sp.wait_ge(scattered[e], 32)
            ys = summed.rearrange("(p i) d -> p i d", p=P)
            for q in range(NT // 2):
                sp.dma_start(Y[:, 2 * q:2 * q + 2, :], ys[:, 2 * q:2 * q + 2, :]).then_inc(y_in[q], 16)
            os_ = out.rearrange("b t d -> (b t) d").rearrange("(p i) d -> p i d", p=P)
            for q in range(NT // 2):
                sp.wait_ge(ln3_out, 2 * (q + 1))
                sp.dma_start(os_[:, 2 * q:2 * q + 2, :], Y[:, 2 * q:2 * q + 2, :]).then_inc(y_out, 16)
            sp.wait_ge(y_out, 8 * NT)
            sp.wait_ge(summed_out, 64)
            sp.wait_ge(routed_out, 64)

        @block.gpsimd
        def _(pool):
            link = chain(pool, pool_step)
            link(pool.memset(ident[:], 0.0))
            pool.affine_select(out=ident[:], in_=ident[:], compare_op=ALU.not_equal, fill=1.0,
                               base=0, pattern=[[-1, P]], channel_multiplier=1).then_inc(ident_made, 1)
            pool.memset(win_s[:, :, 0:NS], 0.0).then_inc(win_zero, 1)
            pool.wait_ge(win_zero, 1)
            link(pool.memset(mx_s[NS:P, 0:NS], 0.0))
            pool.wait_ge(ident_made, 1)
            pool.tensor_copy(mx_s[NS:P, NS:P], ident[NS:P, NS:P]).then_inc(mx_made, 1)
            pool.wait_ge(mx_made, 1)
            link(pool.memset(HU[0:NS, :].rearrange("p (b i c) -> p b i c", b=B, i=L)[:, :, 0, :], 0.0))
            pool.memset(HS[:, :, 0:1], 0.0).then_inc(starts_zero, 1)
            pool.wait_ge(starts_zero, 1)
            link(pool.memset(neg_half[:], -0.5))
            link(pool.iota(pidx[:], pattern=[[0, 1]], base=0, channel_multiplier=1))
            link(pool.iota(col_i[:], pattern=[[1, P]], base=0, channel_multiplier=0))
            link(pool.iota(tok_i[:], pattern=[[T, B], [2, NT // B]], base=0, channel_multiplier=0))
            for j in range(3):
                link(pool.memset(steps[:, 0, j:j + 1], (j + 1) << 28))
            link(pool.memset(reset_g[:], 1.0))
            link(pool.memset(reset_g[:, :, 0:1], 0.0))
            link(pool.memset(reset_e[:], 1.0))
            link(pool.memset(reset_e[:, :, 0:1], 0.0))
            link(pool.memset(ones_b[:], 1.0))
            link(pool.memset(ones_r[:].bitcast(F32), 1.0))
            pool.memset(ones_f[:], 1.0).then_inc(pool_consts, 1)
            pool.wait_ge(pool_consts, 1)
            pool.memset(VB[:], 0.0).then_inc(vb_init, 1)
            pool.wait_ge(vb_init, 1)
            link(pool.memset(VB[0:SE, :, :, 0, DK:DK + 1], 1.0))
            pool.memset(VB[SE:P, :, :, 1, DK:DK + 1], 1.0).then_inc(vb_init, 1)
            pool.wait_ge(vb_init, 2)
            pool.wait_ge(bias1_in, 16 * 3)
            for n in range(NB):
                wait_filled(pool, ("xt", n, KC - 1))
                xs = X[:, TPB * n:TPB * (n + 1), 0:D]
                pool.tensor_tensor(xs, xs, b_out_all[:].unsqueeze(1).to_broadcast([P, TPB, D]), ALU.add)\
                    .then_inc(xb_added, 1)
            link(pool.memset(sel_s[:], 0.0))
            for base in (0, -2):
                link(pool.affine_select(out=sel_s[:], in_=sel_s[:], compare_op=ALU.not_equal, fill=1.0, base=base,
                                        pattern=[[-4, PR], [-1, 2], [0, SE]], channel_multiplier=1))
            pool.tensor_copy(SEL[:], sel_s[:].rearrange("p j h k -> p j (h k)")).then_inc(ks_made, 1)
            pool.wait_ge(ks_made, 1)
            pool.wait_ge(head_masks, 1)
            for c in range(KC):
                wait_moved(pool, ("kt", c))
                for b in range(B):
                    pool.tensor_tensor(
                        KM[:, b, c], kt_s[:, c, b * SE:(b + 1) * SE].unsqueeze(1).to_broadcast([P, HD // KC, SE]),
                        mask_hi3[:].unsqueeze(2).to_broadcast([P, HD // KC, SE]), ALU.mult).then_inc(km_made, 1)
            pool.wait_ge(ks_hi, 1)
            pool.wait_ge(km_made, 4)
            pool.tensor_tensor(KS[32:64], ksf_s[32:64].rearrange("p j b h k -> p j b (h k)"),
                               KS[32:64].bitcast(F32), ALU.subtract).then_inc(ks_made, 1)
            pool.wait_ge(ks_made, 2)
            for n in range(2, NB):
                for c in range(KC):
                    pool.wait_ge(y_hi, KC * n + c + 1)
                    pool.tensor_tensor(YL[:, n, c], G[:, n, c], YH[:, n, c].bitcast(F32), ALU.subtract)\
                        .then_inc(y_lo_pool, 1)

            scaled = [0]

            def scale(k, width=1, shifted=True):
                at = slice(k, k + width)
                pool.wait_ge(ln_var, k + width)
                link(pool.tensor_scalar(var_eps[:, at].unsqueeze(2), mean_var[:, at, 1:2], EPS, None, ALU.add))
                pool.tensor_tensor(rstd[:, at], var_eps[:, at], neg_half[:, 0:width], ALU.pow).then_inc(ln_pool, 1)
                scaled[0] += 1
                pool.wait_ge(ln_pool, scaled[0])
                if shifted:
                    for j in range(k, k + width):
                        pool.tensor_scalar(shift[:, j:j + 1], mean_var[:, j, 0:1], rstd[:, j:j + 1], -1.0,
                                           ALU.mult, ALU.mult).then_inc(ln_scale, 1)

            for g in UNITS:
                n = block_of(g, "x1t")
                if live(g, "z1"):
                    scale(norm_at[1, g - LAG["z1"]])
                if n is not None:
                    if n == 0:
                        pool.wait_ge(bias2_in, 16 * (4 + NG))
                    wait_filled(pool, ("x1t", n, KC - 1))
                    xs = X[:, TPB * n:TPB * (n + 1), 0:D]
                    pool.tensor_tensor(xs, xs, bo_all[:].unsqueeze(1).to_broadcast([P, TPB, D]), ALU.add)\
                        .then_inc(bo_added, 1)
                if live(g, "z2"):
                    t = g - LAG["z2"]
                    k = norm_at[2, t]
                    scale(k, shifted=False)
                    pool.tensor_scalar(X[:, t, 0:D], X[:, t, 0:D], mean_var[:, k, 0:1], rstd[:, k:k + 1],
                                       ALU.subtract, ALU.mult).then_inc(ln2_out, 1)
            phase2_over(pool)

            def up_low(g):
                pool.wait_ge(wu_hi, g + 1)
                pool.tensor_tensor(WUL[:, g % 2], WUR[:, g % 2], WUH[:, g % 2].bitcast(F32), ALU.subtract)\
                    .then_inc(wu_lo_pool, 1)

            def down_low(e):
                pool.wait_ge(wd_hi, e + 1)
                if e >= 3:
                    wait_filled(pool, ("dn", e - 3, 1))
                pool.tensor_tensor(WDL[:, e % 3, 0:FC - 1], WDR[:, e % 2, 0:FC - 1],
                                   WDH[:, e % 3, 0:FC - 1].bitcast(F32), ALU.subtract)
                f = FW[-1]
                pool.tensor_tensor(WDL[0:f, e % 3, FC - 1], WDR[0:f, e % 2, FC - 1],
                                   WDH[0:f, e % 3, FC - 1].bitcast(F32), ALU.subtract)
                pool.tensor_tensor(BDL[:, e % 3], BDR[:, e % 2], BDH[:, e % 3].bitcast(F32), ALU.subtract)\
                    .then_inc(wd_lo, 1)

            up_low(0)
            down_low(0)
            down_low(1)
            up_low(1)
            pool.wait_ge(idx_made, 1)
            pool.wait_ge(routed_out, 64)
            pool.wait_ge(summed_out, 64)
            for s in range(NT):
                pool.indirect_dma_start(
                    XG[:, s, :], None, routed,
                    bass.IndirectOffsetOnAxis(ap=idx[:, s:s + 1].bitcast(U32), axis=0)).then_inc(gathered[s // 2], 16)
            down_low(2)

            for e in range(E):
                if e:
                    pool.wait_ge(scattered[e - 1], 32)
                for h in range(2):
                    wait_moved(pool, ("dn", e, h))
                    pool.indirect_dma_start(
                        summed, bass.IndirectOffsetOnAxis(ap=idx[:, 2 * e + h:2 * e + h + 1].bitcast(U32), axis=0),
                        OUT[:, (2 * e + h) % 4, :], None, compute_op=ALU.add).then_inc(scattered[e], 16)
                if e + 3 < E:
                    down_low(e + 3)
            for q in range(NT // 2):
                scale(2 * NT + 2 * q, 2)

        @block.scalar
        def _(act):
            link = chain(act, act_step)
            with nc.allow_non_contiguous_dma(reason="short bias columns"):
                act.wait_ge(win_zero, 1)
                act.dma_start(win_s[:, :, NS:P], w_in.rearrange("(c p) n -> p c n", p=P)).then_inc(win_in, 16)
                act.dma_start(b_in_c[NS:P, :], b_in.rearrange("(p a) -> p a", a=1)).then_inc(b_in_in, 16)

            def whole(w, src, arrived):
                act.wait_ge(arrived, 16)
                act.activation(w[0][:], src[:], ACT.Copy).then_inc(w_hi, 1)

            whole(WIN, win_s, win_in)
            for n in range(NB):
                for c in range(KC):
                    wait_filled(act, ("xt", n, c))
                    act.activation(XH[:, n, c], bank[c][:], ACT.Copy).then_inc(xh_made, 1)
                if n == 0:
                    act.wait_ge(b_in_in, 16)
                wait_filled(act, ("u", n))
                act.activation(HU[NS:P, n * BLK:(n + 1) * BLK], bank_of(("u", n))[NS:P, :], ACT.Identity,
                               bias=b_in_c[NS:P, :]).then_inc(sem_moved(("u", n)), 1)
                m = POWERS[n]
                wait_filled(act, ("tw", m))
                act.activation(TW[:, n + 1, :], bank[5][0:NS, 0:NS], ACT.Copy).then_inc(moved[5], 1)
                if n == 1:
                    whole(WG, wg_s, wg_in)
            whole(WOUT, wout_s, wout_in)
            whole(WQ, wq_s, wq_in)
            whole(WO, wo_s, wo_in)
            wait_filled(act, "w1")
            act.activation(W1[0][:], bank[7][:, 0:D], ACT.Copy).then_inc(w_hi, 1)
            for i in range(L):
                if i % 2 == 1 and 4 + i // 2 < 9:
                    m = POWERS[4 + i // 2]
                    if m < 256:
                        wait_filled(act, ("tw", m))
                        act.activation(TW[:, 5 + i // 2, :], bank[5][0:NS, 0:NS], ACT.Copy).then_inc(moved[5], 1)
                if i == 0:
                    act.wait_ge(bias1_in, 16 * 3)
                if i % 2 == 1:
                    g = i // 2
                    n, c = g // 2, g % 2
                    wait_filled(act, ("gate", g))
                    act.activation(G[:, n, c], bank_of(("gate", g))[:], ACT.Sigmoid,
                                   bias=b_gate_c[:, c:c + 1]).then_inc(sem_moved(("gate", g)), 1)
            act.wait_ge(kv_in, 128)
            for c in range(KC):
                wait_filled(act, ("kt", c))
                act.activation(kt_s[:, c], bank[c][:, 0:B * SE], ACT.Identity, bias=bk_c[:, c:c + 1])\
                    .then_inc(moved[c], 1)
            for n in range(NB):
                act.wait_ge(h_start, 1)
                wait_moved(act, ("cor", 1 + 2 * (n % 2)))
                wait_moved(act, ("cor", 2 * (n % 2)))
                act.activation(HUH[:, n * BLK:(n + 1) * BLK], HU[:, n * BLK:(n + 1) * BLK], ACT.Copy)\
                    .then_inc(hu_hi, 1)
            for n in range(NB):
                for c in range(KC):
                    wait_moved(act, ("y", n, c))
                    act.activation(YH[:, n, c], G[:, n, c], ACT.Copy).then_inc(y_hi, 1)
            def normalise(which, t):
                k = norm_at[which, t]
                act.wait_ge(ln_scale, t + 1 if which == 1 else NT + t + 1)
                r = Y[:, t, :] if which == 3 else X[:, t, 0:D]
                act.activation(r, r, ACT.Identity, bias=shift[:, k:k + 1], scale=rstd[:, k:k + 1])\
                    .then_inc(ln1_out if which == 1 else ln3_out, 1)

            def exps(m, j):
                if j == 0 and m == 0:
                    act.wait_ge(ks_made, 2)
                    act.wait_ge(km_made, 4)
                if j == 0 and m >= 2:
                    wait_filled(act, ("pv", TPB * (m - 1) - 1))
                wait_filled(act, ("sc", m, j))
                act.activation(PT[m % 2][:, j, :], bank_of(("sc", m, j))[:], ACT.Exp, scale=SCALE)\
                    .then_inc(sem_moved(("sc", m, j)), 1)

            for g in UNITS:
                n = block_of(g, "x1t")
                if n is not None:
                    r = n % 2
                    for c in range(KC):
                        wait_filled(act, ("x1t", n, c))
                        if n < 2:
                            act.wait_ge(y_hi, 4 * n + 4)
                            act.wait_ge(*((y_lo_dve, 4), (y_lo_pool, 4))[n])
                        else:
                            wait_filled(act, ("q", n - 2, KC - 1))
                        act.activation(X1H[r][:, c], bank[c][:], ACT.Copy).then_inc(x1h_made, 1)
                if live(g - 1, "z1"):
                    normalise(1, g - 1 - LAG["z1"])
                for half in range(2):
                    if live(g, "sc"):
                        t = g - LAG["sc"]
                        exps(t // TPB, 2 * (t % TPB) + half)
                    if half == 0 and block_of(g, "nmt") is not None:
                        n = block_of(g, "nmt")
                        wait_filled(act, ("nmt", n))
                        if n >= 2:
                            wait_filled(act, ("sc", n - 2, PR - 1))
                        act.activation(NMT[0:32, n % 2, :], bank[0][0:32, :], ACT.Copy).then_inc(moved[0], 1)
                for c in range(KC):
                    n = block_of(g - c, "q")
                    if n is not None:
                        wait_filled(act, ("q", n, c))
                        wait_filled(act, ("z1", TPB * (n % 2) + TPB - 1))
                        if n >= 2:
                            wait_filled(act, ("mx", TPB * (n - 1) - 1, KC - 1))
                            act.wait_ge(qs_in[n % 2], 16 * 3 * 4 * (n // 2))
                        act.activation(QH[:, n % 2, c], bank_of(("q", n, c))[:], ACT.Identity,
                                       bias=bq_c[:, c:c + 1]).then_inc(q_hi, 1)
                if live(g, "att"):
                    t = g - LAG["att"]
                    wait_filled(act, ("att", t))
                    if t >= 2:
                        wait_filled(act, ("z2", t - 2))
                    act.activation(ATH[:, t % 2], bank_of(("att", t))[:, 0:D], ACT.Copy).then_inc(ath_made, 1)
                if live(g, "x2t"):
                    t = g - LAG["x2t"]
                    wait_filled(act, ("x2t", t))
                    if t >= 2:
                        wait_filled(act, ("lg", t - 2))
                    act.activation(X2T[:, t % 2, :], bank_of(("x2t", t))[:, 0:D], ACT.Copy)\
                        .then_inc(sem_moved(("x2t", t)), 1)
            act.wait_ge(lm_made, 1)
            act.activation(ex[:], lm[:], ACT.Exp).then_inc(ex_made, 1)
            act.wait_ge(s2_made, 1)
            act.activation(X[:, :, D:RW], S2[:], ACT.Copy).then_inc(routed_made, 1)

            def down_high(e):
                act.wait_ge(wd_in[e % 2], 48 * (e // 2 + 1))
                if e >= 3:
                    wait_filled(act, ("dn", e - 3, 1))
                act.activation(WDH[:, e % 3, 0:FC - 1], WDR[:, e % 2, 0:FC - 1], ACT.Copy)
                f = FW[-1]
                act.activation(WDH[0:f, e % 3, FC - 1], WDR[0:f, e % 2, FC - 1], ACT.Copy)
                act.activation(BDH[:, e % 3], BDR[:, e % 2], ACT.Copy).then_inc(wd_hi, 1)

            def up_high(g):
                act.wait_ge(wu_in[g % 2], 16 * (g // 2 + 1))
                if g >= 2:
                    wait_filled(act, ("up", g - 2, FC - 1))
                act.activation(WUH[:, g % 2], WUR[:, g % 2], ACT.Copy).then_inc(wu_hi, 1)

            up_high(0)
            down_high(0)
            down_high(1)
            up_high(1)
            down_high(2)
            for g in range(NG):
                for c in range(KC):
                    wait_filled(act, ("gt", g, c))
                    if g >= 2:
                        wait_filled(act, ("up", g - 2, FC - 1))
                    act.activation(FTH[:, g % 2, c], bank[5 + c][:], ACT.Copy).then_inc(fth_made, 1)
                if g >= 2:
                    down_high(2 * g)
                for f in range(FC):
                    wait_filled(act, ("up", g, f))
                    q = g * FC + f
                    if q >= 3:
                        act.wait_ge(ml_made, q - 2)
                    act.activation(MF[0:FW[f], q % 3], bank[f % 3][0:FW[f], :], ACT.Silu,
                                   bias=b_up_c[0:FW[f], g, f:f + 1]).then_inc(moved[f % 3], 1)
                    if f == 1 and 2 <= g + 1 < NG:
                        up_high(g + 1)
                if g >= 1:
                    down_high(2 * g + 1)
            for t in range(NT):
                normalise(3, t)

        @block.tensor
        def _(pe):
            order = [0] * 8

            def turn(name):
                k, u = turn_of[name]
                assert order[k] == u, name
                order[k] += 1
                if u:
                    pe.wait_ge(moved[k], u)
                return bank[k]

            def split_matmuls(o, pairs):
                last, n = None, 0
                for (ah, al), (bh, bl) in pairs:
                    for a, b in ((ah, bh), (ah, bl), (al, bh)):
                        last = pe.matmul(o, a, b, start=(n == 0), stop=(n == 3 * len(pairs) - 1))
                        n += 1
                return last

            def both(w, *at):
                return tuple(x[at] for x in w)

            ALLP = slice(None)
            pe.wait_ge(ident_made, 1)
            pe.wait_ge(ab_in, 48)
            o = turn("ab")
            pe.transpose(o[0:NS, 0:P], ab_s[:, :], ident[:]).then_inc(filled[6], 1)

            def power(m):
                l = POWERS.index(m)
                o = turn(("pw", m))
                width = m if m <= 8 else 1
                pe.wait_ge(tw1_made, 1)
                if m > 1:
                    wait_moved(pe, ("tw", m // 2))
                    wait_moved(pe, ("pw", m // 2))
                rhs = PW[:, 1:m + 1, :] if m <= 8 else (PW[:, 16, :] if m == 16 else PB[:, l - 5, :])
                own = PW[:, m, :] if m <= 16 else PB[:, l - 5, :]
                pe.matmul(o[0:NS, 0:width * NS], TW[:, l, :], rhs, start=True, stop=True).then_inc(filled[4], 1)
                if m < 256:
                    o = turn(("tw", m))
                    pe.matmul(o[0:NS, 0:NS], own, TW[:, l, :], start=True, stop=True).then_inc(filled[5], 1)

            for n in range(NB):
                pe.wait_ge(x_in[n], 32)
                for c in range(KC):
                    o = turn(("xt", n, c))
                    for s in range(TPB):
                        last = pe.transpose(o[:, s * P:(s + 1) * P], X[:, TPB * n + s, c * P:(c + 1) * P], ident[:])
                    last.then_inc(filled[c], 1)
                if n == 0:
                    pe.wait_ge(w_hi, 1)
                    pe.wait_ge(w_lo, 1)
                o = turn(("u", n))
                wait_moved(pe, ("xt", n, 0))
                wait_moved(pe, ("xt", n, 1))
                split_matmuls(o[:, :], [
                    (both(WIN, ALLP, c, ALLP), (XH[:, n, c], XL[:, n, c])) for c in range(KC)
                ]).then_inc(sem_filled(("u", n)), 1)
                power(POWERS[n])
            pe.wait_ge(cd_in, 32)
            o = turn("cd")
            for c in range(KC):
                last = pe.transpose(o[:, c * P:(c + 1) * P], cd_s[:, c, :], ident[:])
            last.then_inc(filled[0], 1)
            pe.wait_ge(kv_in, 128)
            o = turn("ctx")
            for c in range(KC):
                last = pe.transpose(o[:, c * P:(c + 1) * P], ctx_s[:, c * P:(c + 1) * P], ident[:])
            last.then_inc(filled[1], 1)
            o = turn("w1")
            wait_moved(pe, "cd")
            pe.wait_ge(mx_made, 1)
            pe.matmul(o[:, 0:D], mx_s[:], cdt_s[:], start=True, stop=True).then_inc(filled[7], 1)

            hu4 = HU[:].rearrange("p (b i c) -> p b i c", b=B, i=L)
            for n in range(NB):
                wait_moved(pe, ("u", n))
            pe.wait_ge(w_hi, 2)
            pe.wait_ge(w_lo, 2)
            pe.wait_ge(starts_zero, 1)
            gate_bank = None
            for i in range(L):
                o = turn(("step", i))
                if i:
                    wait_moved(pe, ("step", i - 1))
                pe.matmul(o[0:NS, 0:B * CH], ab_s[:], hu4[:, :, i, :], start=True, stop=True)\
                    .then_inc(sem_filled(("step", i)), 1)
                g = i // 2
                n, m = g // 2, g % 2
                if i % 2 == 0:
                    gate_bank = turn(("gate", g))
                k = 0
                for c in range(KC):
                    for a, b in ((0, 0), (0, 1), (1, 0)):
                        if k // 3 == i % 2:
                            last = pe.matmul(gate_bank[:, :], WG[a][:, c, m * P:(m + 1) * P], (XH, XL)[b][:, n, c],
                                             start=(k == 0), stop=(k == 5))
                        k += 1
                if i % 2 == 1:
                    last.then_inc(sem_filled(("gate", g)), 1)
                    if 4 + i // 2 < 9:
                        power(POWERS[4 + i // 2])
            pe.wait_ge(wk3_made, 1)
            for k, d in enumerate(LEVELS):
                o = turn(("carry", k))
                if k:
                    wait_moved(pe, ("carry", k - 1))
                else:
                    wait_moved(pe, ("step", L - 1))
                    wait_moved(pe, ("pw", 256))
                own = PW[:, 16, :] if k == 0 else PB[:, k - 1, :]
                pe.matmul(o[0:NS, 0:B * (CH - d)], own, HS[:, :, 1:1 + CH - d], start=True, stop=True)\
                    .then_inc(sem_filled(("carry", k)), 1)
                if k < 2:
                    o = turn(("kt", k))
                    wait_moved(pe, "ctx")
                    for c in range(KC):
                        last = pe.matmul(o[:, 0:B * SE], wk_s[:, c, k * P:(k + 1) * P], ctd_s[:, c, :, 0, :],
                                         start=(c == 0), stop=(c == KC - 1))
                    last.then_inc(filled[k], 1)
                    o = turn(("v", k))
                    for c in range(KC):
                        pe.matmul(o[:, 0:D], ctd_s[:, c, k].rearrange("p r s -> p (r s)"), wv_s[:, c, :],
                                  start=(c == 0), stop=False)
                    pe.matmul(o[:, 0:D], ones_f[0:1, :], bv_row[:], start=False, stop=True)\
                        .then_inc(filled[4 + k], 1)
                for j in KSP[k]:
                    o = turn(("ks", j))
                    for c in range(KC):
                        last = pe.matmul(o[0:KQ, 0:B * SE], wk3_s[:, c * PR + j].rearrange("p r s -> p (r s)"),
                                         ctd_s[:, c, :, 0, :], start=(c == 0), stop=(c == KC - 1))
                    last.then_inc(sem_filled(("ks", j)), 1)
            wait_moved(pe, ("carry", 5))
            for q in range(4):
                o = turn(("cor", q))
                for i in range(4 * q, 4 * q + 4):
                    if i:
                        last = pe.matmul(o[0:NS, (i % 4) * P:(i % 4 + 1) * P], PW[:, i, :], HS[:, :, 0:CH],
                                         start=True, stop=True)
                last.then_inc(sem_filled(("cor", q)), 1)
            wait_moved(pe, "w1")
            pe.wait_ge(w_lo, 5)
            for n in range(NB):
                pe.wait_ge(hu_lo, n + 1)
                for c in range(KC):
                    o = turn(("y", n, c))
                    cols = slice(n * BLK, (n + 1) * BLK)
                    split_matmuls(o[:, :], [(both(W1, ALLP, slice(c * P, (c + 1) * P)), (HUH[:, cols], HUL[:, cols]))])\
                        .then_inc(filled[2 + c], 1)

            def mixer_out(t):
                n, s = t // TPB, t % TPB
                if s == 0:
                    pe.wait_ge(y_hi, KC * (n + 1))
                    if n < 2:
                        pe.wait_ge(y_lo_dve, KC * (n + 1))
                    else:
                        pe.wait_ge(y_lo_pool, KC * (n - 1))
                o = turn(("z1", t))
                cols = slice(s * P, (s + 1) * P)
                split_matmuls(o[:, 0:D], [
                    ((YH[:, n, c, cols], YL[:, n, c, cols]), both(WOUT, ALLP, c, ALLP)) for c in range(KC)
                ]).then_inc(sem_filled(("z1", t)), 1)

            def transposed(n):
                pe.wait_ge(ln1_out, TPB * (n + 1))
                for c in range(KC):
                    o = turn(("x1t", n, c))
                    for s in range(TPB):
                        last = pe.transpose(o[:, s * P:(s + 1) * P], X[:, TPB * n + s, c * P:(c + 1) * P], ident[:])
                    last.then_inc(filled[c], 1)

            def queries(n, c):
                o = turn(("q", n, c))
                wait_moved(pe, ("x1t", n, 0))
                wait_moved(pe, ("x1t", n, 1))
                split_matmuls(o[:, :], [
                    (both(WQ, ALLP, k, slice(c * P, (c + 1) * P)), (X1H[n % 2][:, k], X1L[n % 2][:, k]))
                    for k in range(KC)
                ]).then_inc(sem_filled(("q", n, c)), 1)

            def high_scores(t, c):
                n, s = t // TPB, t % TPB
                if t == 0:
                    pe.wait_ge(km_made, 4)
                if s == 0:
                    wait_moved(pe, ("q", n, 0))
                    wait_moved(pe, ("q", n, 1))
                o = turn(("mx", t, c))
                pe.matmul(o[:, :], QH[:, n % 2, c, s * P:(s + 1) * P],
                          KM[:, n // 2, c].rearrange("p h k -> p (h k)"), start=True, stop=True)\
                    .then_inc(sem_filled(("mx", t, c)), 1)

            def maxima_transposed(n):
                pe.wait_ge(nm_made, TPB * (n + 1))
                o = turn(("nmt", n))
                for s in range(TPB):
                    last = pe.transpose(o[0:32, s * P:(s + 1) * P],
                                        NMS[:, n % 2, s].rearrange("p j l h -> p (j l h)").bitcast(F32), ident[:])
                last.then_inc(filled[0], 1)

            def scores(m, j):
                r = m % 2
                if j == 0:
                    pe.wait_ge(ks_made, 2)
                    pe.wait_ge(qs_in[r], 16 * 3 * 4 * (m // 2 + 1))
                    wait_moved(pe, ("nmt", m))
                o = turn(("sc", m, j))
                pe.matmul(o[:, :], KS[0:KQ, j, m // 2, :], QS[0:KQ, r, j, :], start=True, stop=False)
                pe.matmul(o[:, :], SEL[:, j, :], NMT[0:32, r, :], start=False, stop=True)\
                    .then_inc(sem_filled(("sc", m, j)), 1)

            def weighted(t, half):
                m, s = t // TPB, t % TPB
                o = turn(("pv", t)) if half == 0 else bank_of(("pv", t))
                if t == 0 and half == 0:
                    pe.wait_ge(vb_made, 2)
                    wait_moved(pe, ("v", 1))
                for j in range(4 * half, 4 * half + 4):
                    if s == 0:
                        wait_moved(pe, ("sc", m, j))
                    last = pe.matmul(o[:, j * 34:(j + 1) * 34], PT[m % 2][:, j, s * P:(s + 1) * P],
                                     VB[:, m // 2, j].rearrange("p h d -> p (h d)"), start=True, stop=True)
                if half == 1:
                    last.then_inc(sem_filled(("pv", t)), 1)

            def attention_transposed(t):
                wait_moved(pe, ("pv", t))
                o = turn(("att", t))
                for c in range(KC):
                    last = pe.transpose(o[:, c * P:(c + 1) * P], ATT[:, t % TPB, c * P:(c + 1) * P], ident[:])
                last.then_inc(sem_filled(("att", t)), 1)

            def attention_out(t):
                o = turn(("z2", t))
                wait_moved(pe, ("att", t))
                split_matmuls(o[:, 0:D], [
                    ((ATH[:, t % 2, c], ATL[:, t % 2, c]), both(WO, ALLP, c, ALLP)) for c in range(KC)
                ]).then_inc(sem_filled(("z2", t)), 1)

            def x2_transposed(t):
                pe.wait_ge(ln2_out, t + 1)
                o = turn(("x2t", t))
                for c in range(KC):
                    last = pe.transpose(o[:, c * P:(c + 1) * P], X[:, t, c * P:(c + 1) * P], ident[:])
                last.then_inc(sem_filled(("x2t", t)), 1)

            def logits(t):
                if t == 0:
                    pe.wait_ge(bias2_in, 16 * (4 + NG))
                o = turn(("lg", t))
                wait_moved(pe, ("x2t", t))
                for c in range(KC):
                    last = pe.matmul(o[:, 0:E], X2T[:, t % 2, c * P:(c + 1) * P], wr_s[:, c, :],
                                     start=(c == 0), stop=(c == KC - 1))
                last.then_inc(sem_filled(("lg", t)), 1)

            for g in UNITS:
                if block_of(g, "x1t") is not None:
                    transposed(block_of(g, "x1t"))
                if live(g, "z1"):
                    mixer_out(g - LAG["z1"])
                for half in range(2):
                    if live(g, "sc"):
                        t = g - LAG["sc"]
                        scores(t // TPB, 2 * (t % TPB) + half)
                    if half == 0 and live(g, "lg"):
                        logits(g - LAG["lg"])
                    if live(g, "mx"):
                        high_scores(g - LAG["mx"], half)
                    if half == 0 and block_of(g, "nmt") is not None:
                        maxima_transposed(block_of(g, "nmt"))
                    if live(g, "pv"):
                        weighted(g - LAG["pv"], half)
                for c in range(KC):
                    if block_of(g - c, "q") is not None:
                        queries(block_of(g - c, "q"), c)
                if live(g, "att"):
                    attention_transposed(g - LAG["att"])
                if live(g, "z2"):
                    attention_out(g - LAG["z2"])
                if live(g, "x2t"):
                    x2_transposed(g - LAG["x2t"])

            pe.wait_ge(s2_made, 1)
            o = turn("st")
            pe.transpose(o[:, 0:P], S2[:].rearrange("p t e -> p (t e)"), ident[:]).then_inc(filled[0], 1)
            pe.wait_ge(masks_made, 1)
            for r in range(ROUNDS):
                o = turn(("tot", r))
                pe.wait_ge(cnt_made, r + 1)
                pe.matmul(o[:, 0:3], same_expert[:], cnt[:, r, :], start=True, stop=True)\
                    .then_inc(sem_filled(("tot", r)), 1)
            pe.wait_ge(rt_made, 1)
            o = turn("thr")
            pe.matmul(o[:, 0:E], ones_f[:], rt[:], start=True, stop=True).then_inc(filled[3], 1)
            pe.wait_ge(prefix_in, 1)
            rows_g = cig[:, :, NT - 1:NT].to_broadcast([P, E, NT])
            rows_e = cie[:, :, NT // B - 1:NT // B].to_broadcast([P, E * B, NT // B])
            flat = lambda t: t[:].rearrange("p e t -> p (e t)")
            o = turn("pg")
            pe.matmul(o[:, 0:P], before_b[:], rows_g, start=True, stop=False)
            pe.matmul(o[:, 0:P], ident_b[:], flat(cxg), start=False, stop=True).then_inc(filled[4], 1)
            o = turn("pe")
            pe.matmul(o[:, 0:P], chunk_before_b[:], rows_e, start=True, stop=False)
            pe.matmul(o[:, 0:P], even_to_odd_b[:], flat(cie), start=False, stop=False)
            pe.matmul(o[:, 0:P], own_odd_to_even_b[:], flat(cxe), start=False, stop=False)
            second = o[:, 0:P].rearrange("p (e b j) -> p e b j", e=E, b=B)[:, :, 1, :]
            first_rows = cie[:].rearrange("p (e b) j -> p e b j", b=B)[:, :, 0, NT // B - 1:NT // B]
            pe.matmul(second, ones_b[:], first_rows.to_broadcast([P, E, NT // B]), start=False, stop=False)
            pe.matmul(o[:, 0:P], ones_b[:], rows_g, start=False, stop=True).then_inc(filled[5], 1)
            pe.wait_ge(onehot_made, 1)
            o = turn("ids")
            for t in range(NT):
                last = pe.matmul(o[:, 0:P], OHH[:, t].rearrange("p e s -> p (e s)"),
                                 OHI[:, t].rearrange("p e s -> p (e s)"), start=(t == 0), stop=(t == NT - 1))
            last.then_inc(filled[6], 1)
            pe.wait_ge(lh_made, 1)
            o = turn("idx")
            pe.matmul(o[:, 0:16], lh[:].rearrange("p a l -> p (a l)"), mask_16[:], start=True, stop=True)\
                .then_inc(filled[7], 1)

            def tokens(g):
                for c in range(KC):
                    o = turn(("gt", g, c))
                    for k in range(2 * GS):
                        if c == 0 and k % 2 == 0:
                            pe.wait_ge(gathered[GS * g + k // 2], 32)
                        last = pe.transpose(o[:, k * P:(k + 1) * P], XG[:, 2 * GS * g + k, c * P:(c + 1) * P], ident[:])
                    last.then_inc(filled[5 + c], 1)

            def up(g):
                pe.wait_ge(wu_hi, g + 1)
                wait_up_low(pe, g)
                wait_moved(pe, ("gt", g, 0))
                wait_moved(pe, ("gt", g, 1))
                for f in range(FC):
                    o = turn(("up", g, f))
                    cols = slice(f * P, f * P + FW[f])
                    split_matmuls(o[0:FW[f], :], [
                        ((WUH[:, g % 2, c, cols], WUL[:, g % 2, c, cols]), (FTH[:, g % 2, c], FTL[:, g % 2, c]))
                        for c in range(KC)]).then_inc(filled[f % 3], 1)

            def down(e):
                g, first = e // GS, (e % GS) * TOP
                pe.wait_ge(wd_hi, e + 1)
                pe.wait_ge(wd_lo, e + 1)
                pe.wait_ge(ml_made, FC * (g + 1))
                for h in range(2):
                    o = turn(("dn", e, h))
                    pe.matmul(o[:, 0:D], ones_r[0:1, :], BDH[:, e % 3], start=True, stop=False)
                    pe.matmul(o[:, 0:D], ones_r[0:1, :], BDL[:, e % 3], start=False, stop=False)
                    cols = slice(first + h * P, first + (h + 1) * P)
                    for f in range(FC):
                        w = FW[f]
                        for a, b in ((MH, WDH), (MH, WDL), (ML, WDH)):
                            last = pe.matmul(o[:, 0:D], a[0:w, g % 2, f, cols], b[0:w, e % 3, f],
                                             start=False, stop=(f == FC - 1 and b is WDH and a is ML))
                    last.then_inc(filled[3 + h], 1)

            tokens(0)
            up(0)
            for g in range(1, NG + 1):
                if g < NG:
                    tokens(g)
                    up(g)
                for e in range(GS * (g - 1), GS * g):
                    down(e)

        @block.vector
        def _(dve):
            link = chain(dve, dve_step)

            def low(w, src, n):
                dve.wait_ge(w_hi, n)
                dve.tensor_tensor(w[1][:], src[:], w[0][:].bitcast(F32), ALU.subtract).then_inc(w_lo, 1)

            wait_filled(dve, "ab")
            dve.tensor_copy(mx_s[0:NS, :], bank[6][0:NS, 0:P]).then_inc(moved[6], 1)
            wait_moved(dve, "ab")
            dve.tensor_copy(TW[:, 0, :], mx_s[0:NS, 0:NS]).then_inc(tw1_made, 1)
            low(WIN, win_s, 1)
            for n in range(NB):
                for c in range(KC):
                    dve.wait_ge(xh_made, KC * n + c + 1)
                    dve.tensor_tensor(XL[:, n, c], bank[c][:], XH[:, n, c].bitcast(F32), ALU.subtract)\
                        .then_inc(moved[c], 1)
                m = POWERS[n]
                wait_filled(dve, ("pw", m))
                dve.tensor_copy(PW[:, m + 1:2 * m + 1, :],
                                bank[4][0:NS, 0:m * NS].rearrange("p (k n) -> p k n", n=NS)).then_inc(moved[4], 1)
            low(WG, wg_s, 2)
            wait_filled(dve, "cd")
            dve.tensor_copy(cdt_s[:], bank[0][:, 0:D]).then_inc(moved[0], 1)
            wait_filled(dve, "ctx")
            for c in range(KC):
                last = dve.tensor_copy(ctd_s[:, c], bank[1][:, c * P:(c + 1) * P].rearrange("p (b s) -> p b s", b=B)
                                       .unsqueeze(2).to_broadcast([P, B, 2, SE]))
            last.then_inc(moved[1], 1)

            def between_steps(i):
                if i == 0:
                    dve.wait_ge(w_hi, 6)
                    dve.tensor_tensor(W1[1][:], bank[7][:, 0:D], W1[0][:].bitcast(F32), ALU.subtract)\
                        .then_inc(moved[7], 1)
                if i == 2:
                    low(WOUT, wout_s, 3)
                if i == 4:
                    low(WQ, wq_s, 4)
                if i == 6:
                    low(WO, wo_s, 5)
                if i == 8:
                    dve.wait_ge(kv_in, 128)
                    dve.tensor_copy(wk3_s[:], wk_s[:].rearrange("p c (j s) -> p (c j) s", s=32).unsqueeze(2)
                                    .to_broadcast([P, KC * PR, 3, 32])).then_inc(wk3_made, 1)
                if i == 10:
                    dve.wait_ge(pool_consts, 1)
                    dve.tensor_scalar(pbits[:, 0:1], pidx[:], 4, 1, ALU.logical_shift_right, ALU.bitwise_and)
                    dve.tensor_scalar(pbits[:, 1:2], pidx[:], 4, None, ALU.logical_shift_right)
                    link(dve.tensor_copy(col_f[:], col_i[:]))
                    link(dve.tensor_copy(pf[:, 0:2], pbits[:, 0:2]))
                    dve.tensor_scalar(half_mask[:, 0:1], pf[:, 0:1], 0.0, None, ALU.is_equal)
                    dve.tensor_scalar(half_mask[:, 1:2], pf[:, 0:1], 1.0, None, ALU.is_equal)
                    dve.tensor_scalar(mask_hi3[:], col_f[:, 0:8], pf[:, 1:2], None, ALU.is_equal)\
                        .then_inc(head_masks, 1)

            hu4 = HU[0:NS, :].rearrange("p (b i c) -> p b i c", b=B, i=L)
            for i in range(L):
                name = ("step", i)
                wait_filled(dve, name)
                got = bank_of(name)[0:NS, 0:B * CH].rearrange("p (b c) -> p b c", b=B)
                dst = hu4[:, :, i + 1, :] if i + 1 < L else HS[:, :, 1:CH + 1]
                dve.tensor_copy(dst, got).then_inc(sem_moved(name), 1)
                if i % 2 == 1 and 4 + i // 2 < 9:
                    m = POWERS[4 + i // 2]
                    wait_filled(dve, ("pw", m))
                    dst = PB[:, i // 2, :] if m >= 16 else None
                    dve.tensor_copy(dst, bank[4][0:NS, 0:NS]).then_inc(moved[4], 1)
                between_steps(i)
            for k, d in enumerate(LEVELS):
                name = ("carry", k)
                wait_filled(dve, name)
                if k == 0:
                    wait_moved(dve, ("step", L - 1))
                else:
                    wait_moved(dve, ("carry", k - 1))
                dve.tensor_tensor(HS[:, :, 1 + d:CH + 1], HS[:, :, 1 + d:CH + 1],
                                  bank_of(name)[0:NS, 0:B * (CH - d)].rearrange("p (b c) -> p b c", b=B), ALU.add)\
                    .then_inc(sem_moved(name), 1)
                if k < 2:
                    wait_filled(dve, ("v", k))
                    dve.wait_ge(vb_init, 2)
                    got = bank[4 + k][:, 0:D].rearrange("p (j h d) -> p j h d", j=PR, h=2)
                    dve.tensor_copy(VB[0:SE, k, :, 0, 0:DK], got[0:SE, :, 0, :]).then_inc(vb_made, 1)
                    dve.tensor_copy(VB[SE:P, k, :, 1, 0:DK], got[SE:P, :, 1, :]).then_inc(moved[4 + k], 1)
                for j in KSP[k]:
                    wait_filled(dve, ("ks", j))
                    got = bank_of(("ks", j))[0:KQ, 0:B * SE].rearrange("p (b s) -> p b s", b=B)
                    for h in range(2):
                        last = dve.tensor_scalar(ksf_s[0:KQ, j, :, h, :], got, bk3_c[0:KQ, j:j + 1],
                                                 half_mask[0:KQ, h:h + 1], ALU.add, ALU.mult)
                    last.then_inc(sem_moved(("ks", j)), 1)
            wait_moved(dve, ("carry", 5))
            dve.tensor_copy(hu4[:, :, 0, :], HS[:, :, 0:CH]).then_inc(h_start, 1)
            for q in range(4):
                name = ("cor", q)
                wait_filled(dve, name)
                i0 = 1 if q == 0 else 0
                to = hu4[:, :, 4 * q + i0:4 * q + 4, :]
                got = bank_of(name)[0:NS, :].rearrange("p (i b c) -> p b i c", i=4, b=B)[:, :, i0:, :]
                dve.tensor_tensor(to, to, got, ALU.add).then_inc(sem_moved(name), 1)
            for n in range(NB):
                dve.wait_ge(hu_hi, n + 1)
                cols = slice(n * BLK, (n + 1) * BLK)
                dve.tensor_tensor(HUL[:, cols], HU[:, cols], HUH[:, cols].bitcast(F32), ALU.subtract)\
                    .then_inc(hu_lo, 1)
            wait_moved(dve, ("ks", PR - 1))
            wait_moved(dve, ("ks", PR - 2))
            dve.tensor_copy(KS[0:KQ], ksf_s[0:KQ].rearrange("p j b h k -> p j b (h k)")).then_inc(ks_hi, 1)
            for n in range(NB):
                for c in range(KC):
                    wait_filled(dve, ("y", n, c))
                    wait_moved(dve, ("gate", 2 * n + c))
                    dve.tensor_tensor(G[:, n, c], bank[2 + c][:], G[:, n, c], ALU.mult).then_inc(moved[2 + c], 1)
                if n < 2:
                    for c in range(KC):
                        dve.wait_ge(y_hi, KC * n + c + 1)
                        dve.tensor_tensor(YL[:, n, c], G[:, n, c], YH[:, n, c].bitcast(F32), ALU.subtract)\
                            .then_inc(y_lo_dve, 1)

            def add(which, t, name):
                if t % TPB == 0:
                    dve.wait_ge(xb_added if which == 1 else bo_added, t // TPB + 1)
                wait_filled(dve, name)
                r = X[:, t, 0:D]
                dve.tensor_tensor(r, bank_of(name)[:, 0:D], r, ALU.add).then_inc(sem_moved(name), 1)

            def statistics(which, t, name):
                wait_moved(dve, name)
                k = norm_at[which, t]
                dve.bn_stats(bn6[:, k, :], X[:, t, 0:D]).then_inc(ln_stats, 1)

            def mean_variance(which, t):
                k = norm_at[which, t]
                dve.wait_ge(ln_stats, k + 1)
                dve.bn_aggr(mean_var[:, k, :], bn6[:, k, :]).then_inc(ln_var, 1)

            def maxima(t, c):
                name = ("mx", t, c)
                wait_filled(dve, name)
                half = HD // KC
                dve.tensor_reduce(NMF[:, t % 2, c * half:(c + 1) * half],
                                  bank_of(name)[:].rearrange("p (h k) -> p h k", k=SE), AX.X, ALU.max,
                                  negate=True).then_inc(sem_moved(name), 1)

            def by_pair(t):
                return NMF[:, t % 2, :].rearrange("p (j h) -> p j h", h=2)

            def maxima_high(t):
                for c in range(KC):
                    wait_moved(dve, ("mx", t, c))
                n, s = t // TPB, t % TPB
                if n >= 2 and s == 0:
                    wait_filled(dve, ("nmt", n - 2))
                dve.tensor_copy(NMS[:, n % 2, s, :, 0, :], by_pair(t)).then_inc(nm_hi, 1)

            def maxima_low(t):
                dve.wait_ge(nm_hi, t + 1)
                ns = NMS[:, t // TPB % 2, t % TPB]
                dve.tensor_tensor(ns[:, :, 1, :], by_pair(t), ns[:, :, 0, :].bitcast(F32), ALU.subtract)\
                    .then_inc(nm_made, 1)

            def weighted_sums(t):
                return bank_of(("pv", t))[:, 0:34 * PR].rearrange("p (h d) -> p h d", d=DK + 1)

            def inverse_sums(t):
                wait_filled(dve, ("pv", t))
                dve.reciprocal(REC[:, t % 2, :].unsqueeze(2), weighted_sums(t)[:, :, DK:DK + 1]).then_inc(rec_made, 1)

            def attended(t):
                dve.wait_ge(rec_made, t + 1)
                if t >= TPB:
                    wait_filled(dve, ("att", t - TPB))
                dve.tensor_tensor(ATT[:, t % TPB, :].rearrange("p (h d) -> p h d", d=DK), weighted_sums(t)[:, :, 0:DK],
                                  REC[:, t % 2, :].unsqueeze(2).to_broadcast([P, HD, DK]), ALU.mult)\
                    .then_inc(sem_moved(("pv", t)), 1)

            def masks():
                for k, (sh, m) in enumerate(((0, 7), (0, 63), (3, 15), (6, 1))):
                    dve.tensor_scalar(pbits[:, 2 + k:3 + k], pidx[:], sh, m, ALU.logical_shift_right, ALU.bitwise_and)
                dve.tensor_scalar(colm_i[:], col_i[:], 63, None, ALU.bitwise_and)
                link(dve.tensor_copy(pf[:, 6:7], pidx[:]))
                dve.tensor_copy(pf[:, 2:6], pbits[:, 2:6])
                dve.tensor_copy(colm_f[:], colm_i[:])
                link(dve.tensor_copy(ident_b[:], ident[:]))
                dve.tensor_scalar(pf[:, 7:8], pf[:, 6:7], 64.0, None, ALU.add)
                dve.tensor_scalar(pf[:, 0:1], pf[:, 6:7], -64.0, None, ALU.add)
                link(dve.tensor_scalar(colm_i[:], col_i[:], 7, None, ALU.bitwise_and))
                dve.tensor_scalar(chunk_before_b[:], colm_f[:], pf[:, 3:4], None, ALU.is_gt)
                dve.tensor_scalar(pf[:, 1:2], pf[:, 3:4], 16.0, pf[:, 5:6], ALU.mult, ALU.add)
                dve.tensor_scalar(own_odd_to_even_b[:], col_f[:], pf[:, 0:1], None, ALU.is_equal)
                link(dve.tensor_copy(col7_f[:], colm_i[:]))
                dve.tensor_scalar(tok_f[:], tok_i[:], pf[:, 1:2], None, ALU.add)
                dve.tensor_scalar(same_expert[:], col7_f[:], pf[:, 2:3], None, ALU.is_equal)
                dve.tensor_scalar(before_b[:], col_f[:], pf[:, 6:7], None, ALU.is_gt)
                dve.tensor_scalar(even_to_odd_b[:], col_f[:], pf[:, 7:8], None, ALU.is_equal)
                dve.tensor_tensor(own_odd_to_even_b[:], own_odd_to_even_b[:], ident_b[:], ALU.add)
                dve.tensor_scalar(mask_lo3[:], col_f[:, 0:8], pf[:, 2:3], None, ALU.is_equal)
                dve.tensor_scalar(mask_16[:], col_f[:, 0:16], pf[:, 4:5], None, ALU.is_equal)
                for a, b, sh in ((1, 2, 2), (2, 4, 4), (4, 8, 8), (8, ROUNDS, 16)):
                    link(dve.tensor_scalar(steps[:, a:b, :], steps[:, 0:b - a, :], sh, None, ALU.logical_shift_right))
                dve.tensor_scalar(junk_m[:], col_f[:, 0:1], 0.0, None, ALU.mult).then_inc(masks_made, 1)

            for g in UNITS:
                n = block_of(g, "x1t")
                if n is not None:
                    for c in range(KC):
                        dve.wait_ge(x1h_made, KC * n + c + 1)
                        dve.tensor_tensor(X1L[n % 2][:, c], bank[c][:], X1H[n % 2][:, c].bitcast(F32), ALU.subtract)\
                            .then_inc(moved[c], 1)
                z1, mx, pv, z2 = [g - LAG[k] for k in ("z1", "mx", "pv", "z2")]
                if live(g, "z1"):
                    add(1, z1, ("z1", z1))
                if live(g, "lg"):
                    t = g - LAG["lg"]
                    if t == 0:
                        dve.wait_ge(bias2_in, 16 * (4 + NG))
                    wait_filled(dve, ("lg", t))
                    dve.tensor_tensor(lgt[:, t, :], bank_of(("lg", t))[:, 0:E], br_all[:], ALU.add)\
                        .then_inc(sem_moved(("lg", t)), 1)
                if live(g - 1, "z2"):
                    mean_variance(2, z2 - 1)
                if live(g, "mx"):
                    maxima(mx, 0)
                if live(g, "z1"):
                    statistics(1, z1, ("z1", z1))
                if live(g, "mx"):
                    maxima(mx, 1)
                if live(g, "z1"):
                    mean_variance(1, z1)
                if live(g, "mx"):
                    maxima_high(mx)
                if live(g, "pv"):
                    inverse_sums(pv)
                if live(g, "mx"):
                    maxima_low(mx)
                if live(g, "pv"):
                    attended(pv)
                for c in range(KC):
                    n = block_of(g - c, "q")
                    if n is not None:
                        dve.wait_ge(q_hi, KC * n + c + 1)
                        dve.scalar_tensor_tensor(QL[:, n % 2, c], bank_of(("q", n, c))[:], bq_c[:, c:c + 1],
                                                 QH[:, n % 2, c].bitcast(F32), ALU.add, ALU.subtract)\
                            .then_inc(sem_moved(("q", n, c)), 1)
                if g == 1:
                    masks()
                if live(g, "att"):
                    t = g - LAG["att"]
                    dve.wait_ge(ath_made, t + 1)
                    dve.tensor_tensor(ATL[:, t % 2].rearrange("p c k -> p (c k)"), bank_of(("att", t))[:, 0:D],
                                      ATH[:, t % 2].rearrange("p c k -> p (c k)").bitcast(F32), ALU.subtract)\
                        .then_inc(sem_moved(("att", t)), 1)
                if live(g, "z2"):
                    add(2, z2, ("z2", z2))
                    statistics(2, z2, ("z2", z2))

            phase2_over(dve)
            link(dve.tensor_reduce(mxl[:], lgt[:], AX.X, ALU.max))
            dve.tensor_tensor(lm[:], lgt[:], mxl[:].unsqueeze(2).to_broadcast([P, NT, E]), ALU.subtract)\
                .then_inc(lm_made, 1)
            dve.wait_ge(ex_made, 1)
            link(dve.tensor_reduce(sm[:], ex[:], AX.X, ALU.add))
            link(dve.reciprocal(rcp[:], sm[:]))
            dve.tensor_tensor(S2[:], ex[:], rcp[:].unsqueeze(2).to_broadcast([P, NT, E]), ALU.mult)\
                .then_inc(s2_made, 1)
            link(dve.memset(best[:, 0, 0:1], 0.0))
            wait_filled(dve, "st")
            dve.tensor_copy(ST[:], bank[0][:, 0:P]).then_inc(moved[0], 1)
            wait_moved(dve, "st")
            dve.wait_ge(masks_made, 1)
            link(dve.tensor_copy(cand[:, 0, :], steps[:, 0, :]))
            for r in range(ROUNDS):
                for j in range(3):
                    last = dve.tensor_scalar(junk[:, j, :], ST[:], cand[:, r, j:j + 1].bitcast(F32), 0.0, ALU.is_ge,
                                             ALU.add, accum_out=cnt[:, r, j:j + 1])
                last.then_inc(cnt_made, 1)
                name = ("tot", r)
                wait_filled(dve, name)
                dve.scalar_tensor_tensor(best[:, r, 1:4], bank_of(name)[:, 0:3], TOP - 0.5,
                                         cand[:, r, :].bitcast(F32), ALU.is_ge, ALU.mult)\
                    .then_inc(sem_moved(name), 1)
                wait_moved(dve, name)
                link(dve.tensor_reduce(best[:, r + 1, 0:1], best[:, r, :], AX.X, ALU.max))
                if r + 1 < ROUNDS:
                    link(dve.tensor_tensor(cand[:, r + 1, :], steps[:, r + 1, :],
                                           best[:, r + 1, 0:1].bitcast(I32).to_broadcast([P, 3]), ALU.bitwise_or))
            dve.tensor_scalar(rt[:], ident[:, 0:E], best[:, ROUNDS, 0:1], None, ALU.mult).then_inc(rt_made, 1)
            wait_filled(dve, "thr")
            dve.tensor_copy(thr[:], bank[3][:, 0:E]).then_inc(moved[3], 1)
            wait_moved(dve, "thr")
            probs = S2[:].rearrange("p t e -> p e t")
            limit = thr[:].unsqueeze(2).to_broadcast([P, E, NT])
            flat = lambda t: t[:].rearrange("p e t -> p (e t)")
            link(dve.tensor_tensor(gt[:], probs, limit, ALU.is_gt))
            link(dve.tensor_tensor(ge[:], probs, limit, ALU.is_ge))
            link(dve.tensor_tensor(eq[:], ge[:], gt[:], ALU.subtract))
            link(dve.tensor_tensor_scan(flat(cig), flat(reset_g), flat(gt), 0.0, ALU.mult, ALU.add))
            link(dve.tensor_tensor_scan(flat(cie), flat(reset_e), flat(eq), 0.0, ALU.mult, ALU.add))
            link(dve.tensor_tensor(cxg[:], cig[:], gt[:], ALU.subtract))
            dve.tensor_tensor(flat(cxe), flat(cie), flat(eq), ALU.subtract).then_inc(prefix_in, 1)
            dve.tensor_scalar(sl[2][:], ge[:], -4096.0, 4096.0, ALU.mult, ALU.add)
            wait_filled(dve, "pg")
            dve.tensor_tensor(flat(sl[0]), bank[4][:, 0:P], flat(gt), ALU.mult).then_inc(moved[4], 1)
            wait_filled(dve, "pe")
            dve.tensor_tensor(flat(sl[1]), bank[5][:, 0:P], flat(eq), ALU.mult).then_inc(moved[5], 1)
            wait_moved(dve, "pe")
            link(dve.tensor_tensor(sl[3][:], sl[0][:], sl[1][:], ALU.add))
            link(dve.tensor_tensor(sl_i[:, 0], sl[3][:], sl[2][:], ALU.add))
            dve.tensor_scalar(sl_i[:, 1], sl_i[:, 0], 4, None, ALU.logical_shift_right)
            link(dve.tensor_scalar(sl_i[:, 2], sl_i[:, 0], 15, None, ALU.bitwise_and))
            dve.tensor_copy(sl_f[:], sl_i[:, 1:3]).then_inc(slots_made, 1)
            dve.wait_ge(slots_made, 1)
            digit = col_f[:, 0:16].unsqueeze(1).unsqueeze(1)

            def by_tile(k):
                return sl_f[:, k].rearrange("p e t -> p t e").unsqueeze(3).to_broadcast([P, NT, E, 16])

            link(dve.tensor_tensor(OHL[:], by_tile(1), digit.to_broadcast([P, NT, E, 16]), ALU.is_equal))
            link(dve.tensor_tensor(OHH[:], by_tile(0), digit.to_broadcast([P, NT, E, 16]), ALU.is_equal))
            dve.tensor_tensor(OHI[:].rearrange("p t e s -> p t (e s)"), OHL[:].rearrange("p t e s -> p t (e s)"),
                              tok_f[:].unsqueeze(2).to_broadcast([P, NT, E * 16]), ALU.mult).then_inc(onehot_made, 1)
            wait_filled(dve, "ids")
            dve.tensor_tensor(ym[:], bank[6][:, 0:P].rearrange("p (e s) -> p e s", e=E),
                              mask_hi3[:].unsqueeze(2).to_broadcast([P, E, 16]), ALU.mult).then_inc(moved[6], 1)
            wait_moved(dve, "ids")
            link(dve.tensor_reduce(lk[:], ym[:].rearrange("p e s -> p s e"), AX.X, ALU.add))
            dve.tensor_tensor(lh[:], lk[:].unsqueeze(1).to_broadcast([P, 8, 16]),
                              mask_lo3[:].unsqueeze(2).to_broadcast([P, 8, 16]), ALU.mult).then_inc(lh_made, 1)
            wait_filled(dve, "idx")
            dve.tensor_copy(idx[:], bank[7][:, 0:16]).then_inc(idx_made, 1)

            def experts_out(e):
                for h in range(2):
                    s = 2 * e + h
                    wait_filled(dve, ("dn", e, h))
                    if e >= 2:
                        dve.wait_ge(scattered[e - 2], 32)
                    dve.tensor_scalar(OUT[:, s % 4, :], bank[3 + h][:, 0:D], XG[:, s, D + e:D + e + 1], None,
                                      ALU.mult).then_inc(moved[3 + h], 1)

            for g in range(NG):
                for c in range(KC):
                    dve.wait_ge(fth_made, KC * g + c + 1)
                    dve.tensor_tensor(FTL[:, g % 2, c], bank[5 + c][:], FTH[:, g % 2, c].bitcast(F32), ALU.subtract)\
                        .then_inc(moved[5 + c], 1)
                for f in range(FC):
                    w, q = FW[f], g * FC + f
                    if g >= 2 and f == 0:
                        wait_filled(dve, ("dn", GS * (g - 2) + 1, 1))
                    wait_moved(dve, ("up", g, f))
                    dve.tensor_copy(MH[0:w, g % 2, f], MF[0:w, q % 3]).then_inc(mh_made, 1)
                    dve.wait_ge(mh_made, q + 1)
                    dve.tensor_tensor(ML[0:w, g % 2, f], MF[0:w, q % 3], MH[0:w, g % 2, f].bitcast(F32),
                                      ALU.subtract).then_inc(ml_made, 1)
                    if f == 1 and 2 <= g + 1 < NG:
                        dve.wait_ge(wu_hi, g + 2)
                        dve.tensor_tensor(WUL[:, (g + 1) % 2], WUR[:, (g + 1) % 2], WUH[:, (g + 1) % 2].bitcast(F32),
                                          ALU.subtract).then_inc(wu_lo_dve, 1)
                if g:
                    experts_out(GS * (g - 1))
                    experts_out(GS * (g - 1) + 1)
            experts_out(E - 2)
            experts_out(E - 1)
            for t in range(NT + 1):
                if t < NT:
                    dve.wait_ge(y_in[t // 2], 16)
                    dve.bn_stats(bn6[:, 2 * NT + t, :], Y[:, t, :]).then_inc(ln_stats, 1)
                if t:
                    mean_variance(3, t - 1)


_INPUTS = ["x", "ctx_1024", "L0_attn_W_in", "L0_attn_b_in", "L0_attn_W_gate", "L0_attn_b_gate", "L0_attn_W_out",
           "L0_attn_b_out", "L0_attn_A", "L0_attn_Bm", "L0_attn_C", "L0_attn_D", "L0_xattn_Wq", "L0_xattn_bq",
           "L0_xattn_Wk", "L0_xattn_bk", "L0_xattn_Wv", "L0_xattn_bv", "L0_xattn_Wo", "L0_xattn_bo", "L0_ffn_Wr",
           "L0_ffn_br", "L0_ffn_W_up", "L0_ffn_b_up", "L0_ffn_W_down", "L0_ffn_b_down"]


def kernel(**inputs):
    import numpy as np
    from concourse import bacc
    from concourse.bass_utils import run_bass_kernel_spmd

    nc = bacc.Bacc("TRN2", target_bir_lowering=False, num_devices=1)
    arrays, args = {}, []
    for name in _INPUTS:
        a = np.ascontiguousarray(inputs[name])
        arrays[f"in_{name}"] = a
        args.append(nc.dram_tensor(f"in_{name}", a.shape, mybir.dt.from_np(a.dtype), kind="ExternalInput").ap())
    out = nc.dram_tensor("out", arrays["in_x"].shape, mybir.dt.float32, kind="ExternalOutput").ap()
    decoder_block(nc, *args, out)
    return run_bass_kernel_spmd(nc, [arrays], core_ids=[0]).results[0]["out"]
```

```python
from contextlib import ExitStack

import concourse.bass as bass
from concourse import mybir


def decoder_block(
    nc, x, ctx, w_in, b_in, w_gate, b_gate, w_out, b_out, a_mat, b_mat, c_mat, d_mat,
    wq, bq, wk, bk, wv, bv, wo, bo, wr, br, w_up, b_up, w_down, b_down, out,
):
    F32, F32R, BF16 = mybir.dt.float32, mybir.dt.float32r, mybir.dt.bfloat16
    I32, U32 = mybir.dt.int32, mybir.dt.uint32
    ALU, ACT, AX = mybir.AluOpType, mybir.ActivationFunctionType, mybir.AxisListType

    B, T, D = x.shape
    P = 128
    KC = D // P
    TOK = B * T
    L = 16
    CH = T // L
    NT = TOK // P
    NB = 4
    BLK = TOK // NB
    TPB = BLK // P
    NS = w_in.shape[1]
    SE = ctx.shape[1]
    DK = 16
    HD = D // DK
    PR = HD // 2
    E = wr.shape[1]
    TOP = TOK // E
    NG = w_up.shape[0]
    GS = E // NG
    F = w_up.shape[2]
    FC = -(-F // P)
    FW = [min(P, F - f * P) for f in range(FC)]
    RW = D + E
    EPS = 1e-5
    SCALE = DK ** -0.5
    ROUNDS = 15
    KQ = 3 * 32
    LAG = {"z1": -5, "mx": 2, "nmt": 6, "sc": 7, "pv": 11, "att": 12, "z2": 13, "x2t": 15, "lg": 16}
    QM_BY_ACT = 2
    LOW_BY_DVE = 5
    BY_POOL = 8
    UNITS = range(LAG["z1"], NT + LAG["lg"])
    LEVELS = [1 << k for k in range(6)]

    es = ExitStack()
    with es:
        def dram(name, shape):
            return nc.dram_tensor(name, shape, F32, kind="Internal").ap()

        routed = dram("routed_rows", (TOK, RW))
        summed = dram("summed_rows", (TOK, D))

        top = [16512]

        def place(name, shape, dt, at=None):
            size = 2 if dt is BF16 else 4
            for s in shape[1:]:
                size *= s
            size = -(-size // 32) * 32
            if at is None:
                at = top[0]
                top[0] += size
            assert at + size <= 229344, (name, at + size)
            t = nc.alloc_sbuf_tensor_at(name, shape, dt, offset=at)
            offset_of[name] = at
            end_of[name] = at + size
            return t

        offset_of, end_of = {}, {}

        ident = place("ident", [P, P], F32)
        ones_f = place("ones_f", [P, P], F32)
        ones_r = place("ones_r", [P, P], F32R)
        ones_b = place("ones_b", [P, P], BF16)
        ident_b = place("ident_b", [P, P], BF16)
        same_expert = place("same_expert", [P, P], BF16)
        before_b = place("before_b", [P, P], BF16)
        chunk_before_b = place("chunk_before_b", [P, P], BF16)
        even_to_odd_b = place("even_to_odd_b", [P, P], BF16)
        own_odd_to_even_b = place("own_odd_to_even_b", [P, P], BF16)
        pidx = place("pidx", [P, 1], I32)
        pbits = place("pbits", [P, 8], I32)
        pf = place("pf", [P, 8], F32)
        col_i = place("col_i", [P, P], I32)
        col_f = place("col_f", [P, P], F32)
        colm_i = place("colm_i", [P, P], I32)
        colm_f = place("colm_f", [P, P], F32)
        col7_f = place("col7_f", [P, P], F32)
        half_mask = place("half_mask", [P, 2], F32)
        mask_hi3 = place("mask_hi3", [P, 8], F32)
        mask_lo3 = place("mask_lo3", [P, 8], F32)
        mask_16 = place("mask_16", [P, 16], F32)
        steps = place("steps", [P, ROUNDS, 4], I32)
        reset_g = place("reset_g", [P, E, NT], BF16)
        reset_e = place("reset_e", [P, E * B, NT // B], BF16)
        tok_i = place("tok_i", [P, NT], I32)
        junk_m = place("junk_m", [P, 1], F32)
        step_f = place("step_f", [P, NT], F32)
        chunk16 = place("chunk16", [P, B], F32)
        col8_i = place("col8_i", [P, P], I32)
        digit_b = place("digit_b", [P, 16, E], BF16)
        warm = place("warm", [P, 1], F32)
        mask_own = place("mask_own", [P, E], F32)
        b_in_c = place("b_in_c", [P, 1], F32)
        b_gate_c = place("b_gate_c", [P, KC], F32)
        bq_c = place("bq_c", [P, KC], F32)
        bk_c = place("bk_c", [P, KC], F32)
        bk3_c = place("bk3_c", [P, PR], F32)
        bk3h = place("bk3h", [P, 2, PR], F32)
        bv_row = place("bv_row", [1, D], F32)
        br_all = place("br_all", [P, E], F32)
        b_up_c = place("b_up_c", [P, NG, FC], F32)
        wr_s = place("wr_s", [P, KC, E], F32)
        bn6 = place("bn6", [P, 3 * NT, 6], F32)
        mean_var = place("mean_var", [P, 3 * NT, 2], F32)
        var_eps = place("var_eps", [P, 3 * NT], F32)
        neg_half = place("neg_half", [P, 4], F32)
        rstd = place("rstd", [P, 3 * NT], F32)
        shift = place("shift", [P, 3 * NT], F32)
        lgt = place("lgt", [P, NT, E], F32)
        X = place("X", [P, NT, RW], F32)
        PHASE3 = top[0]

        b_out_all = place("b_out_all", [P, D], F32)
        bo_all = place("bo_all", [P, D], F32)
        XH = place("XH", [P, NB, KC, BLK], F32R)
        XL = place("XL", [P, NB, KC, BLK], F32R)
        YH = place("YH", [P, NB, KC, BLK], F32R, offset_of["XH"])
        YL = place("YL", [P, NB, KC, BLK], F32R, offset_of["XL"])
        QH = place("QH", [P, 2, KC, BLK], F32R, offset_of["XH"])
        QL = place("QL", [P, 2, KC, BLK], F32R, offset_of["XL"])
        HU = place("HU", [P, TOK], F32)
        NMT = place("NMT", [P, 2, BLK], F32R, offset_of["HU"])
        X2T = place("X2T", [P, 2, D], F32, end_of["NMT"])
        HUH = place("HUH", [P, TOK], F32R)
        HUL = place("HUL", [P, TOK], F32R)
        PT1 = place("PT1", [P, PR, BLK], F32, offset_of["HUH"])
        G = place("G", [P, NB, KC, BLK], F32)
        X1H = [place(f"X1H{r}", [P, KC, BLK], F32R, offset_of["G"] + 8192 * r) for r in range(2)]
        X1L = [place(f"X1L{r}", [P, KC, BLK], F32R, offset_of["G"] + 8192 * r + 4096) for r in range(2)]
        QS = place("QS", [P, 2, PR, BLK], F32R)
        PT0 = place("PT0", [P, PR, BLK], F32)
        PT = [PT0, PT1]
        WIN = [place(n, [P, KC, P], F32R) for n in ("WINH", "WINL")]
        WG = [place(n, [P, KC, D], F32R) for n in ("WGH", "WGL")]
        WOUT = [place(n, [P, KC, D], F32R) for n in ("WOUTH", "WOUTL")]
        WQ = [place(n, [P, KC, D], F32R) for n in ("WQH", "WQL")]
        WO = [place(n, [P, KC, D], F32R) for n in ("WOH", "WOL")]
        W1 = [place(n, [P, D], F32R) for n in ("W1H", "W1L")]
        KS = place("KS", [P, PR, B, P], F32R)
        KM = place("KM", [P, B, KC, HD // KC, SE], F32R)
        VB = place("VB", [P, B, PR, 2, DK + 1], F32)
        ATT = place("ATT", [P, TPB, D], F32)
        ATH = place("ATH", [P, 2, KC, P], F32R)
        ATL = place("ATL", [P, 2, KC, P], F32R)
        PW = place("PW", [NS, L + 1, NS], F32, offset_of["ATT"])
        PB = place("PB", [NS, 5, NS], F32, end_of["PW"])
        TW = place("TW", [NS, 9, NS], F32)
        HS = place("HS", [NS, B, CH + 1], F32)
        NMF = place("NMF", [P, TPB, HD], F32)
        NMS = place("NMS", [P, 2, TPB, PR, 2, 2], F32R)
        REC = place("REC", [P, 2, HD], F32)
        SEL = place("SEL", [32, PR, P], F32R)
        stage = [offset_of["QS"]]

        def staged(name, shape, dt=F32):
            t = place(name, shape, dt, stage[0])
            stage[0] = end_of[name]
            assert stage[0] <= end_of["PT0"]
            return t

        win_s = staged("win_s", [P, KC, P])
        wg_s = staged("wg_s", [P, KC, D])
        wout_s = staged("wout_s", [P, KC, D])
        wq_s = staged("wq_s", [P, KC, D])
        wo_s = staged("wo_s", [P, KC, D])
        wk_s = staged("wk_s", [P, KC, D])
        wv_s = staged("wv_s", [P, KC, D])
        wk3_s = staged("wk3_s", [P, KC * PR, 3, 32])
        ab_s = staged("ab_s", [P, NS])
        mx_s = staged("mx_s", [P, P])
        cd_s = staged("cd_s", [P, KC, P])
        cdt_s = staged("cdt_s", [P, D])
        ctx_s = staged("ctx_s", [P, D])
        ctd_s = staged("ctd_s", [P, KC, B, 2, SE])
        kt_s = staged("kt_s", [P, KC, B * SE])
        ksf_s = staged("ksf_s", [P, PR, B, 2, SE])
        sel_s = staged("sel_s", [32, PR, 2, SE])

        top[0] = PHASE3
        idx = place("idx", [P, NT], I32)
        XG = place("XG", [P, NT, RW], F32)
        FTH = place("FTH", [P, 2, KC, GS * TOP], F32R, offset_of["X"])
        FTL = place("FTL", [P, 2, KC, GS * TOP], F32R, end_of["FTH"])
        MF = place("MF", [P, 3, GS * TOP], F32)
        MH = place("MH", [P, 2, FC, GS * TOP], F32R)
        ML = place("ML", [P, 2, FC, GS * TOP], F32R)
        OHH = place("OHH", [P, NT, 16, E], BF16, offset_of["MH"])
        OHL = place("OHL", [P, NT, 16, E], BF16, end_of["OHH"])
        OHC = place("OHC", [P, NT, 16, E], BF16, end_of["OHL"])
        OHS = place("OHS", [P, NT, 16, E], BF16, end_of["OHC"])
        step_b = place("step_b", [P, NT, P], BF16, end_of["OHS"])
        WUR = place("WUR", [P, 2, KC, F], F32)
        WUH = place("WUH", [P, 2, KC, F], F32R)
        WUL = place("WUL", [P, 2, KC, F], F32R)
        WDR = place("WDR", [P, 2, FC, D], F32)
        WDH = place("WDH", [P, 3, FC, D], F32R)
        WDL = place("WDL", [P, 3, FC, D], F32R)
        BDR = place("BDR", [1, 2, D], F32)
        BDH = place("BDH", [1, 3, D], F32R)
        BDL = place("BDL", [1, 3, D], F32R)
        OUT = place("OUT", [P, 4, D], F32)
        Y = place("Y", [P, NT, D], F32, offset_of["MH"])

        top[0] = offset_of["ML"]
        S2 = place("S2", [P, NT, E], F32)
        mxl = place("mxl", [P, NT], F32)
        lm = place("lm", [P, NT, E], F32)
        ex = place("ex", [P, NT, E], F32)
        sm = place("sm", [P, NT], F32)
        rcp = place("rcp", [P, NT], F32)
        ST = place("ST", [P, P], F32)
        junk = place("junk", [P, 3, P], BF16)
        cand = place("cand", [P, ROUNDS + 1, 4], I32)
        follow = place("follow", [P, ROUNDS, 4, 4], I32)
        cnt = place("cnt", [P, ROUNDS, 3], BF16)
        rt = place("rt", [P, E], F32)
        thr = place("thr", [P, E], F32)
        gt = place("gt", [P, E, NT], BF16)
        ge = place("ge", [P, E, NT], BF16)
        eq = place("eq", [P, E, NT], BF16)
        cig = place("cig", [P, E, NT], BF16)
        cie = place("cie", [P, E * B, NT // B], BF16)
        cxg = place("cxg", [P, E, NT], BF16)
        cxe = place("cxe", [P, E, NT], BF16)
        sl = [place(f"sl{k}", [P, E, NT], F32) for k in range(5)]
        sl_i = place("sl_i", [P, 3, E, NT], I32)
        sl_f = place("sl_f", [P, 2, NT, E], BF16)
        ym = place("ym", [P, 16, E], F32)
        lk = place("lk", [P, 16], F32)
        lh = place("lh", [P, 8, 16], F32)
        assert top[0] <= end_of["ML"]

        bank = [es.enter_context(nc.psum_tensor(f"bank{k}", [P, 512], F32)) for k in range(8)]

        def sem(name):
            return es.enter_context(nc.semaphore(name))

        filled = [sem(f"filled{k}") for k in range(8)]
        moved = [sem(f"moved{k}") for k in range(8)]

        def live(g, stage):
            return 0 <= g - LAG[stage] < NT

        def block_of(g, stage):
            t = g - LAG.get(stage, 0)
            return t // TPB if 0 <= t < NT and t % TPB == 0 else None

        norm_order = []
        for g in UNITS:
            for which, stage in ((1, "z1"), (2, "z2")):
                if live(g, stage):
                    norm_order.append((which, g - LAG[stage]))
        norm_order += [(3, t) for t in range(NT)]
        norm_at = {what: k for k, what in enumerate(norm_order)}

        turn_of, uses = {}, [0] * 8

        def product(name, k):
            turn_of[name] = (k, uses[k])
            uses[k] += 1

        POWERS = [1 << k for k in range(9)]
        def xt_products(n):
            for c in range(KC):
                product(("xt", n, c), 6 * (n % 2) + c)

        xt_products(0)
        product("ab", 6)
        for n in range(NB):
            if n + 1 < NB:
                xt_products(n + 1)
            product(("u", n), 2 + n % 2)
            product(("pw", POWERS[n]), 4)
            product(("tw", POWERS[n]), 5)
        product("cd", 0)
        product("ctx", 1)
        product("w1", 7)
        for i in range(L):
            product(("step", i), 6 + i % 2)
            if i % 2 == 0:
                product(("gate", i // 2), 2 + (i // 2) % 2)
            if i % 2 == 1 and 4 + i // 2 < 9:
                product(("pw", POWERS[4 + i // 2]), 4)
                if POWERS[4 + i // 2] < 256:
                    product(("tw", POWERS[4 + i // 2]), 5)
        KSP = [(0, 1, 2), (3, 4), (5, 6), (7,), (), ()]
        for k in range(6):
            product(("carry", k), 6 + k % 2)
            if k < 2:
                product(("kt", k), k)
                product(("v", k), 4 + k)
            for j in KSP[k]:
                product(("ks", j), 2 + j % 2)
        for q in range(4):
            product(("cor", q), 6 + q % 2)
        Y_UNIT = {2: -1, 3: 2}

        def y_products(n):
            for c in range(KC):
                product(("y", n, c), 2 + c)

        y_products(0)
        y_products(1)

        for g in UNITS:
            n = block_of(g, "x1t")
            if n is not None:
                for c in range(KC):
                    product(("x1t", n, c), c)
            if live(g, "z1"):
                product(("z1", g - LAG["z1"]), 6 + g % 2)
            for n in (2, 3):
                if g == Y_UNIT[n]:
                    y_products(n)
            for half in range(2):
                if live(g, "sc"):
                    t = g - LAG["sc"]
                    product(("sc", t // TPB, 2 * (t % TPB) + half), 4 + half)
                if half == 1 and live(g, "lg"):
                    product(("lg", g - LAG["lg"]), 1)
                if live(g, "mx"):
                    product(("mx", g - LAG["mx"], half), 2 + half)
                if half == 0 and block_of(g, "nmt") is not None:
                    product(("nmt", block_of(g, "nmt")), 0)
                if half == 0 and live(g, "pv"):
                    product(("pv", g - LAG["pv"]), 7)
            for c in range(KC):
                if block_of(g - c, "q") is not None:
                    product(("q", block_of(g - c, "q"), c), 4 + c)
            if live(g, "att"):
                product(("att", g - LAG["att"]), 0)
            if live(g, "z2"):
                product(("z2", g - LAG["z2"]), 6)
            if live(g, "x2t"):
                product(("x2t", g - LAG["x2t"]), 1)
        product("st", 0)
        for r in range(ROUNDS):
            product(("tot", r), 1 + r % 2)
        product("thr", 3)
        product("pg", 4)
        product("pe", 5)
        product("ids", 6)
        product("idx", 7)
        half_up = FC // 2
        expert_steps = [("gt", 0)] + [("up", 0, f) for f in range(half_up)] + [("gt", 1)]
        expert_steps += [("up", 0, f) for f in range(half_up, FC)]
        for g in range(1, NG):
            expert_steps += [("up", g, f) for f in range(FC)]
            if g + 1 < NG:
                expert_steps.append(("gt", g + 1))
            expert_steps += [("dn", e) for e in range(GS * (g - 1), GS * g)]
        expert_steps += [("dn", e) for e in range(E - GS, E)]
        for step in expert_steps:
            if step[0] == "up":
                product(step, step[2] % 3)
            else:
                for c in range(2):
                    product(step + (c,), (5 if step[0] == "gt" else 3) + c)

        def bank_of(name):
            return bank[turn_of[name][0]]

        def wait_filled(eng, name):
            k, u = turn_of[name]
            eng.wait_ge(filled[k], u + 1)

        def wait_moved(eng, name):
            k, u = turn_of[name]
            eng.wait_ge(moved[k], u + 1)

        def wait_up_low(eng, g):
            eng.wait_ge(wu_lo_pool, min(g + 1, 2))
            if g >= 2:
                eng.wait_ge(wu_lo_dve, g - 1)

        def wait_down_low(eng, e):
            eng.wait_ge(*((wd_lo, e + 1) if e < LOW_BY_DVE else (wd_lo_dve, e + 1 - LOW_BY_DVE)))

        def phase2_over(eng):
            wait_moved(eng, ("lg", NT - 1))

        def sem_filled(name):
            return filled[turn_of[name][0]]

        def sem_moved(name):
            return moved[turn_of[name][0]]

        x_in = [sem(f"x_in{n}") for n in range(NB)]
        ab_in, cd_in, win_in, wg_in, wout_in, wq_in, wo_in = [
            sem(n) for n in ("ab_in", "cd_in", "win_in", "wg_in", "wout_in", "wq_in", "wo_in")]
        b_in_in = sem("b_in_in")
        kv_in, bias1_in, bias2_in = sem("kv_in"), sem("bias1_in"), sem("bias2_in")
        ident_made, pool_consts = sem("ident_made"), sem("pool_consts")
        head_masks, masks_made = sem("head_masks"), sem("masks_made")
        win_zero, mx_made, starts_zero = sem("win_zero"), sem("mx_made"), sem("starts_zero")
        w_hi, w_lo = sem("w_hi"), sem("w_lo")
        xh_made, u_made, xb_added = sem("xh_made"), sem("u_made"), sem("xb_added")
        tw1_made = sem("tw1_made")
        h_start = sem("h_start")
        hu_hi, hu_lo = sem("hu_hi"), sem("hu_lo")
        km_made = sem("km_made")
        wk3_made, ks_hi, ks_made, vb_made, vb_init = [
            sem(n) for n in ("wk3_made", "ks_hi", "ks_made", "vb_made", "vb_init")]
        y_hi, y_lo_dve, y_lo_pool = sem("y_hi"), sem("y_lo_dve"), sem("y_lo_pool")
        ln_stats, ln_var, ln_pool, ln_scale = sem("ln_stats"), sem("ln_var"), sem("ln_pool"), sem("ln_scale")
        ln3_shift, ln1_out, ln2_out = sem("ln3_shift"), sem("ln1_out"), sem("ln2_out")
        ln2_out_dve = sem("ln2_out_dve")
        ln3_out, ln3_out_dve = sem("ln3_out"), sem("ln3_out_dve")
        step_made = sem("step_made")
        x1h_made, q_hi, qs_in = sem("x1h_made"), sem("q_hi"), [sem("qs_in0"), sem("qs_in1")]
        bo_added = sem("bo_added")
        rec_made = sem("rec_made")
        low_digit, sel_in, qm_made, qm_in = \
            sem("low_digit"), sem("sel_in"), sem("qm_made"), [sem("qm_in0"), sem("qm_in1")]
        nm_hi, nm_made = sem("nm_hi"), sem("nm_made")
        ath_made = sem("ath_made")
        lm_made, ex_made, s2_made, routed_made = [
            sem(n) for n in ("lm_made", "ex_made", "s2_made", "routed_made")]
        routed_out, summed_out = sem("routed_out"), sem("summed_out")
        cnt_made, rt_made, prefix_in, slots_made, onehot_made, lh_made, idx_made = [
            sem(n) for n in ("cnt_made", "rt_made", "prefix_in", "slots_made",
                             "onehot_made", "lh_made", "idx_made")]
        gathered = [sem(f"gathered{e}") for e in range(E)]
        scattered = [sem(f"scattered{e}") for e in range(E)]
        wu_in, wd_in = [sem("wu_in0"), sem("wu_in1")], [sem("wd_in0"), sem("wd_in1")]
        wu_hi, wu_lo_pool, wu_lo_dve = sem("wu_hi"), sem("wu_lo_pool"), sem("wu_lo_dve")
        wd_hi, wd_lo, wd_lo_dve = sem("wd_hi"), sem("wd_lo"), sem("wd_lo_dve")
        fth_made = sem("fth_made")
        mh_made, ml_made = sem("mh_made"), sem("ml_made")
        y_in = [sem(f"y_in{q}") for q in range(NT // 2)]
        y_out = sem("y_out")
        dve_step, act_step, pool_step = sem("dve_step"), sem("act_step"), sem("pool_step")

        def chain(eng, s):
            count = [0]

            def link(ins):
                count[0] += 1
                ins.then_inc(s, 1)
                eng.wait_ge(s, count[0])

            return link

        block = es.enter_context(nc.Block())

        def by_tiles(ap):
            return ap.rearrange("(b c j i) d -> i c b j d", b=B, c=CH, i=2)

        @block.sync
        def _(sp):
            xr = by_tiles(x.rearrange("b t d -> (b t) d"))
            for n in range(NB):
                b, j0 = n // 2, (n % 2) * TPB
                for i in range(2):
                    sp.dma_start(X[CH * i:CH * (i + 1), TPB * n:TPB * (n + 1), 0:D],
                                 xr[i, :, b, j0:j0 + TPB, :]).then_inc(x_in[n], 16)
                if n == 0:
                    sp.dma_start(ab_s[0:NS, :], a_mat).then_inc(ab_in, 16)
                    sp.dma_start(ab_s[NS:P, :], b_mat).then_inc(ab_in, 16)
                    sp.dma_start(PW[:, 1, :], a_mat).then_inc(ab_in, 16)
            sp.dma_start(cd_s[:, :, 0:NS], c_mat.rearrange("(c p) n -> p c n", p=P)).then_inc(cd_in, 16)
            sp.dma_start(cd_s[:, :, NS:P], d_mat.rearrange("(c p) n -> p c n", p=P)).then_inc(cd_in, 16)
            sp.dma_start(wg_s[:], w_gate.rearrange("(c p) n -> p c n", p=P)).then_inc(wg_in, 16)
            with nc.allow_non_contiguous_dma(reason="short bias columns"):
                sp.dma_start(b_gate_c[:], b_gate.rearrange("(c p) -> p c", p=P)).then_inc(bias1_in, 16)
                sp.dma_start(b_out_all[:], b_out.rearrange("(a n) -> a n", a=1).to_broadcast([P, D]))\
                    .then_inc(bias1_in, 16)
                sp.dma_start(bq_c[:], bq.rearrange("(c p) -> p c", p=P)).then_inc(bias1_in, 16)
                sp.dma_start(ctx_s[:], ctx.rearrange("b s d -> (b s) d")).then_inc(kv_in, 16)
                sp.dma_start(wk_s[:], wk.rearrange("(c p) n -> p c n", p=P)).then_inc(kv_in, 16)
                sp.dma_start(wv_s[:], wv.rearrange("(c p) n -> p c n", p=P)).then_inc(kv_in, 16)
                sp.dma_start(bk_c[:], bk.rearrange("(c p) -> p c", p=P)).then_inc(kv_in, 16)
                for k in range(3):
                    sp.dma_start(bk3_c[32 * k:32 * k + 32, :], bk.rearrange("(j p) -> p j", p=32))\
                        .then_inc(kv_in, 16)
                sp.dma_start(bv_row[:], bv.rearrange("(a n) -> a n", a=1)).then_inc(kv_in, 16)
            sp.dma_start(wout_s[:], w_out.rearrange("(c p) n -> p c n", p=P)).then_inc(wout_in, 16)
            sp.dma_start(wq_s[:], wq.rearrange("(c p) n -> p c n", p=P)).then_inc(wq_in, 16)
            sp.dma_start(wo_s[:], wo.rearrange("(c p) n -> p c n", p=P)).then_inc(wo_in, 16)
            with nc.allow_non_contiguous_dma(reason="short bias columns"):
                sp.dma_start(bo_all[:], bo.rearrange("(a n) -> a n", a=1).to_broadcast([P, D]))\
                    .then_inc(bias2_in, 16)
                sp.dma_start(br_all[:], br.rearrange("(a n) -> a n", a=1).to_broadcast([P, E]))\
                    .then_inc(bias2_in, 16)
                sp.dma_start(wr_s[:], wr.rearrange("(c p) n -> p c n", p=P)).then_inc(bias2_in, 16)
                full = (FC - 1) * P
                for g in range(NG):
                    sp.dma_start(b_up_c[:, g, 0:FC - 1], b_up[g, 0:full].rearrange("(c p) -> p c", p=P))\
                        .then_inc(bias2_in, 16)
                sp.dma_start(b_up_c[0:FW[-1], :, FC - 1], b_up[:, full:F].rearrange("g p -> p g"))\
                    .then_inc(bias2_in, 16)
            sp.wait_ge(ks_made, 1)
            for b in range(B):
                sp.dma_start(KS[KQ:P, :, b, :].bitcast(F32), SEL[:].bitcast(F32)).then_inc(sel_in, 16)
            for n in range(NB):
                r = n % 2
                wait_moved(sp, ("q", n, 0))
                wait_moved(sp, ("q", n, 1))
                if n >= 2:
                    wait_filled(sp, ("sc", n - 2, PR - 1))
                else:
                    sp.wait_ge(ks_made, 3)
                    sp.wait_ge(km_made, 4)
                    sp.wait_ge(w_lo, 5)
                for q in range(PR // KC):
                    for k, src in enumerate((QH, QH, QL)):
                        sp.dma_start(QS[32 * k:32 * k + 32, r].rearrange("p (c q) n -> p c q n", c=KC)[:, :, q, :].bitcast(F32),
                                     src[32 * q:32 * q + 32, r].bitcast(F32)).then_inc(qs_in[r], 16)
                wait_moved(sp, ("nmt", n))
                if n >= 2:
                    wait_filled(sp, ("sc", n - 2, PR - 1))
                sp.dma_start(QS[KQ:P, r, QM_BY_ACT:PR, :].bitcast(F32),
                             NMT[0:32, r:r + 1, :].to_broadcast([32, PR - QM_BY_ACT, BLK]).bitcast(F32))\
                    .then_inc(qm_in[r], 16)
            phase2_over(sp)

            def load_up(g):
                if g >= 2:
                    sp.wait_ge(wu_hi, g - 1)
                    wait_up_low(sp, g - 2)
                sp.dma_start(WUR[:, g % 2], w_up[g].rearrange("(c p) f -> p c f", p=P))\
                    .then_inc(wu_in[g % 2], 16)

            def load_down(e):
                if e >= 2:
                    sp.wait_ge(wd_hi, e - 1)
                    wait_down_low(sp, e - 2)
                full = (FC - 1) * P
                sp.dma_start(WDR[:, e % 2, 0:FC - 1, :],
                             w_down[e, 0:full, :].rearrange("(c p) n -> p c n", p=P))\
                    .then_inc(wd_in[e % 2], 16)
                sp.dma_start(WDR[0:FW[-1], e % 2, FC - 1, :], w_down[e, full:F, :])\
                    .then_inc(wd_in[e % 2], 16)
                sp.dma_start(BDR[:, e % 2, :], b_down[e:e + 1, :]).then_inc(wd_in[e % 2], 16)

            load_up(0)
            load_down(0)
            load_down(1)
            load_up(1)
            for i in range(2):
                for b in range(B):
                    sp.dma_start(by_tiles(summed)[i, :, b],
                                 X[CH * i:CH * (i + 1), NT // B * b:NT // B * (b + 1), 0:D])\
                        .then_inc(summed_out, 16)
            sp.wait_ge(routed_made, 1)
            for i in range(2):
                for b in range(B):
                    sp.dma_start(by_tiles(routed)[i, :, b],
                                 X[CH * i:CH * (i + 1), NT // B * b:NT // B * (b + 1), :])\
                        .then_inc(routed_out, 16)
            load_down(2)
            for g in range(2, NG):
                load_up(g)
                load_down(2 * g - 1)
                load_down(2 * g)
            load_down(E - 1)
            for e in range(E):
                sp.wait_ge(scattered[e], 32)
            ys = summed.rearrange("(p i) d -> p i d", p=P)
            for q in range(NT // 2):
                sp.dma_start(Y[:, 2 * q:2 * q + 2, :], ys[:, 2 * q:2 * q + 2, :]).then_inc(y_in[q], 16)
            os_ = out.rearrange("b t d -> (b t) d").rearrange("(p i) d -> p i d", p=P)
            for q in range(NT // 2):
                sp.wait_ge(ln3_out, 3 * (q // 2) + 2 if q % 2 == 0 else 3 * (q // 2) + 3)
                if q % 2:
                    sp.wait_ge(ln3_out_dve, q // 2 + 1)
                sp.dma_start(os_[:, 2 * q:2 * q + 2, :], Y[:, 2 * q:2 * q + 2, :]).then_inc(y_out, 16)
            sp.wait_ge(y_out, 8 * NT)
            sp.wait_ge(summed_out, 64)
            sp.wait_ge(routed_out, 64)

        @block.gpsimd
        def _(pool):
            link = chain(pool, pool_step)
            link(pool.memset(ident[:], 0.0))
            pool.affine_select(out=ident[:], in_=ident[:], compare_op=ALU.not_equal, fill=1.0,
                               base=0, pattern=[[-1, P]], channel_multiplier=1).then_inc(ident_made, 1)
            pool.memset(win_s[:, :, 0:NS], 0.0).then_inc(win_zero, 1)
            pool.wait_ge(win_zero, 1)
            link(pool.memset(mx_s[NS:P, 0:NS], 0.0))
            pool.wait_ge(ident_made, 1)
            pool.tensor_copy(mx_s[NS:P, NS:P], ident[NS:P, NS:P]).then_inc(mx_made, 1)
            pool.wait_ge(mx_made, 1)
            link(pool.memset(HU[0:NS, :].rearrange("p (b i c) -> p b i c", b=B, i=L)[:, :, 0, :], 0.0))
            pool.memset(HS[:, :, 0:1], 0.0).then_inc(starts_zero, 1)
            pool.wait_ge(starts_zero, 1)
            link(pool.memset(neg_half[:], -0.5))
            link(pool.iota(pidx[:], pattern=[[0, 1]], base=0, channel_multiplier=1))
            link(pool.iota(col_i[:], pattern=[[1, P]], base=0, channel_multiplier=0))
            link(pool.iota(tok_i[:], pattern=[[0, B], [2, NT // B]], base=0, channel_multiplier=0))
            for j in range(4):
                link(pool.memset(steps[:, 0, j:j + 1], (j + 1) % 4 << 28))
            link(pool.memset(reset_g[:], 1.0))
            link(pool.memset(reset_g[:, :, 0:1], 0.0))
            link(pool.memset(reset_e[:], 1.0))
            link(pool.memset(reset_e[:, :, 0:1], 0.0))
            link(pool.memset(ones_b[:], 1.0))
            link(pool.memset(ones_r[:].bitcast(F32), 1.0))
            pool.memset(ones_f[:], 1.0).then_inc(pool_consts, 1)
            pool.wait_ge(pool_consts, 1)
            pool.memset(VB[:], 0.0).then_inc(vb_init, 1)
            pool.wait_ge(vb_init, 1)
            link(pool.memset(VB[0:SE, :, :, 0, DK:DK + 1], 1.0))
            pool.memset(VB[SE:P, :, :, 1, DK:DK + 1], 1.0).then_inc(vb_init, 1)
            pool.wait_ge(vb_init, 2)
            pool.wait_ge(bias1_in, 16 * 3)
            for n in range(NB):
                wait_filled(pool, ("xt", n, KC - 1))
                xs = X[:, TPB * n:TPB * (n + 1), 0:D]
                pool.tensor_tensor(xs, xs, b_out_all[:].unsqueeze(1).to_broadcast([P, TPB, D]), ALU.add)\
                    .then_inc(xb_added, 1)
            link(pool.memset(sel_s[:], 0.0))
            for base in (0, -2):
                link(pool.affine_select(out=sel_s[:], in_=sel_s[:], compare_op=ALU.not_equal, fill=1.0, base=base,
                                        pattern=[[-4, PR], [-1, 2], [0, SE]], channel_multiplier=1))
            pool.tensor_copy(SEL[:], sel_s[:].rearrange("p j h k -> p j (h k)")).then_inc(ks_made, 1)
            pool.wait_ge(ks_made, 1)
            pool.wait_ge(head_masks, 1)
            for c in range(KC):
                wait_moved(pool, ("kt", c))
                for b in range(B):
                    pool.tensor_tensor(
                        KM[:, b, c], kt_s[:, c, b * SE:(b + 1) * SE].unsqueeze(1).to_broadcast([P, HD // KC, SE]),
                        mask_hi3[:].unsqueeze(2).to_broadcast([P, HD // KC, SE]), ALU.mult).then_inc(km_made, 1)

            def gated_low(n):
                for c in range(KC):
                    pool.wait_ge(y_hi, KC * n + c + 1)
                    pool.tensor_tensor(YL[:, n, c], G[:, n, c], YH[:, n, c].bitcast(F32), ALU.subtract)\
                        .then_inc(y_lo_pool, 1)

            scaled = [0]

            pool.wait_ge(km_made, 4)
            for part in range(2):
                js = slice(part * PR // 2, (part + 1) * PR // 2)
                pool.wait_ge(ks_hi, part + 1)
                pool.tensor_tensor(KS[32:64, js], ksf_s[32:64, js].rearrange("p j b h k -> p j b (h k)"),
                                   KS[32:64, js].bitcast(F32), ALU.subtract).then_inc(ks_made, 1)
                pool.wait_ge(ks_made, part + 2)
            gated_low(1)

            def scale(k, width=1, shifted=True):
                at = slice(k, k + width)
                pool.wait_ge(ln_var, k + width)
                link(pool.tensor_scalar(var_eps[:, at].unsqueeze(2), mean_var[:, at, 1:2], EPS, None, ALU.add))
                pool.tensor_tensor(rstd[:, at], var_eps[:, at], neg_half[:, 0:width], ALU.pow).then_inc(ln_pool, 1)
                scaled[0] += 1
                pool.wait_ge(ln_pool, scaled[0])
                if shifted:
                    pool.tensor_scalar(shift[:, k:k + 1], mean_var[:, k, 0:1], rstd[:, k:k + 1], -1.0,
                                       ALU.mult, ALU.mult).then_inc(ln_scale, 1)

            for g in UNITS:
                n = block_of(g, "x1t")
                if live(g, "z1"):
                    scale(norm_at[1, g - LAG["z1"]])
                for m in (2, 3):
                    if g == Y_UNIT[m]:
                        gated_low(m)
                if n is not None:
                    if n == 0:
                        pool.wait_ge(bias2_in, 16 * (4 + NG))
                    wait_filled(pool, ("x1t", n, KC - 1))
                    xs = X[:, TPB * n:TPB * (n + 1), 0:D]
                    pool.tensor_tensor(xs, xs, bo_all[:].unsqueeze(1).to_broadcast([P, TPB, D]), ALU.add)\
                        .then_inc(bo_added, 1)
                if live(g, "z2"):
                    t = g - LAG["z2"]
                    k = norm_at[2, t]
                    scale(k, shifted=False)
                    if t < BY_POOL:
                        pool.tensor_scalar(X[:, t, 0:D], X[:, t, 0:D], mean_var[:, k, 0:1], rstd[:, k:k + 1],
                                           ALU.subtract, ALU.mult).then_inc(ln2_out, 1)
            phase2_over(pool)

            def up_low(g):
                pool.wait_ge(wu_hi, g + 1)
                pool.tensor_tensor(WUL[:, g % 2], WUR[:, g % 2], WUH[:, g % 2].bitcast(F32), ALU.subtract)\
                    .then_inc(wu_lo_pool, 1)

            def down_low(e):
                pool.wait_ge(wd_hi, e + 1)
                if e >= 3:
                    wait_filled(pool, ("dn", e - 3, 1))
                pool.tensor_tensor(WDL[:, e % 3, 0:FC - 1], WDR[:, e % 2, 0:FC - 1],
                                   WDH[:, e % 3, 0:FC - 1].bitcast(F32), ALU.subtract)
                f = FW[-1]
                pool.tensor_tensor(WDL[0:f, e % 3, FC - 1], WDR[0:f, e % 2, FC - 1],
                                   WDH[0:f, e % 3, FC - 1].bitcast(F32), ALU.subtract)
                pool.tensor_tensor(BDL[:, e % 3], BDR[:, e % 2], BDH[:, e % 3].bitcast(F32), ALU.subtract)\
                    .then_inc(wd_lo, 1)

            up_low(0)
            down_low(0)
            down_low(1)
            up_low(1)
            pool.wait_ge(idx_made, 1)
            pool.wait_ge(routed_out, 64)
            pool.wait_ge(summed_out, 64)
            for s in range(NT):
                pool.indirect_dma_start(
                    XG[:, s, :], None, routed,
                    bass.IndirectOffsetOnAxis(ap=idx[:, s:s + 1].bitcast(U32), axis=0)).then_inc(gathered[s // 2], 16)
            down_low(2)

            for e in range(E):
                if e:
                    pool.wait_ge(scattered[e - 1], 32)
                for h in range(2):
                    wait_moved(pool, ("dn", e, h))
                    pool.indirect_dma_start(
                        summed, bass.IndirectOffsetOnAxis(ap=idx[:, 2 * e + h:2 * e + h + 1].bitcast(U32), axis=0),
                        OUT[:, (2 * e + h) % 4, :], None, compute_op=ALU.add).then_inc(scattered[e], 16)
                if e + 3 < LOW_BY_DVE:
                    down_low(e + 3)
            for q in range(NT // 4):
                scale(2 * NT + 4 * q, 4, shifted=False)

        @block.scalar
        def _(act):
            link = chain(act, act_step)
            with nc.allow_non_contiguous_dma(reason="short bias columns"):
                act.wait_ge(win_zero, 1)
                act.dma_start(win_s[:, :, NS:P], w_in.rearrange("(c p) n -> p c n", p=P)).then_inc(win_in, 16)
                act.dma_start(b_in_c[NS:P, :], b_in.rearrange("(p a) -> p a", a=1)).then_inc(b_in_in, 16)

            def whole(w, src, arrived):
                act.wait_ge(arrived, 16)
                act.activation(w[0][:], src[:], ACT.Copy).then_inc(w_hi, 1)

            whole(WIN, win_s, win_in)
            def x_high(n):
                for c in range(KC):
                    wait_filled(act, ("xt", n, c))
                    act.activation(XH[:, n, c], bank_of(("xt", n, c))[:], ACT.Copy).then_inc(xh_made, 1)

            x_high(0)
            for n in range(NB):
                if n + 1 < NB:
                    x_high(n + 1)
                if n == 0:
                    act.wait_ge(b_in_in, 16)
                wait_filled(act, ("u", n))
                act.activation(HU[NS:P, n * BLK:(n + 1) * BLK], bank_of(("u", n))[NS:P, :], ACT.Identity,
                               bias=b_in_c[NS:P, :]).then_inc(sem_moved(("u", n)), 1)
                m = POWERS[n]
                wait_filled(act, ("tw", m))
                act.activation(TW[:, n + 1, :], bank[5][0:NS, 0:NS], ACT.Copy).then_inc(moved[5], 1)
                if n == 1:
                    whole(WG, wg_s, wg_in)
            whole(WOUT, wout_s, wout_in)
            whole(WQ, wq_s, wq_in)
            whole(WO, wo_s, wo_in)
            wait_filled(act, "w1")
            act.activation(W1[0][:], bank[7][:, 0:D], ACT.Copy).then_inc(w_hi, 1)
            for i in range(L):
                if i % 2 == 1 and 4 + i // 2 < 9:
                    m = POWERS[4 + i // 2]
                    if m < 256:
                        wait_filled(act, ("tw", m))
                        act.activation(TW[:, 5 + i // 2, :], bank[5][0:NS, 0:NS], ACT.Copy).then_inc(moved[5], 1)
                if i == 0:
                    act.wait_ge(bias1_in, 16 * 3)
                if i % 2 == 1:
                    g = i // 2
                    n, c = g // 2, g % 2
                    wait_filled(act, ("gate", g))
                    act.activation(G[:, n, c], bank_of(("gate", g))[:], ACT.Sigmoid,
                                   bias=b_gate_c[:, c:c + 1]).then_inc(sem_moved(("gate", g)), 1)
            act.wait_ge(kv_in, 128)
            act.wait_ge(head_masks, 2)
            for k in range(len(LEVELS)):
                if k < KC:
                    wait_filled(act, ("kt", k))
                    act.activation(kt_s[:, k], bank[k][:, 0:B * SE], ACT.Identity, bias=bk_c[:, k:k + 1])\
                        .then_inc(moved[k], 1)
                for j in KSP[k]:
                    wait_filled(act, ("ks", j))
                    got = bank_of(("ks", j))[0:KQ, 0:B * SE].rearrange("p (b s) -> p b s", b=B)
                    for h in range(2):
                        last = act.activation(ksf_s[0:KQ, j, :, h, :], got, ACT.Identity,
                                              bias=bk3h[0:KQ, h, j:j + 1], scale=half_mask[0:KQ, h:h + 1])
                    last.then_inc(sem_moved(("ks", j)), 1)
                if k in (1, 3):
                    js = slice(k // 2 * PR // 2, (k // 2 + 1) * PR // 2)
                    wait_moved(act, ("ks", js.stop - 1))
                    wait_moved(act, ("ks", js.stop - 2))
                    act.activation(KS[0:KQ, js], ksf_s[0:KQ, js].rearrange("p j b h k -> p j b (h k)"), ACT.Copy)\
                        .then_inc(ks_hi, 1)
            for n in range(NB):
                act.wait_ge(h_start, 1)
                wait_moved(act, ("cor", 1 + 2 * (n % 2)))
                wait_moved(act, ("cor", 2 * (n % 2)))
                act.activation(HUH[:, n * BLK:(n + 1) * BLK], HU[:, n * BLK:(n + 1) * BLK], ACT.Copy)\
                    .then_inc(hu_hi, 1)

            def gated_high(n):
                for c in range(KC):
                    wait_moved(act, ("y", n, c))
                    act.activation(YH[:, n, c], G[:, n, c], ACT.Copy).then_inc(y_hi, 1)

            gated_high(0)
            gated_high(1)

            def normalise(which, t):
                k = norm_at[which, t]
                act.wait_ge(*((ln_scale, t + 1) if which == 1 else (ln3_shift, t // 4 + 1)))
                r = Y[:, t, :] if which == 3 else X[:, t, 0:D]
                act.activation(r, r, ACT.Identity, bias=shift[:, k:k + 1], scale=rstd[:, k:k + 1])\
                    .then_inc(ln1_out if which == 1 else ln3_out, 1)

            def exps(m, j):
                if j == 0 and m == 0:
                    act.wait_ge(ks_made, 3)
                    act.wait_ge(km_made, 4)
                if j == 0 and m >= 2:
                    wait_filled(act, ("pv", TPB * (m - 1) - 1))
                wait_filled(act, ("sc", m, j))
                act.activation(PT[m % 2][:, j, :], bank_of(("sc", m, j))[:], ACT.Exp, scale=SCALE)\
                    .then_inc(sem_moved(("sc", m, j)), 1)

            for g in UNITS:
                n = block_of(g, "x1t")
                if n is not None:
                    r = n % 2
                    for c in range(KC):
                        wait_filled(act, ("x1t", n, c))
                        if n < 2:
                            act.wait_ge(y_hi, 4 * n + 4)
                            act.wait_ge(y_lo_dve, KC)
                            act.wait_ge(y_lo_pool, KC * (2 * n + 1))
                        else:
                            wait_filled(act, ("q", n - 2, KC - 1))
                        act.activation(X1H[r][:, c], bank[c][:], ACT.Copy).then_inc(x1h_made, 1)
                if live(g - 1, "z1"):
                    normalise(1, g - 1 - LAG["z1"])
                for n in (2, 3):
                    if g == Y_UNIT[n]:
                        gated_high(n)
                for half in range(2):
                    if live(g, "sc"):
                        t = g - LAG["sc"]
                        exps(t // TPB, 2 * (t % TPB) + half)
                    if half == 0 and block_of(g, "nmt") is not None:
                        n = block_of(g, "nmt")
                        wait_filled(act, ("nmt", n))
                        if n >= 2:
                            act.wait_ge(qm_in[n % 2], 16 * (n // 2))
                        act.activation(NMT[0:32, n % 2, :], bank[0][0:32, :], ACT.Copy).then_inc(moved[0], 1)
                        wait_moved(act, ("nmt", n))
                        if n == 0:
                            act.wait_ge(ks_made, 3)
                            act.wait_ge(km_made, 4)
                            act.wait_ge(w_lo, 5)
                        elif n >= 2:
                            wait_filled(act, ("sc", n - 2, QM_BY_ACT - 1))
                        for j in range(QM_BY_ACT):
                            act.activation(QS[KQ:P, n % 2, j, :], NMT[0:32, n % 2, :].bitcast(F32), ACT.Copy)\
                                .then_inc(qm_made, 1)
                for c in range(KC):
                    n = block_of(g - c, "q")
                    if n is not None:
                        wait_filled(act, ("q", n, c))
                        wait_filled(act, ("z1", TPB * (n % 2) + TPB - 1))
                        if n >= 2:
                            wait_filled(act, ("mx", TPB * (n - 1) - 1, KC - 1))
                            act.wait_ge(qs_in[n % 2], 16 * 3 * 4 * (n // 2))
                        act.activation(QH[:, n % 2, c], bank_of(("q", n, c))[:], ACT.Identity,
                                       bias=bq_c[:, c:c + 1]).then_inc(q_hi, 1)
                if live(g, "att"):
                    t = g - LAG["att"]
                    wait_filled(act, ("att", t))
                    if t >= 2:
                        wait_filled(act, ("z2", t - 2))
                    act.activation(ATH[:, t % 2], bank_of(("att", t))[:, 0:D], ACT.Copy).then_inc(ath_made, 1)
                if live(g, "x2t"):
                    t = g - LAG["x2t"]
                    wait_filled(act, ("x2t", t))
                    if t >= 2:
                        wait_filled(act, ("lg", t - 2))
                    act.activation(X2T[:, t % 2, :], bank_of(("x2t", t))[:, 0:D], ACT.Copy)\
                        .then_inc(sem_moved(("x2t", t)), 1)
            act.wait_ge(lm_made, 1)
            act.activation(ex[:], lm[:], ACT.Exp).then_inc(ex_made, 1)
            act.activation(step_b[:], step_f[:].unsqueeze(2).to_broadcast([P, NT, P]), ACT.Identity,
                           bias=pf[:, 5:6]).then_inc(step_made, 1)
            act.wait_ge(s2_made, 1)
            act.activation(X[:, :, D:RW], S2[:], ACT.Copy).then_inc(routed_made, 1)

            def down_high(e):
                act.wait_ge(wd_in[e % 2], 48 * (e // 2 + 1))
                if e >= 3:
                    wait_filled(act, ("dn", e - 3, 1))
                act.activation(WDH[:, e % 3, 0:FC - 1], WDR[:, e % 2, 0:FC - 1], ACT.Copy)
                f = FW[-1]
                act.activation(WDH[0:f, e % 3, FC - 1], WDR[0:f, e % 2, FC - 1], ACT.Copy)
                act.activation(BDH[:, e % 3], BDR[:, e % 2], ACT.Copy).then_inc(wd_hi, 1)

            def up_high(g):
                act.wait_ge(wu_in[g % 2], 16 * (g // 2 + 1))
                if g >= 2:
                    wait_filled(act, ("up", g - 2, FC - 1))
                act.activation(WUH[:, g % 2], WUR[:, g % 2], ACT.Copy).then_inc(wu_hi, 1)

            up_high(0)
            down_high(0)
            down_high(1)
            up_high(1)
            down_high(2)
            act.activation(warm[:], half_mask[:, 0:1], ACT.Silu)
            splits = {("up", 2, 0): 3, ("up", 2, 3): 4, ("up", 3, 0): 5, ("up", 3, 3): 6, ("dn", E - 3): 7}
            for step in expert_steps:
                g = step[1]
                if step[0] == "gt":
                    for c in range(KC):
                        wait_filled(act, ("gt", g, c))
                        if g >= 2:
                            wait_filled(act, ("up", g - 2, FC - 1))
                        act.activation(FTH[:, g % 2, c], bank[5 + c][:], ACT.Copy).then_inc(fth_made, 1)
                if step[0] == "up":
                    f = step[2]
                    wait_filled(act, step)
                    q = g * FC + f
                    if q >= 3:
                        act.wait_ge(ml_made, q - 2)
                    act.activation(MF[0:FW[f], q % 3], bank[f % 3][0:FW[f], :], ACT.Silu,
                                   bias=b_up_c[0:FW[f], g, f:f + 1]).then_inc(moved[f % 3], 1)
                    if f == 1 and 2 <= g + 1 < NG:
                        up_high(g + 1)
                if step in splits:
                    down_high(splits[step])
            for t in range(NT):
                if t % 4 < 3:
                    normalise(3, t)

        @block.tensor
        def _(pe):
            order = [0] * 8

            def turn(name):
                k, u = turn_of[name]
                assert order[k] == u, name
                order[k] += 1
                if u:
                    pe.wait_ge(moved[k], u)
                return bank[k]

            def split_matmuls(o, pairs):
                last, n = None, 0
                for (ah, al), (bh, bl) in pairs:
                    for a, b in ((ah, bh), (ah, bl), (al, bh)):
                        last = pe.matmul(o, a, b, start=(n == 0), stop=(n == 3 * len(pairs) - 1))
                        n += 1
                return last

            def both(w, *at):
                return tuple(x[at] for x in w)

            ALLP = slice(None)
            def power(m):
                l = POWERS.index(m)
                o = turn(("pw", m))
                width = m if m <= 8 else 1
                pe.wait_ge(tw1_made, 1)
                if m > 1:
                    wait_moved(pe, ("tw", m // 2))
                    wait_moved(pe, ("pw", m // 2))
                rhs = PW[:, 1:m + 1, :] if m <= 8 else (PW[:, 16, :] if m == 16 else PB[:, l - 5, :])
                own = PW[:, m, :] if m <= 16 else PB[:, l - 5, :]
                pe.matmul(o[0:NS, 0:width * NS], TW[:, l, :], rhs, start=True, stop=True).then_inc(filled[4], 1)
                if m < 256:
                    o = turn(("tw", m))
                    pe.matmul(o[0:NS, 0:NS], own, TW[:, l, :], start=True, stop=True).then_inc(filled[5], 1)

            def x_transposed(n):
                pe.wait_ge(x_in[n], 32)
                for c in range(KC):
                    o = turn(("xt", n, c))
                    for s in range(TPB):
                        last = pe.transpose(o[:, s * P:(s + 1) * P], X[:, TPB * n + s, c * P:(c + 1) * P], ident[:])
                    last.then_inc(sem_filled(("xt", n, c)), 1)

            pe.wait_ge(ident_made, 1)
            x_transposed(0)
            pe.wait_ge(ab_in, 48)
            o = turn("ab")
            pe.transpose(o[0:NS, 0:P], ab_s[:, :], ident[:]).then_inc(filled[6], 1)
            for n in range(NB):
                if n + 1 < NB:
                    x_transposed(n + 1)
                if n == 0:
                    pe.wait_ge(w_hi, 1)
                    pe.wait_ge(w_lo, 1)
                o = turn(("u", n))
                wait_moved(pe, ("xt", n, 0))
                wait_moved(pe, ("xt", n, 1))
                split_matmuls(o[:, :], [
                    (both(WIN, ALLP, c, ALLP), (XH[:, n, c], XL[:, n, c])) for c in range(KC)
                ]).then_inc(sem_filled(("u", n)), 1)
                power(POWERS[n])
            pe.wait_ge(cd_in, 32)
            o = turn("cd")
            for c in range(KC):
                last = pe.transpose(o[:, c * P:(c + 1) * P], cd_s[:, c, :], ident[:])
            last.then_inc(filled[0], 1)
            pe.wait_ge(kv_in, 128)
            o = turn("ctx")
            for c in range(KC):
                last = pe.transpose(o[:, c * P:(c + 1) * P], ctx_s[:, c * P:(c + 1) * P], ident[:])
            last.then_inc(filled[1], 1)
            o = turn("w1")
            wait_moved(pe, "cd")
            pe.wait_ge(mx_made, 1)
            pe.matmul(o[:, 0:D], mx_s[:], cdt_s[:], start=True, stop=True).then_inc(filled[7], 1)

            hu4 = HU[:].rearrange("p (b i c) -> p b i c", b=B, i=L)
            for n in range(NB):
                wait_moved(pe, ("u", n))
            pe.wait_ge(w_hi, 2)
            pe.wait_ge(w_lo, 2)
            pe.wait_ge(starts_zero, 1)
            gate_bank = None
            for i in range(L):
                o = turn(("step", i))
                if i:
                    wait_moved(pe, ("step", i - 1))
                pe.matmul(o[0:NS, 0:B * CH], ab_s[:], hu4[:, :, i, :], start=True, stop=True)\
                    .then_inc(sem_filled(("step", i)), 1)
                g = i // 2
                n, m = g // 2, g % 2
                if i % 2 == 0:
                    gate_bank = turn(("gate", g))
                k = 0
                for c in range(KC):
                    for a, b in ((0, 0), (0, 1), (1, 0)):
                        if k // 3 == i % 2:
                            last = pe.matmul(gate_bank[:, :], WG[a][:, c, m * P:(m + 1) * P], (XH, XL)[b][:, n, c],
                                             start=(k == 0), stop=(k == 5))
                        k += 1
                if i % 2 == 1:
                    last.then_inc(sem_filled(("gate", g)), 1)
                    if 4 + i // 2 < 9:
                        power(POWERS[4 + i // 2])
            pe.wait_ge(wk3_made, 1)
            for k, d in enumerate(LEVELS):
                o = turn(("carry", k))
                if k:
                    wait_moved(pe, ("carry", k - 1))
                else:
                    wait_moved(pe, ("step", L - 1))
                    wait_moved(pe, ("pw", 256))
                own = PW[:, 16, :] if k == 0 else PB[:, k - 1, :]
                pe.matmul(o[0:NS, 0:B * (CH - d)], own, HS[:, :, 1:1 + CH - d], start=True, stop=True)\
                    .then_inc(sem_filled(("carry", k)), 1)
                if k < 2:
                    o = turn(("kt", k))
                    wait_moved(pe, "ctx")
                    for c in range(KC):
                        last = pe.matmul(o[:, 0:B * SE], wk_s[:, c, k * P:(k + 1) * P], ctd_s[:, c, :, 0, :],
                                         start=(c == 0), stop=(c == KC - 1))
                    last.then_inc(filled[k], 1)
                    o = turn(("v", k))
                    for c in range(KC):
                        pe.matmul(o[:, 0:D], ctd_s[:, c, k].rearrange("p r s -> p (r s)"), wv_s[:, c, :],
                                  start=(c == 0), stop=False)
                    pe.matmul(o[:, 0:D], ones_f[0:1, :], bv_row[:], start=False, stop=True)\
                        .then_inc(filled[4 + k], 1)
                for j in KSP[k]:
                    o = turn(("ks", j))
                    for c in range(KC):
                        last = pe.matmul(o[0:KQ, 0:B * SE], wk3_s[:, c * PR + j].rearrange("p r s -> p (r s)"),
                                         ctd_s[:, c, :, 0, :], start=(c == 0), stop=(c == KC - 1))
                    last.then_inc(sem_filled(("ks", j)), 1)
            wait_moved(pe, ("carry", 5))
            for q in range(4):
                o = turn(("cor", q))
                for i in range(4 * q, 4 * q + 4):
                    if i:
                        last = pe.matmul(o[0:NS, (i % 4) * P:(i % 4 + 1) * P], PW[:, i, :], HS[:, :, 0:CH],
                                         start=True, stop=True)
                last.then_inc(sem_filled(("cor", q)), 1)
            wait_moved(pe, "w1")
            pe.wait_ge(w_lo, 5)

            def state_output(n):
                pe.wait_ge(hu_lo, n + 1)
                for c in range(KC):
                    o = turn(("y", n, c))
                    cols = slice(n * BLK, (n + 1) * BLK)
                    split_matmuls(o[:, :], [(both(W1, ALLP, slice(c * P, (c + 1) * P)), (HUH[:, cols], HUL[:, cols]))])\
                        .then_inc(filled[2 + c], 1)

            state_output(0)
            state_output(1)

            def mixer_out(t):
                n, s = t // TPB, t % TPB
                if s == 0:
                    pe.wait_ge(y_hi, KC * (n + 1))
                    if n == 0:
                        pe.wait_ge(y_lo_dve, KC)
                    else:
                        pe.wait_ge(y_lo_pool, KC * n)
                o = turn(("z1", t))
                cols = slice(s * P, (s + 1) * P)
                split_matmuls(o[:, 0:D], [
                    ((YH[:, n, c, cols], YL[:, n, c, cols]), both(WOUT, ALLP, c, ALLP)) for c in range(KC)
                ]).then_inc(sem_filled(("z1", t)), 1)

            def transposed(n):
                pe.wait_ge(ln1_out, TPB * (n + 1))
                for c in range(KC):
                    o = turn(("x1t", n, c))
                    for s in range(TPB):
                        last = pe.transpose(o[:, s * P:(s + 1) * P], X[:, TPB * n + s, c * P:(c + 1) * P], ident[:])
                    last.then_inc(filled[c], 1)

            def queries(n, c):
                o = turn(("q", n, c))
                wait_moved(pe, ("x1t", n, 0))
                wait_moved(pe, ("x1t", n, 1))
                split_matmuls(o[:, :], [
                    (both(WQ, ALLP, k, slice(c * P, (c + 1) * P)), (X1H[n % 2][:, k], X1L[n % 2][:, k]))
                    for k in range(KC)
                ]).then_inc(sem_filled(("q", n, c)), 1)

            def high_scores(t, c):
                n, s = t // TPB, t % TPB
                if t == 0:
                    pe.wait_ge(km_made, 4)
                if s == 0:
                    wait_moved(pe, ("q", n, 0))
                    wait_moved(pe, ("q", n, 1))
                o = turn(("mx", t, c))
                pe.matmul(o[:, :], QH[:, n % 2, c, s * P:(s + 1) * P],
                          KM[:, n // 2, c].rearrange("p h k -> p (h k)"), start=True, stop=True)\
                    .then_inc(sem_filled(("mx", t, c)), 1)

            def maxima_transposed(n):
                pe.wait_ge(nm_made, TPB * (n + 1))
                o = turn(("nmt", n))
                for s in range(TPB):
                    last = pe.transpose(o[0:32, s * P:(s + 1) * P],
                                        NMS[:, n % 2, s].rearrange("p j l h -> p (j l h)").bitcast(F32), ident[:])
                last.then_inc(filled[0], 1)

            def scores(m, j):
                r = m % 2
                if j == 0:
                    pe.wait_ge(ks_made, 3)
                    pe.wait_ge(sel_in, 16 * B)
                    pe.wait_ge(qs_in[r], 16 * 3 * 4 * (m // 2 + 1))
                if j < QM_BY_ACT:
                    pe.wait_ge(qm_made, QM_BY_ACT * m + j + 1)
                else:
                    pe.wait_ge(qm_in[r], 16 * (m // 2 + 1))
                o = turn(("sc", m, j))
                pe.matmul(o[:, :], KS[:, j, m // 2, :], QS[:, r, j, :], start=True, stop=True)\
                    .then_inc(sem_filled(("sc", m, j)), 1)

            def weighted(t, half):
                m, s = t // TPB, t % TPB
                o = turn(("pv", t)) if half == 0 else bank_of(("pv", t))
                if t == 0 and half == 0:
                    pe.wait_ge(vb_made, 2)
                    wait_moved(pe, ("v", 1))
                for j in range(4 * half, 4 * half + 4):
                    if s == 0:
                        wait_moved(pe, ("sc", m, j))
                    last = pe.matmul(o[:, j * 34:(j + 1) * 34], PT[m % 2][:, j, s * P:(s + 1) * P],
                                     VB[:, m // 2, j].rearrange("p h d -> p (h d)"), start=True, stop=True)
                if half == 1:
                    last.then_inc(sem_filled(("pv", t)), 1)

            def attention_transposed(t):
                wait_moved(pe, ("pv", t))
                o = turn(("att", t))
                for c in range(KC):
                    last = pe.transpose(o[:, c * P:(c + 1) * P], ATT[:, t % TPB, c * P:(c + 1) * P], ident[:])
                last.then_inc(sem_filled(("att", t)), 1)

            def attention_out(t):
                o = turn(("z2", t))
                wait_moved(pe, ("att", t))
                split_matmuls(o[:, 0:D], [
                    ((ATH[:, t % 2, c], ATL[:, t % 2, c]), both(WO, ALLP, c, ALLP)) for c in range(KC)
                ]).then_inc(sem_filled(("z2", t)), 1)

            def x2_transposed(t):
                pe.wait_ge(*((ln2_out, t + 1) if t < BY_POOL else (ln2_out_dve, t - BY_POOL + 1)))
                o = turn(("x2t", t))
                for c in range(KC):
                    last = pe.transpose(o[:, c * P:(c + 1) * P], X[:, t, c * P:(c + 1) * P], ident[:])
                last.then_inc(sem_filled(("x2t", t)), 1)

            def logits(t):
                if t == 0:
                    pe.wait_ge(bias2_in, 16 * (4 + NG))
                o = turn(("lg", t))
                wait_moved(pe, ("x2t", t))
                for c in range(KC):
                    last = pe.matmul(o[:, 0:E], X2T[:, t % 2, c * P:(c + 1) * P], wr_s[:, c, :],
                                     start=(c == 0), stop=(c == KC - 1))
                last.then_inc(sem_filled(("lg", t)), 1)

            for g in UNITS:
                if block_of(g, "x1t") is not None:
                    transposed(block_of(g, "x1t"))
                if live(g, "z1"):
                    mixer_out(g - LAG["z1"])
                for n in (2, 3):
                    if g == Y_UNIT[n]:
                        state_output(n)
                for half in range(2):
                    if live(g, "sc"):
                        t = g - LAG["sc"]
                        scores(t // TPB, 2 * (t % TPB) + half)
                    if half == 1 and live(g, "lg"):
                        logits(g - LAG["lg"])
                    if live(g, "mx"):
                        high_scores(g - LAG["mx"], half)
                    if half == 0 and block_of(g, "nmt") is not None:
                        maxima_transposed(block_of(g, "nmt"))
                    if live(g, "pv"):
                        weighted(g - LAG["pv"], half)
                for c in range(KC):
                    if block_of(g - c, "q") is not None:
                        queries(block_of(g - c, "q"), c)
                if live(g, "att"):
                    attention_transposed(g - LAG["att"])
                if live(g, "z2"):
                    attention_out(g - LAG["z2"])
                if live(g, "x2t"):
                    x2_transposed(g - LAG["x2t"])

            pe.wait_ge(s2_made, 1)
            o = turn("st")
            pe.transpose(o[:, 0:P], S2[:].rearrange("p t e -> p (t e)"), ident[:]).then_inc(filled[0], 1)
            pe.wait_ge(masks_made, 1)
            for r in range(ROUNDS):
                o = turn(("tot", r))
                pe.wait_ge(cnt_made, r + 1)
                pe.matmul(o[:, 0:3], same_expert[:], cnt[:, r, :], start=True, stop=True)\
                    .then_inc(sem_filled(("tot", r)), 1)
            pe.wait_ge(rt_made, 1)
            o = turn("thr")
            pe.matmul(o[:, 0:E], ones_f[:], rt[:], start=True, stop=True).then_inc(filled[3], 1)
            pe.wait_ge(prefix_in, 1)
            rows_g = cig[:, :, NT - 1:NT].to_broadcast([P, E, NT])
            rows_e = cie[:, :, NT // B - 1:NT // B].to_broadcast([P, E * B, NT // B])
            flat = lambda t: t[:].rearrange("p e t -> p (e t)")
            o = turn("pg")
            pe.matmul(o[:, 0:P], before_b[:], rows_g, start=True, stop=False)
            pe.matmul(o[:, 0:P], ident_b[:], flat(cxg), start=False, stop=True).then_inc(filled[4], 1)
            o = turn("pe")
            pe.matmul(o[:, 0:P], chunk_before_b[:], rows_e, start=True, stop=False)
            pe.matmul(o[:, 0:P], even_to_odd_b[:], flat(cie), start=False, stop=False)
            pe.matmul(o[:, 0:P], own_odd_to_even_b[:], flat(cxe), start=False, stop=False)
            second = o[:, 0:P].rearrange("p (e b j) -> p e b j", e=E, b=B)[:, :, 1, :]
            first_rows = cie[:].rearrange("p (e b) j -> p e b j", b=B)[:, :, 0, NT // B - 1:NT // B]
            pe.matmul(second, ones_b[:], first_rows.to_broadcast([P, E, NT // B]), start=False, stop=False)
            pe.matmul(o[:, 0:P], ones_b[:], rows_g, start=False, stop=True).then_inc(filled[5], 1)
            o = turn("ids")
            for t in range(NT):
                if t % (NT // 2) == 0:
                    pe.wait_ge(onehot_made, 2 * t // NT + 1)
                for k, w in enumerate((OHC, OHS)):
                    last = pe.matmul(o[:, 0:P], OHH[:, t].rearrange("p s e -> p (s e)"),
                                     w[:, t].rearrange("p s e -> p (s e)"),
                                     start=(t == 0 and k == 0), stop=(t == NT - 1 and k == 1))
            last.then_inc(filled[6], 1)
            pe.wait_ge(lh_made, 1)
            o = turn("idx")
            pe.matmul(o[:, 0:16], lh[:].rearrange("p a l -> p (a l)"), mask_16[:], start=True, stop=True)\
                .then_inc(filled[7], 1)

            def tokens(g):
                for c in range(KC):
                    o = turn(("gt", g, c))
                    for k in range(2 * GS):
                        if c == 0 and k % 2 == 0:
                            pe.wait_ge(gathered[GS * g + k // 2], 32)
                        last = pe.transpose(o[:, k * P:(k + 1) * P], XG[:, 2 * GS * g + k, c * P:(c + 1) * P], ident[:])
                    last.then_inc(filled[5 + c], 1)

            def up(g, f):
                if f == 0:
                    pe.wait_ge(wu_hi, g + 1)
                    wait_up_low(pe, g)
                    wait_moved(pe, ("gt", g, 0))
                    wait_moved(pe, ("gt", g, 1))
                o = turn(("up", g, f))
                cols = slice(f * P, f * P + FW[f])
                split_matmuls(o[0:FW[f], :], [
                    ((WUH[:, g % 2, c, cols], WUL[:, g % 2, c, cols]), (FTH[:, g % 2, c], FTL[:, g % 2, c]))
                    for c in range(KC)]).then_inc(filled[f % 3], 1)

            def down(e):
                g, first = e // GS, (e % GS) * TOP
                pe.wait_ge(wd_hi, e + 1)
                wait_down_low(pe, e)
                pe.wait_ge(ml_made, FC * (g + 1))
                for h in range(2):
                    o = turn(("dn", e, h))
                    pe.matmul(o[:, 0:D], ones_r[0:1, :], BDH[:, e % 3], start=True, stop=False)
                    pe.matmul(o[:, 0:D], ones_r[0:1, :], BDL[:, e % 3], start=False, stop=False)
                    cols = slice(first + h * P, first + (h + 1) * P)
                    for f in range(FC):
                        w = FW[f]
                        for a, b in ((MH, WDH), (MH, WDL), (ML, WDH)):
                            last = pe.matmul(o[:, 0:D], a[0:w, g % 2, f, cols], b[0:w, e % 3, f],
                                             start=False, stop=(f == FC - 1 and b is WDH and a is ML))
                    last.then_inc(filled[3 + h], 1)

            for kind, *at in expert_steps:
                {"gt": tokens, "up": up, "dn": down}[kind](*at)

        @block.vector
        def _(dve):
            link = chain(dve, dve_step)

            def low(w, src, n):
                dve.wait_ge(w_hi, n)
                dve.tensor_tensor(w[1][:], src[:], w[0][:].bitcast(F32), ALU.subtract).then_inc(w_lo, 1)

            low(WIN, win_s, 1)
            def x_low(n):
                for c in range(KC):
                    dve.wait_ge(xh_made, KC * n + c + 1)
                    dve.tensor_tensor(XL[:, n, c], bank_of(("xt", n, c))[:], XH[:, n, c].bitcast(F32), ALU.subtract)\
                        .then_inc(sem_moved(("xt", n, c)), 1)

            x_low(0)
            wait_filled(dve, "ab")
            dve.tensor_copy(mx_s[0:NS, :], bank[6][0:NS, 0:P]).then_inc(moved[6], 1)
            wait_moved(dve, "ab")
            dve.tensor_copy(TW[:, 0, :], mx_s[0:NS, 0:NS]).then_inc(tw1_made, 1)
            for n in range(NB):
                if n + 1 < NB:
                    x_low(n + 1)
                m = POWERS[n]
                wait_filled(dve, ("pw", m))
                dve.tensor_copy(PW[:, m + 1:2 * m + 1, :],
                                bank[4][0:NS, 0:m * NS].rearrange("p (k n) -> p k n", n=NS)).then_inc(moved[4], 1)
            low(WG, wg_s, 2)
            wait_filled(dve, "cd")
            dve.tensor_copy(cdt_s[:], bank[0][:, 0:D]).then_inc(moved[0], 1)
            wait_filled(dve, "ctx")
            for c in range(KC):
                last = dve.tensor_copy(ctd_s[:, c], bank[1][:, c * P:(c + 1) * P].rearrange("p (b s) -> p b s", b=B)
                                       .unsqueeze(2).to_broadcast([P, B, 2, SE]))
            last.then_inc(moved[1], 1)

            def masks(part):
                if part == 0:
                    for k, (sh, m) in enumerate(((0, 7), (0, 63), (3, 7), (6, 1))):
                        dve.tensor_scalar(pbits[:, 2 + k:3 + k], pidx[:], sh, m, ALU.logical_shift_right,
                                          ALU.bitwise_and)
                    dve.tensor_scalar(colm_i[:], col_i[:], 63, None, ALU.bitwise_and)
                    dve.tensor_scalar(col8_i[:], col_i[:], 3, None, ALU.logical_shift_right)
                    link(dve.tensor_copy(pf[:, 6:7], pidx[:]))
                if part == 1:
                    dve.tensor_copy(pf[:, 2:6], pbits[:, 2:6])
                    dve.tensor_copy(colm_f[:], colm_i[:])
                    link(dve.tensor_copy(ident_b[:], ident[:]))
                if part == 2:
                    dve.tensor_scalar(pf[:, 7:8], pf[:, 6:7], 64.0, None, ALU.add)
                    dve.tensor_scalar(pf[:, 0:1], pf[:, 6:7], -64.0, None, ALU.add)
                    link(dve.tensor_scalar(colm_i[:], col_i[:], 7, None, ALU.bitwise_and))
                if part == 3:
                    dve.tensor_scalar(chunk_before_b[:], colm_f[:], pf[:, 3:4], None, ALU.is_gt)
                    for b in range(B):
                        dve.tensor_scalar(chunk16[:, b:b + 1], pf[:, 3:4], float(L), float(b * T), ALU.mult, ALU.add)
                    dve.tensor_scalar(pf[:, 1:2], pf[:, 2:3], 2.0, pf[:, 5:6], ALU.mult, ALU.add)
                    dve.tensor_scalar(own_odd_to_even_b[:], col_f[:], pf[:, 0:1], None, ALU.is_equal)
                    link(dve.tensor_copy(col7_f[:], colm_i[:]))
                if part == 4:
                    dve.tensor_copy(step_f[:], tok_i[:])
                    dve.tensor_copy(digit_b[:], col8_i[:].rearrange("p (s e) -> p s e", e=E))
                    dve.tensor_scalar(mask_own[:], col_f[:, 0:E], pf[:, 2:3], None, ALU.is_equal)
                    dve.tensor_scalar(same_expert[:], col7_f[:], pf[:, 2:3], None, ALU.is_equal)
                    dve.tensor_scalar(before_b[:], col_f[:], pf[:, 6:7], None, ALU.is_gt)
                if part == 5:
                    dve.tensor_scalar(even_to_odd_b[:], col_f[:], pf[:, 7:8], None, ALU.is_equal)
                    dve.tensor_tensor(own_odd_to_even_b[:], own_odd_to_even_b[:], ident_b[:], ALU.add)
                    dve.tensor_scalar(mask_lo3[:], col_f[:, 0:8], pf[:, 4:5], None, ALU.is_equal)
                    dve.tensor_scalar(mask_16[:], col_f[:, 0:16], pf[:, 1:2], None, ALU.is_equal)
                if part >= 6:
                    a, b, sh = ((1, 2, 2), (2, 4, 4), (4, 8, 8), (8, ROUNDS, 16))[part - 6]
                    link(dve.tensor_scalar(steps[:, a:b, :], steps[:, 0:b - a, :], sh, None, ALU.logical_shift_right))
                if part == 9:
                    dve.tensor_scalar(junk_m[:], col_f[:, 0:1], 0.0, None, ALU.mult).then_inc(masks_made, 1)

            def between_steps(i):
                if i == 0:
                    dve.wait_ge(w_hi, 6)
                    dve.tensor_tensor(W1[1][:], bank[7][:, 0:D], W1[0][:].bitcast(F32), ALU.subtract)\
                        .then_inc(moved[7], 1)
                if i == 2:
                    low(WOUT, wout_s, 3)
                if i == 4:
                    low(WQ, wq_s, 4)
                if i == 6:
                    low(WO, wo_s, 5)
                if i == 8:
                    dve.wait_ge(kv_in, 128)
                    dve.tensor_copy(wk3_s[:], wk_s[:].rearrange("p c (j s) -> p (c j) s", s=32).unsqueeze(2)
                                    .to_broadcast([P, KC * PR, 3, 32])).then_inc(wk3_made, 1)
                if i == 10:
                    dve.wait_ge(pool_consts, 1)
                    dve.tensor_scalar(pbits[:, 0:1], pidx[:], 4, 1, ALU.logical_shift_right, ALU.bitwise_and)
                    dve.tensor_scalar(pbits[:, 1:2], pidx[:], 4, None, ALU.logical_shift_right)
                    link(dve.tensor_copy(col_f[:], col_i[:]))
                    link(dve.tensor_copy(pf[:, 0:2], pbits[:, 0:2]))
                    dve.tensor_scalar(half_mask[:, 0:1], pf[:, 0:1], 0.0, None, ALU.is_equal)
                    dve.tensor_scalar(half_mask[:, 1:2], pf[:, 0:1], 1.0, None, ALU.is_equal)
                    dve.tensor_scalar(mask_hi3[:], col_f[:, 0:8], pf[:, 1:2], None, ALU.is_equal)\
                        .then_inc(head_masks, 1)
                    dve.wait_ge(head_masks, 1)
                    for h in range(2):
                        last = dve.tensor_scalar(bk3h[0:KQ, h, :], bk3_c[0:KQ, :], half_mask[0:KQ, h:h + 1], None, ALU.mult)
                    last.then_inc(head_masks, 1)
                if i > 10:
                    masks(i - 11)

            hu4 = HU[0:NS, :].rearrange("p (b i c) -> p b i c", b=B, i=L)
            for i in range(L):
                name = ("step", i)
                wait_filled(dve, name)
                got = bank_of(name)[0:NS, 0:B * CH].rearrange("p (b c) -> p b c", b=B)
                dst = hu4[:, :, i + 1, :] if i + 1 < L else HS[:, :, 1:CH + 1]
                dve.tensor_copy(dst, got).then_inc(sem_moved(name), 1)
                if i % 2 == 1 and 4 + i // 2 < 9:
                    m = POWERS[4 + i // 2]
                    wait_filled(dve, ("pw", m))
                    dst = PB[:, i // 2, :] if m >= 16 else None
                    dve.tensor_copy(dst, bank[4][0:NS, 0:NS]).then_inc(moved[4], 1)
                between_steps(i)
            for k, d in enumerate(LEVELS):
                name = ("carry", k)
                wait_filled(dve, name)
                if k == 0:
                    wait_moved(dve, ("step", L - 1))
                else:
                    wait_moved(dve, ("carry", k - 1))
                dve.tensor_tensor(HS[:, :, 1 + d:CH + 1], HS[:, :, 1 + d:CH + 1],
                                  bank_of(name)[0:NS, 0:B * (CH - d)].rearrange("p (b c) -> p b c", b=B), ALU.add)\
                    .then_inc(sem_moved(name), 1)
                if k < 2:
                    wait_filled(dve, ("v", k))
                    dve.wait_ge(vb_init, 2)
                    got = bank[4 + k][:, 0:D].rearrange("p (j h d) -> p j h d", j=PR, h=2)
                    dve.tensor_copy(VB[0:SE, k, :, 0, 0:DK], got[0:SE, :, 0, :]).then_inc(vb_made, 1)
                    dve.tensor_copy(VB[SE:P, k, :, 1, 0:DK], got[SE:P, :, 1, :]).then_inc(moved[4 + k], 1)
                elif k < 5:
                    masks(2 * k + 1)
                    if k < 4:
                        masks(2 * k + 2)
            wait_moved(dve, ("carry", 5))
            dve.tensor_copy(hu4[:, :, 0, :], HS[:, :, 0:CH]).then_inc(h_start, 1)

            def state_low(n):
                dve.wait_ge(hu_hi, n + 1)
                cols = slice(n * BLK, (n + 1) * BLK)
                dve.tensor_tensor(HUL[:, cols], HU[:, cols], HUH[:, cols].bitcast(F32), ALU.subtract)\
                    .then_inc(hu_lo, 1)

            for q in range(4):
                name = ("cor", q)
                wait_filled(dve, name)
                i0 = 1 if q == 0 else 0
                to = hu4[:, :, 4 * q + i0:4 * q + 4, :]
                got = bank_of(name)[0:NS, :].rearrange("p (i b c) -> p b i c", i=4, b=B)[:, :, i0:, :]
                dve.tensor_tensor(to, to, got, ALU.add).then_inc(sem_moved(name), 1)
                if q == 2:
                    state_low(0)
            state_low(1)

            def gated(n):
                for c in range(KC):
                    wait_filled(dve, ("y", n, c))
                    wait_moved(dve, ("gate", 2 * n + c))
                    dve.tensor_tensor(G[:, n, c], bank[2 + c][:], G[:, n, c], ALU.mult).then_inc(moved[2 + c], 1)
                if n == 0:
                    for c in range(KC):
                        dve.wait_ge(y_hi, KC * n + c + 1)
                        dve.tensor_tensor(YL[:, n, c], G[:, n, c], YH[:, n, c].bitcast(F32), ALU.subtract)\
                            .then_inc(y_lo_dve, 1)

            gated(0)
            state_low(2)
            gated(1)
            state_low(3)

            def add(which, t, name):
                if t % TPB == 0:
                    dve.wait_ge(xb_added if which == 1 else bo_added, t // TPB + 1)
                wait_filled(dve, name)
                r = X[:, t, 0:D]
                dve.tensor_tensor(r, bank_of(name)[:, 0:D], r, ALU.add).then_inc(sem_moved(name), 1)

            def statistics(which, t, name):
                wait_moved(dve, name)
                k = norm_at[which, t]
                dve.bn_stats(bn6[:, k, :], X[:, t, 0:D]).then_inc(ln_stats, 1)

            def mean_variance(which, t):
                k = norm_at[which, t]
                dve.wait_ge(ln_stats, k + 1)
                dve.bn_aggr(mean_var[:, k, :], bn6[:, k, :]).then_inc(ln_var, 1)

            def x1_low(g, c):
                n = block_of(g, "x1t")
                if n is not None:
                    dve.wait_ge(x1h_made, KC * n + c + 1)
                    dve.tensor_tensor(X1L[n % 2][:, c], bank[c][:], X1H[n % 2][:, c].bitcast(F32), ALU.subtract)\
                        .then_inc(moved[c], 1)

            def maxima(t, c):
                name = ("mx", t, c)
                wait_filled(dve, name)
                half = HD // KC
                dve.tensor_reduce(NMF[:, t % 2, c * half:(c + 1) * half],
                                  bank_of(name)[:].rearrange("p (h k) -> p h k", k=SE), AX.X, ALU.max,
                                  negate=True).then_inc(sem_moved(name), 1)

            def by_pair(t):
                return NMF[:, t % 2, :].rearrange("p (j h) -> p j h", h=2)

            def maxima_high(t):
                for c in range(KC):
                    wait_moved(dve, ("mx", t, c))
                n, s = t // TPB, t % TPB
                if n >= 2 and s == 0:
                    wait_filled(dve, ("nmt", n - 2))
                dve.tensor_copy(NMS[:, n % 2, s, :, 0, :], by_pair(t)).then_inc(nm_hi, 1)

            def maxima_low(t):
                dve.wait_ge(nm_hi, t + 1)
                ns = NMS[:, t // TPB % 2, t % TPB]
                dve.tensor_tensor(ns[:, :, 1, :], by_pair(t), ns[:, :, 0, :].bitcast(F32), ALU.subtract)\
                    .then_inc(nm_made, 1)

            def weighted_sums(t):
                return bank_of(("pv", t))[:, 0:34 * PR].rearrange("p (h d) -> p h d", d=DK + 1)

            def inverse_sums(t):
                wait_filled(dve, ("pv", t))
                dve.reciprocal(REC[:, t % 2, :].unsqueeze(2), weighted_sums(t)[:, :, DK:DK + 1]).then_inc(rec_made, 1)

            def attended(t):
                dve.wait_ge(rec_made, t + 1)
                if t >= TPB:
                    wait_filled(dve, ("att", t - TPB))
                dve.tensor_tensor(ATT[:, t % TPB, :].rearrange("p (h d) -> p h d", d=DK), weighted_sums(t)[:, :, 0:DK],
                                  REC[:, t % 2, :].unsqueeze(2).to_broadcast([P, HD, DK]), ALU.mult)\
                    .then_inc(sem_moved(("pv", t)), 1)

            for g in UNITS:
                for c in range(KC):
                    x1_low(g, c)
                z1, mx, pv, z2 = [g - LAG[k] for k in ("z1", "mx", "pv", "z2")]
                if live(g, "z1"):
                    add(1, z1, ("z1", z1))
                for n in (2, 3):
                    if g == Y_UNIT[n]:
                        gated(n)
                if live(g - 1, "z2"):
                    mean_variance(2, z2 - 1)
                if live(g, "mx"):
                    maxima(mx, 0)
                if live(g, "z1"):
                    statistics(1, z1, ("z1", z1))
                if live(g, "mx"):
                    maxima(mx, 1)
                if live(g, "z1"):
                    mean_variance(1, z1)
                if live(g, "lg"):
                    t = g - LAG["lg"]
                    if t == 0:
                        dve.wait_ge(bias2_in, 16 * (4 + NG))
                    wait_filled(dve, ("lg", t))
                    dve.tensor_tensor(lgt[:, t, :], bank_of(("lg", t))[:, 0:E], br_all[:], ALU.add)\
                        .then_inc(sem_moved(("lg", t)), 1)
                if live(g, "mx"):
                    maxima_high(mx)
                if live(g, "pv"):
                    inverse_sums(pv)
                if live(g, "mx"):
                    maxima_low(mx)
                if live(g, "pv"):
                    attended(pv)
                for c in range(KC):
                    n = block_of(g - c, "q")
                    if n is not None:
                        dve.wait_ge(q_hi, KC * n + c + 1)
                        dve.scalar_tensor_tensor(QL[:, n % 2, c], bank_of(("q", n, c))[:], bq_c[:, c:c + 1],
                                                 QH[:, n % 2, c].bitcast(F32), ALU.add, ALU.subtract)\
                            .then_inc(sem_moved(("q", n, c)), 1)
                if live(g - 1, "z2") and z2 - 1 >= BY_POOL:
                    k = norm_at[2, z2 - 1]
                    dve.wait_ge(ln_pool, k + 1)
                    dve.tensor_scalar(X[:, z2 - 1, 0:D], X[:, z2 - 1, 0:D], mean_var[:, k, 0:1], rstd[:, k:k + 1],
                                      ALU.subtract, ALU.mult).then_inc(ln2_out_dve, 1)
                if live(g, "att"):
                    t = g - LAG["att"]
                    dve.wait_ge(ath_made, t + 1)
                    dve.tensor_tensor(ATL[:, t % 2].rearrange("p c k -> p (c k)"), bank_of(("att", t))[:, 0:D],
                                      ATH[:, t % 2].rearrange("p c k -> p (c k)").bitcast(F32), ALU.subtract)\
                        .then_inc(sem_moved(("att", t)), 1)
                if live(g, "z2"):
                    add(2, z2, ("z2", z2))
                    statistics(2, z2, ("z2", z2))

            phase2_over(dve)
            link(dve.tensor_reduce(mxl[:], lgt[:], AX.X, ALU.max))
            dve.tensor_tensor(lm[:], lgt[:], mxl[:].unsqueeze(2).to_broadcast([P, NT, E]), ALU.subtract)\
                .then_inc(lm_made, 1)
            dve.wait_ge(ex_made, 1)
            link(dve.tensor_reduce(sm[:], ex[:], AX.X, ALU.add))
            link(dve.reciprocal(rcp[:], sm[:]))
            dve.tensor_tensor(S2[:], ex[:], rcp[:].unsqueeze(2).to_broadcast([P, NT, E]), ALU.mult)\
                .then_inc(s2_made, 1)
            wait_filled(dve, "st")
            dve.tensor_copy(ST[:], bank[0][:, 0:P]).then_inc(moved[0], 1)
            wait_moved(dve, "st")
            dve.wait_ge(masks_made, 1)
            link(dve.tensor_copy(cand[:, 0, :], steps[:, 0, :]))
            for r in range(ROUNDS):
                for j in range(3):
                    last = dve.tensor_scalar(junk[:, j, :], ST[:], cand[:, r, j:j + 1].bitcast(F32), 0.0, ALU.is_ge,
                                             ALU.add, accum_out=cnt[:, r, j:j + 1])
                last.then_inc(cnt_made, 1)
                nxt = steps[:, r + 1, :] if r + 1 < ROUNDS else steps[:, 0, 3:4].to_broadcast([P, 4])
                link(dve.tensor_tensor(follow[:, r], cand[:, r, :].unsqueeze(2).to_broadcast([P, 4, 4]),
                                       nxt.unsqueeze(1).to_broadcast([P, 4, 4]), ALU.bitwise_or))
                name = ("tot", r)
                wait_filled(dve, name)
                held = follow[:, r, 0:3, :].bitcast(F32)
                dve.scalar_tensor_tensor(held, bank_of(name)[:, 0:3].unsqueeze(2).to_broadcast([P, 3, 4]),
                                         TOP - 0.5, held, ALU.is_ge, ALU.mult).then_inc(sem_moved(name), 1)
                wait_moved(dve, name)
                link(dve.tensor_reduce(cand[:, r + 1, :].bitcast(F32),
                                       follow[:, r].bitcast(F32).rearrange("p v j -> p j v"), AX.X, ALU.max))
            dve.tensor_scalar(rt[:], ident[:, 0:E], cand[:, ROUNDS, 3:4].bitcast(F32), None, ALU.mult)\
                .then_inc(rt_made, 1)
            wait_filled(dve, "thr")
            dve.tensor_copy(thr[:], bank[3][:, 0:E]).then_inc(moved[3], 1)
            wait_moved(dve, "thr")
            probs = S2[:].rearrange("p t e -> p e t")
            limit = thr[:].unsqueeze(2).to_broadcast([P, E, NT])
            flat = lambda t: t[:].rearrange("p e t -> p (e t)")
            dve.tensor_tensor(gt[:], probs, limit, ALU.is_gt)
            link(dve.tensor_tensor(ge[:], probs, limit, ALU.is_ge))
            dve.tensor_tensor(eq[:], ge[:], gt[:], ALU.subtract)
            link(dve.tensor_tensor_scan(flat(cig), flat(reset_g), flat(gt), 0.0, ALU.mult, ALU.add))
            link(dve.tensor_tensor_scan(flat(cie), flat(reset_e), flat(eq), 0.0, ALU.mult, ALU.add))
            link(dve.tensor_tensor(cxg[:], cig[:], gt[:], ALU.subtract))
            dve.tensor_tensor(flat(cxe), flat(cie), flat(eq), ALU.subtract).then_inc(prefix_in, 1)
            dve.tensor_scalar(sl[2][:], ge[:], -4096.0, 4096.0, ALU.mult, ALU.add)
            wait_filled(dve, "pg")
            dve.tensor_tensor(flat(sl[0]), bank[4][:, 0:P], flat(gt), ALU.mult).then_inc(moved[4], 1)
            wait_filled(dve, "pe")
            dve.tensor_tensor(flat(sl[1]), bank[5][:, 0:P], flat(eq), ALU.mult).then_inc(moved[5], 1)
            wait_moved(dve, "pe")
            link(dve.tensor_tensor(sl[3][:], sl[0][:], sl[1][:], ALU.add))
            link(dve.tensor_tensor(sl_i[:, 0], sl[3][:], sl[2][:], ALU.add))
            dve.tensor_scalar(sl_i[:, 1], sl_i[:, 0], 4, None, ALU.logical_shift_right)
            link(dve.tensor_scalar(sl_i[:, 2], sl_i[:, 0], 15, None, ALU.bitwise_and))
            dve.tensor_copy(sl_f[:], sl_i[:, 1:3].rearrange("p k e t -> p k t e")).then_inc(slots_made, 1)
            dve.wait_ge(slots_made, 1)
            h = NT // 2

            def one_hot(out, k, b):
                at = slice(b * h, (b + 1) * h)
                return dve.tensor_tensor(out[:, at], sl_f[:, k, at, :].unsqueeze(2).to_broadcast([P, h, 16, E]),
                                         digit_b[:].unsqueeze(1).to_broadcast([P, h, 16, E]), ALU.is_equal)

            flat3 = lambda t, b: t[:, b * h:(b + 1) * h].rearrange("p t s e -> p (t s e)")
            for b in range(B):
                one_hot(OHL, 1, b).then_inc(low_digit, 1)
                one_hot(OHH, 0, b)
                dve.wait_ge(low_digit, b + 1)
                dve.tensor_scalar(flat3(OHC, b), flat3(OHL, b), chunk16[:, b:b + 1], None, ALU.mult)
                if b == 0:
                    dve.wait_ge(step_made, 1)
                dve.tensor_tensor(flat3(OHS, b), flat3(OHL, b),
                                  step_b[:, b * h:(b + 1) * h].rearrange("p t s -> p (t s)"), ALU.mult)\
                    .then_inc(onehot_made, 1)
            wait_filled(dve, "ids")
            dve.tensor_tensor(ym[:], bank[6][:, 0:P].rearrange("p (s e) -> p s e", e=E),
                              mask_own[:].unsqueeze(1).to_broadcast([P, 16, E]), ALU.mult).then_inc(moved[6], 1)
            wait_moved(dve, "ids")
            link(dve.tensor_reduce(lk[:], ym[:], AX.X, ALU.add))
            dve.tensor_tensor(lh[:], lk[:].unsqueeze(1).to_broadcast([P, 8, 16]),
                              mask_lo3[:].unsqueeze(2).to_broadcast([P, 8, 16]), ALU.mult).then_inc(lh_made, 1)
            wait_filled(dve, "idx")
            dve.tensor_copy(idx[:], bank[7][:, 0:16]).then_inc(idx_made, 1)

            def experts_out(e):
                for h in range(2):
                    s = 2 * e + h
                    wait_filled(dve, ("dn", e, h))
                    if e >= 2:
                        dve.wait_ge(scattered[e - 2], 32)
                    dve.tensor_scalar(OUT[:, s % 4, :], bank[3 + h][:, 0:D], XG[:, s, D + e:D + e + 1], None,
                                      ALU.mult).then_inc(moved[3 + h], 1)

            low_after = {("up", 3, 1): 5, ("up", 3, 4): 6, ("dn", 4): 7}
            for step in expert_steps:
                g = step[1]
                if step[0] == "gt":
                    for c in range(KC):
                        dve.wait_ge(fth_made, KC * g + c + 1)
                        dve.tensor_tensor(FTL[:, g % 2, c], bank[5 + c][:], FTH[:, g % 2, c].bitcast(F32),
                                          ALU.subtract).then_inc(moved[5 + c], 1)
                if step[0] == "up":
                    f = step[2]
                    w, q = FW[f], g * FC + f
                    if g >= 2 and f == 0:
                        wait_filled(dve, ("dn", GS * (g - 2) + 1, 1))
                    wait_moved(dve, step)
                    dve.tensor_copy(MH[0:w, g % 2, f], MF[0:w, q % 3]).then_inc(mh_made, 1)
                    dve.wait_ge(mh_made, q + 1)
                    dve.tensor_tensor(ML[0:w, g % 2, f], MF[0:w, q % 3], MH[0:w, g % 2, f].bitcast(F32),
                                      ALU.subtract).then_inc(ml_made, 1)
                    if f == 2 and 2 <= g + 1 < NG:
                        dve.wait_ge(wu_hi, g + 2)
                        dve.tensor_tensor(WUL[:, (g + 1) % 2], WUR[:, (g + 1) % 2], WUH[:, (g + 1) % 2].bitcast(F32),
                                          ALU.subtract).then_inc(wu_lo_dve, 1)
                if step[0] == "dn":
                    experts_out(g)
                if step in low_after:
                    e = low_after[step]
                    dve.wait_ge(wd_hi, e + 1)
                    dve.tensor_tensor(WDL[:, e % 3, 0:FC - 1], WDR[:, e % 2, 0:FC - 1],
                                      WDH[:, e % 3, 0:FC - 1].bitcast(F32), ALU.subtract)
                    f = FW[-1]
                    dve.tensor_tensor(WDL[0:f, e % 3, FC - 1], WDR[0:f, e % 2, FC - 1],
                                      WDH[0:f, e % 3, FC - 1].bitcast(F32), ALU.subtract)
                    dve.tensor_tensor(BDL[:, e % 3], BDR[:, e % 2], BDH[:, e % 3].bitcast(F32), ALU.subtract)\
                        .then_inc(wd_lo_dve, 1)
            for q in range(NT // 4 + 1):
                for t in range(4 * q, min(4 * q + 4, NT)):
                    dve.wait_ge(y_in[t // 2], 16)
                    dve.bn_stats(bn6[:, 2 * NT + t, :], Y[:, t, :]).then_inc(ln_stats, 1)
                    if t % 4:
                        mean_variance(3, t - 1)
                if 4 * q < NT:
                    mean_variance(3, 4 * q + 3)
                if q:
                    k = 2 * NT + 4 * (q - 1)
                    dve.wait_ge(ln_pool, 2 * NT + q)
                    dve.scalar_tensor_tensor(shift[:, k:k + 4].unsqueeze(2), mean_var[:, k:k + 4, 0:1], -1.0,
                                             rstd[:, k:k + 4].unsqueeze(2), ALU.mult, ALU.mult).then_inc(ln3_shift, 1)
                    r = Y[:, 4 * q - 1, :]
                    dve.tensor_scalar(r, r, mean_var[:, k + 3, 0:1], rstd[:, k + 3:k + 4], ALU.subtract, ALU.mult)\
                        .then_inc(ln3_out_dve, 1)


_INPUTS = ["x", "ctx_1024", "L0_attn_W_in", "L0_attn_b_in", "L0_attn_W_gate", "L0_attn_b_gate", "L0_attn_W_out",
           "L0_attn_b_out", "L0_attn_A", "L0_attn_Bm", "L0_attn_C", "L0_attn_D", "L0_xattn_Wq", "L0_xattn_bq",
           "L0_xattn_Wk", "L0_xattn_bk", "L0_xattn_Wv", "L0_xattn_bv", "L0_xattn_Wo", "L0_xattn_bo", "L0_ffn_Wr",
           "L0_ffn_br", "L0_ffn_W_up", "L0_ffn_b_up", "L0_ffn_W_down", "L0_ffn_b_down"]


def kernel(**inputs):
    import numpy as np
    from concourse import bacc
    from concourse.bass_utils import run_bass_kernel_spmd

    nc = bacc.Bacc("TRN2", target_bir_lowering=False, num_devices=1)
    arrays, args = {}, []
    for name in _INPUTS:
        a = np.ascontiguousarray(inputs[name])
        arrays[f"in_{name}"] = a
        args.append(nc.dram_tensor(f"in_{name}", a.shape, mybir.dt.from_np(a.dtype), kind="ExternalInput").ap())
    out = nc.dram_tensor("out", arrays["in_x"].shape, mybir.dt.float32, kind="ExternalOutput").ap()
    decoder_block(nc, *args, out)
    return run_bass_kernel_spmd(nc, [arrays], core_ids=[0]).results[0]["out"]
```
